# Optimizing a Trainium2 kernel written in Bass

```python
import numpy as np
import jax
import jax.numpy as jnp

def _softmax(x, axis=-1):
    return jax.nn.softmax(x, axis=axis)

def _gelu(x):
    return jax.nn.gelu(x, approximate=True)

def _silu(x):
    return jax.nn.silu(x)

def _sigmoid(x):
    return jax.nn.sigmoid(x)

def _layernorm(x, axis=-1, eps=1e-05):
    m = jnp.mean(x, axis=axis, keepdims=True)
    v = jnp.var(x, axis=axis, keepdims=True)
    return (x - m) / jnp.sqrt(v + eps)

def _scatter_add(tgt, idx, src, axis=0):
    return tgt.at[idx].add(src)

def _segment_sum(src, seg, n):
    return jax.ops.segment_sum(src, seg, n)
kernel_name = 'mk_seq_postln_d2_jaxref_r8_2a2c57'

def setup_inputs(seed: int=0):
    np.random.seed(seed)
    _w = jnp.asarray

    def _L0_attn_setup():
        import jax, jax.numpy as jnp
        import numpy as np
        B, S, H = (1, 256, 512)
        NH = 32
        Q_LORA, KV_LORA = (192, 64)
        QK_NOPE, QK_ROPE = (128, 64)
        Q_HEAD = QK_NOPE + QK_ROPE
        V_HEAD = 128
        key = jax.random.key(seed)
        ks = jax.random.split(key, 12)

        def lin(k, out_d, in_d):
            s = 1.0 / np.sqrt(in_d)
            return jax.random.uniform(k, (out_d, in_d), jnp.float32, -s, s)
        return {'hidden_size': jax.random.normal(ks[0], (B, S, H), jnp.float32), 'Wq_c': lin(ks[1], Q_LORA, H), 'bq_c': jnp.zeros((Q_LORA,), jnp.float32), 'Wq_up': lin(ks[2], NH * Q_HEAD, Q_LORA), 'bq_up': jnp.zeros((NH * Q_HEAD,), jnp.float32), 'Wkv_c': lin(ks[3], KV_LORA + QK_ROPE, H), 'bkv_c': jnp.zeros((KV_LORA + QK_ROPE,), jnp.float32), 'Wkv_up': lin(ks[4], NH * (QK_NOPE + V_HEAD), KV_LORA), 'bkv_up': jnp.zeros((NH * (QK_NOPE + V_HEAD),), jnp.float32), 'Wo': lin(ks[5], H, V_HEAD), 'bo': jnp.zeros((H,), jnp.float32)}
    _L0_attn_in = _L0_attn_setup()

    def _L0_ffn_setup():
        import jax, jax.numpy as jnp
        import numpy as np
        B, S, H, I = (4, 256, 512, 1376)

        def _dequant(wq, scale):
            return wq.astype(jnp.float32) * scale[:, None]
        key = jax.random.key(seed)
        ks = jax.random.split(key, 7)
        x = jax.random.normal(ks[0], (B, S, H), dtype=jnp.float32)
        gate_wq = jax.random.randint(ks[1], (I, H), -128, 128, dtype=jnp.int32)
        up_wq = jax.random.randint(ks[2], (I, H), -128, 128, dtype=jnp.int32)
        down_wq = jax.random.randint(ks[3], (H, I), -128, 128, dtype=jnp.int32)
        gate_scale = jax.random.uniform(ks[4], (I,), dtype=jnp.float32) * 0.01 + 0.0001
        up_scale = jax.random.uniform(ks[5], (I,), dtype=jnp.float32) * 0.01 + 0.0001
        down_scale = jax.random.uniform(ks[6], (H,), dtype=jnp.float32) * 0.01 + 0.0001
        return {'x': x, 'gate_wq': gate_wq, 'up_wq': up_wq, 'down_wq': down_wq, 'gate_scale': gate_scale, 'up_scale': up_scale, 'down_scale': down_scale}
    _L0_ffn_in = _L0_ffn_setup()

    def _L1_attn_setup():
        import jax, jax.numpy as jnp
        import numpy as np
        H = 32
        DN = 128
        DR = 64
        DV = 128
        DQ = DN + DR
        HID = 512
        NEG_INF = -1e+30
        key = jax.random.key(seed)
        k0, k1, k2, k3 = jax.random.split(key, 4)
        B, S = (4, 128)
        hidden_states = jax.random.normal(k0, (B, S, HID), dtype=jnp.float32)
        wq = jax.random.normal(k1, (HID, H * DQ), dtype=jnp.float32) * 0.02
        wkv = jax.random.normal(k2, (HID, H * (DN + DV) + DR), dtype=jnp.float32) * 0.02
        wo = jax.random.normal(k3, (H * DV, HID), dtype=jnp.float32) * 0.02
        return {'hidden_states': hidden_states, 'wq': wq, 'wkv': wkv, 'wo': wo}
    _L1_attn_in = _L1_attn_setup()

    def _L1_ffn_setup():
        import jax, jax.numpy as jnp
        import numpy as np
        import math
        E, DK, R = (8, 32, 16)
        SCALING = 16.0 / 16.0
        key = jax.random.key(seed)
        ks = jax.random.split(key, 7)
        Bt, S, Din, Dout = (4, 256, 512, 512)
        x = jax.random.normal(ks[0], (Bt, S, Din), jnp.float32)
        W = jax.random.normal(ks[1], (Dout, Din), jnp.float32) * 0.02
        b = jnp.zeros((Dout,), jnp.float32)
        Wq = jax.random.normal(ks[2], (E * DK, Din), jnp.float32) * 0.02
        Wk = jax.random.normal(ks[3], (E * DK, Din), jnp.float32) * 0.02
        A = jax.random.normal(ks[4], (E, R, Din), jnp.float32) * 0.02
        Bm = jax.random.normal(ks[5], (E, Dout, R), jnp.float32) * 0.02
        return {'x': x, 'W': W, 'b': b, 'Wq': Wq, 'Wk': Wk, 'A': A, 'Bm': Bm}
    _L1_ffn_in = _L1_ffn_setup()
    _d = {'L0_attn_hidden_size': _L0_attn_in['hidden_size'], 'L0_attn_Wq_c': _L0_attn_in['Wq_c'], 'L0_attn_bq_c': _L0_attn_in['bq_c'], 'L0_attn_Wq_up': _L0_attn_in['Wq_up'], 'L0_attn_bq_up': _L0_attn_in['bq_up'], 'L0_attn_Wkv_c': _L0_attn_in['Wkv_c'], 'L0_attn_bkv_c': _L0_attn_in['bkv_c'], 'L0_attn_Wkv_up': _L0_attn_in['Wkv_up'], 'L0_attn_bkv_up': _L0_attn_in['bkv_up'], 'L0_attn_Wo': _L0_attn_in['Wo'], 'L0_attn_bo': _L0_attn_in['bo'], 'L0_ffn_gate_wq': _L0_ffn_in['gate_wq'], 'L0_ffn_up_wq': _L0_ffn_in['up_wq'], 'L0_ffn_down_wq': _L0_ffn_in['down_wq'], 'L0_ffn_gate_scale': _L0_ffn_in['gate_scale'], 'L0_ffn_up_scale': _L0_ffn_in['up_scale'], 'L0_ffn_down_scale': _L0_ffn_in['down_scale'], 'L1_attn_wq': _L1_attn_in['wq'], 'L1_attn_wkv': _L1_attn_in['wkv'], 'L1_attn_wo': _L1_attn_in['wo'], 'L1_ffn_W': _L1_ffn_in['W'], 'L1_ffn_b': _L1_ffn_in['b'], 'L1_ffn_Wq': _L1_ffn_in['Wq'], 'L1_ffn_Wk': _L1_ffn_in['Wk'], 'L1_ffn_A': _L1_ffn_in['A'], 'L1_ffn_Bm': _L1_ffn_in['Bm']}
    _x0 = _d['L0_attn_hidden_size']
    _d['L0_attn_hidden_size'] = jax.random.normal(jax.random.fold_in(jax.random.key(seed), 1), (4, 256, 512), dtype=_x0.dtype)
    del _x0
    return _d

def reference(L0_attn_hidden_size, L0_attn_Wq_c, L0_attn_bq_c, L0_attn_Wq_up, L0_attn_bq_up, L0_attn_Wkv_c, L0_attn_bkv_c, L0_attn_Wkv_up, L0_attn_bkv_up, L0_attn_Wo, L0_attn_bo, L0_ffn_gate_wq, L0_ffn_up_wq, L0_ffn_down_wq, L0_ffn_gate_scale, L0_ffn_up_scale, L0_ffn_down_scale, L1_attn_wq, L1_attn_wkv, L1_attn_wo, L1_ffn_W, L1_ffn_b, L1_ffn_Wq, L1_ffn_Wk, L1_ffn_A, L1_ffn_Bm):

    def _L0_attn_ref(hidden_size, Wq_c, bq_c, Wq_up, bq_up, Wkv_c, bkv_c, Wkv_up, bkv_up, Wo, bo):
        import jax, jax.numpy as jnp
        import numpy as np
        B, S, H = (1, 256, 512)
        NH = 32
        Q_LORA, KV_LORA = (192, 64)
        QK_NOPE, QK_ROPE = (128, 64)
        Q_HEAD = QK_NOPE + QK_ROPE
        V_HEAD = 128
        b, s, _ = hidden_size.shape
        q_c = hidden_size @ Wq_c.T + bq_c
        q = (q_c @ Wq_up.T + bq_up).reshape(b, s, NH, Q_HEAD).transpose(0, 2, 1, 3)
        kv = hidden_size @ Wkv_c.T + bkv_c
        kv_nope, kv_rope = (kv[..., :KV_LORA], kv[..., KV_LORA:])
        kvu = (kv_nope @ Wkv_up.T + bkv_up).reshape(b, s, NH, QK_NOPE + V_HEAD).transpose(0, 2, 1, 3)
        k_nope, v = (kvu[..., :QK_NOPE], kvu[..., QK_NOPE:])
        k_rope = jnp.broadcast_to(kv_rope[:, None, :, :], (b, NH, s, QK_ROPE))
        k = jnp.concatenate([k_nope, k_rope], axis=-1)
        scores = jnp.einsum('bhqd,bhkd->bhqk', q, k) / np.sqrt(Q_HEAD)
        attn = jax.nn.softmax(scores, axis=-1)
        o = jnp.einsum('bhqk,bhkv->bhqv', attn, v)
        out = jnp.einsum('bhsv,Hv->bsH', o, Wo) + bo
        return out

    def _L0_ffn_ref(x, gate_wq, up_wq, down_wq, gate_scale, up_scale, down_scale):
        import jax, jax.numpy as jnp
        import numpy as np
        B, S, H, I = (4, 256, 512, 1376)

        def _dequant(wq, scale):
            return wq.astype(jnp.float32) * scale[:, None]
        gate_w = _dequant(gate_wq, gate_scale)
        up_w = _dequant(up_wq, up_scale)
        down_w = _dequant(down_wq, down_scale)
        gate = jax.nn.silu(jnp.einsum('bsh,ih->bsi', x, gate_w))
        up = jnp.einsum('bsh,ih->bsi', x, up_w)
        intermediate = gate * up
        return jnp.einsum('bsi,hi->bsh', intermediate, down_w)

    def _L1_attn_ref(hidden_states, wq, wkv, wo):
        import jax, jax.numpy as jnp
        import numpy as np
        H = 32
        DN = 128
        DR = 64
        DV = 128
        DQ = DN + DR
        HID = 512
        NEG_INF = -1e+30
        B, S, D = hidden_states.shape
        q = jnp.einsum('bsd,de->bse', hidden_states, wq).reshape(B, S, H, DQ)
        kv = jnp.einsum('bsd,de->bse', hidden_states, wkv)
        k = kv[..., :H * DN].reshape(B, S, H, DN)
        v = kv[..., H * DN:H * (DN + DV)].reshape(B, S, H, DV)
        scale = DQ ** (-0.5)
        scores = jnp.einsum('bqhd,bkhd->bhqk', q[..., :DN], k) * scale
        causal = jnp.tril(jnp.ones((S, S), dtype=bool))
        scores = jnp.where(causal[None, None], scores, NEG_INF)
        probs = jax.nn.softmax(scores, axis=-1)
        attn = jnp.einsum('bhqk,bkhd->bqhd', probs, v).reshape(B, S, H * DV)
        return jnp.einsum('bse,ed->bsd', attn, wo)

    def _L1_ffn_ref(x, W, b, Wq, Wk, A, Bm):
        import jax, jax.numpy as jnp
        import numpy as np
        import math
        E, DK, R = (8, 32, 16)
        SCALING = 16.0 / 16.0
        Bt, S, Din = x.shape
        result = jnp.einsum('bsi,oi->bso', x, W) + b
        q = jnp.einsum('bsi,ni->bsn', x, Wq).reshape(Bt, S, E, DK)
        k = jnp.einsum('bsi,ni->bsn', x, Wk).reshape(Bt, S, E, DK)
        scores = jnp.einsum('bsed,bsed->bse', q, k) / math.sqrt(DK)
        w = jax.nn.softmax(scores, axis=-1)
        h = jnp.einsum('bsi,eri->bser', x, A)
        combined = jnp.einsum('bse,bser,eor->bso', w, h, Bm) * SCALING
        return result + combined
    x = L0_attn_hidden_size
    x = _layernorm(x + _L0_attn_ref(x, L0_attn_Wq_c, L0_attn_bq_c, L0_attn_Wq_up, L0_attn_bq_up, L0_attn_Wkv_c, L0_attn_bkv_c, L0_attn_Wkv_up, L0_attn_bkv_up, L0_attn_Wo, L0_attn_bo), axis=-1)
    x = _layernorm(x + _L0_ffn_ref(x, L0_ffn_gate_wq, L0_ffn_up_wq, L0_ffn_down_wq, L0_ffn_gate_scale, L0_ffn_up_scale, L0_ffn_down_scale), axis=-1)
    x = _layernorm(x + _L1_attn_ref(x, L1_attn_wq, L1_attn_wkv, L1_attn_wo), axis=-1)
    x = _layernorm(x + _L1_ffn_ref(x, L1_ffn_W, L1_ffn_b, L1_ffn_Wq, L1_ffn_Wk, L1_ffn_A, L1_ffn_Bm), axis=-1)
    return x

_drawn_inputs = setup_inputs


def setup_inputs(seed=0):
    import zlib

    import numpy as np

    out = dict(_drawn_inputs(seed))
    spreads = {'L0_attn_bq_c': (0.0, 0.8),
     'L0_attn_bq_up': (0.0, 0.8),
     'L0_attn_bkv_c': (0.0, 0.1),
     'L0_attn_bkv_up': (0.0, 0.1),
     'L0_attn_bo': (0.0, 0.1),
     'L1_ffn_b': (0.0, 0.1)}
    factors = {'L1_attn_wq': 4.038,
     'L1_ffn_Wq': 8.0,
     'L1_ffn_Wk': 8.0,
     'L1_ffn_A': 4.771,
     'L1_ffn_Bm': 4.776}
    for name, (base, spread) in spreads.items():
        noise = np.random.default_rng([zlib.crc32(name.encode()), seed]).standard_normal(out[name].shape)
        drawn = base * np.exp(spread * noise) if base else spread * noise
        out[name] = jnp.asarray(drawn.astype(out[name].dtype))
    for name, factor in factors.items():
        out[name] = (out[name] * factor).astype(out[name].dtype)
    return out
```

```python
from contextlib import ExitStack

import numpy as np

import concourse.bass as bass
from concourse import mybir

F32 = mybir.dt.float32
F32R = mybir.dt.float32r
I32 = mybir.dt.int32
ALU = mybir.AluOpType
ACT = mybir.ActivationFunctionType
AX = mybir.AxisListType.X

P = 128
NB, S, HID = 4, 256, 512
T = NB * S
NT = T // P
KC = HID // P
HALF = 512
EPS = 1e-5

NH = 32
QL, KVL, NOPE, ROPE, VH = 192, 64, 128, 64, 128
SCALE0 = float(NOPE + ROPE) ** -0.5
W0 = 2 * P + KVL + 2 * ROPE + 2

INTER = 1376
NI = -(-INTER // P)

DN, DR, DV = 128, 64, 128
SCALE1 = float(DN + DR) ** -0.5
NG = NH // 2

E, DK, R = 8, 32, 16
W1F = HID + 2 * E * DK + E * R


def f32(ap):
    return ap.bitcast(F32)


def need(eng, sem, value):
    if isinstance(value, int) and value <= 0:
        return
    eng.wait_ge(sem, value)


def loop(eng, n, body):
    body(0)
    with eng.Fori(1, n) as i:
        body(i)


def plain(eng, sem):
    eng.sem_inc(sem, 1)


def matmul3(pe, out, w, x, start, stop):
    pe.matmul(out, w[0], x[0], start=start, stop=False, skip_group_check=True)
    pe.matmul(out, w[0], x[1], start=False, stop=False, skip_group_check=True)
    return pe.matmul(out, w[1], x[0], start=False, stop=stop, skip_group_check=True)


class Kit:

    def __init__(self, nc, ctx, tag):
        self.nc, self.ctx, self.tag = nc, ctx, tag

    def sb(self, name, shape, dt=F32):
        return self.ctx.enter_context(self.nc.sbuf_tensor(f"{self.tag}_{name}", shape, dt))

    def ps(self, name):
        return self.ctx.enter_context(self.nc.psum_tensor(f"{self.tag}_{name}", [P, 512], F32))

    def sem(self, name):
        return self.ctx.enter_context(self.nc.semaphore(f"{self.tag}_{name}"))


def build(nc, io):
    with ExitStack() as ctx:
        k = Kit(nc, ctx, "g")
        g = {}
        g["res"] = k.sb("res", [P, NT, HID])
        g["xT"] = (k.sb("xT_hi", [P, KC, T], F32R), k.sb("xT_lo", [P, KC, T], F32R))
        g["ident"] = k.sb("ident", [P, P])
        g["tick"] = k.sem("tick")
        g["ln"] = {n: k.sem(n) for n in ("c", "st", "mv", "add", "rs", "xn", "cp", "t", "hi", "lo")}
        sems = ExitStack()
        ctx.enter_context(sems)
        with ExitStack() as c:
            a = Kit(nc, c, "a")
            a.sem = Kit(nc, sems, "a").sem
            latent = attention0_prepare(nc, a, io, g)
            attention0_heads(nc, a, io, g, latent)
            attention0_out(nc, a, io, g, latent)
        with ExitStack() as c:
            n = Kit(nc, c, "n0")
            n.sem = Kit(nc, sems, "n0").sem
            layernorm(nc, n, g, 0)
        with ExitStack() as c:
            f = Kit(nc, c, "f")
            f.sem = Kit(nc, sems, "f").sem
            ffn0(nc, f, io, g)
        with ExitStack() as c:
            n = Kit(nc, c, "n1")
            n.sem = Kit(nc, sems, "n1").sem
            layernorm(nc, n, g, 1)
        with ExitStack() as c:
            b = Kit(nc, c, "b")
            b.sem = Kit(nc, sems, "b").sem
            attention1(nc, b, io, g)
        with ExitStack() as c:
            e = Kit(nc, c, "e")
            e.sem = Kit(nc, sems, "e").sem
            ffn1(nc, e, io, g)


def attention0_prepare(nc, k, io, g):
    res, ident = g["res"], g["ident"]
    xhi, xlo = g["xT"]
    qa = (k.sb("qa_hi", [P, T], F32R), k.sb("qa_lo", [P, T], F32R))
    qb = k.sb("qb", [P, T], F32R)
    kv = (k.sb("kv_hi", [P, T], F32R), k.sb("kv_lo", [P, T], F32R))
    cs = k.sb("cs", [P, NT, P], F32R)
    acc0 = k.ps("acc0")
    acc1 = k.ps("acc1")
    with ExitStack() as ctx:
        t = Kit(nc, ctx, "p")
        xraw = t.sb("xraw", [P, KC, T])
        wraw = t.sb("wraw", [P, KC, 3 * P])
        whi = t.sb("whi", [P, KC, 3 * P], F32R)
        wlo = t.sb("wlo", [P, KC, 3 * P], F32R)
        kvraw = t.sb("kvraw", [P, T])
        bias = t.sb("bias", [P, 3])
        zero = t.sb("zero", [P, P])
        banks = [t.ps(f"b{i}") for i in range(4)]
        s_x, s_w = k.sem("x_in"), k.sem("w_in")
        s_xk = [k.sem(f"xk{i}") for i in range(KC)]
        s_res = k.sem("res_in")
        s_id, s_whi, s_wlo = k.sem("ident"), k.sem("whi"), k.sem("wlo")
        s_xhi, s_xlo = k.sem("xhi"), k.sem("xlo")
        s_mm, s_hi, s_lo = k.sem("p_mm"), k.sem("p_hi"), k.sem("p_lo")
        s_raw, s_tr, s_chi, s_clo = k.sem("p_raw"), k.sem("p_tr"), k.sem("p_chi"), k.sem("p_clo")
        chunks = [(m, n) for m in (2, 0, 1) for n in range(2)]
        with nc.Block() as block:
            @block.sync
            def _(sp):
                sp.dma_start(wraw[:, :, :], io["w_down0"].rearrange("(c p) n -> p c n", p=P)).then_inc(s_w, 16)
                for c in range(KC):
                    sp.dma_start(xraw[:, c, :], io["xT"][c * P:(c + 1) * P, :]).then_inc(s_xk[c], 16)
                sp.dma_start(bias[:, :], io["b_down0"]).then_inc(s_x, 16)
                sp.dma_start(res[:, :, :], io["x"].rearrange("(t p) n -> p t n", p=P)).then_inc(s_res, 16)
                sp.wait_ge(s_res, 16)

            @block.gpsimd
            def _(pool):
                pool.memset(ident[:, :], 0.0).then_inc(s_id, 1)
                pool.memset(zero[:, :], 0.0).then_inc(s_id, 1)
                pool.wait_ge(s_id, 2)
                pool.affine_select(out=ident[:, :], in_=ident[:, :], compare_op=ALU.not_equal, fill=1.0, base=0,
                                   pattern=[[-1, P]], channel_multiplier=1).then_inc(s_id, 1)

            @block.scalar
            def _(act):
                act.wait_ge(s_w, 16)
                act.activation(whi[:, :, :], wraw[:, :, :], ACT.Identity).then_inc(s_whi, 1)
                for c in range(KC):
                    act.wait_ge(s_xk[c], 16)
                    act.activation(xhi[:, c, :], xraw[:, c, :], ACT.Identity).then_inc(s_xhi, 1)
                act.wait_ge(s_x, 16)
                for i, (m, n) in enumerate(chunks):
                    tok = slice(n * HALF, (n + 1) * HALF)
                    act.wait_ge(s_mm, i + 1)
                    if m == 2:
                        act.activation(kvraw[:, tok], banks[i % 2][:, :], ACT.Identity,
                                       bias=bias[:, m:m + 1]).then_inc(s_raw, 1)
                        act.wait_ge(s_raw, n + 1)
                        act.activation(kv[0][:, tok], kvraw[:, tok], ACT.Identity).then_inc(s_hi, 1)
                    else:
                        out = qa[0] if m == 0 else qb
                        act.activation(out[:, tok], banks[i % 2][:, :], ACT.Identity,
                                       bias=bias[:, m:m + 1]).then_inc(s_hi, 1)
                for n in range(2):
                    act.wait_ge(s_tr, n + 1)
                    src = banks[2 + n][:, :].rearrange("p (t l) -> p t l", l=P)
                    act.activation(cs[:, 4 * n:4 * n + 4, 0:KVL], src[:, :, 0:KVL], ACT.Identity).then_inc(s_chi, 1)

            @block.vector
            def _(dve):
                dve.wait_ge(s_whi, 1)
                dve.tensor_tensor(wlo[:, :, :], wraw[:, :, :], f32(whi[:, :, :]), ALU.subtract).then_inc(s_wlo, 1)
                for c in range(KC):
                    dve.wait_ge(s_xhi, c + 1)
                    dve.tensor_tensor(xlo[:, c, :], xraw[:, c, :], f32(xhi[:, c, :]), ALU.subtract).then_inc(s_xlo, 1)
                dve.wait_ge(s_x, 16)
                for i, (m, n) in enumerate(chunks):
                    tok = slice(n * HALF, (n + 1) * HALF)
                    dve.wait_ge(s_hi, i + 1)
                    if m == 2:
                        dve.tensor_tensor(kv[1][:, tok], kvraw[:, tok], f32(kv[0][:, tok]),
                                          ALU.subtract).then_inc(s_lo, 1)
                    else:
                        r = slice(0, P) if m == 0 else slice(QL - P, P)
                        hi, lo = (qa[0], qa[1]) if m == 0 else (qb, qb)
                        dve.scalar_tensor_tensor(out=lo[r, tok], in0=banks[i % 2][r, :], scalar=bias[r, m:m + 1],
                                                 in1=f32(hi[r, tok]), op0=ALU.add, op1=ALU.subtract).then_inc(s_lo, 1)
                for n in range(2):
                    dve.wait_ge(s_chi, n + 1)
                    src = banks[2 + n][:, :].rearrange("p (t l) -> p t l", l=P)
                    dve.tensor_tensor(cs[:, 4 * n:4 * n + 4, KVL:P], src[:, :, 0:KVL],
                                      f32(cs[:, 4 * n:4 * n + 4, 0:KVL]), ALU.subtract).then_inc(s_clo, 1)

            @block.tensor
            def _(pe):
                pe.wait_ge(s_wlo, 1)
                for i, (m, n) in enumerate(chunks):
                    need(pe, s_lo, i - 1)
                    tok = slice(n * HALF, (n + 1) * HALF)
                    for c in range(KC):
                        if i == 0:
                            pe.wait_ge(s_xlo, c + 1)
                        w = (whi[:, c, m * P:(m + 1) * P], wlo[:, c, m * P:(m + 1) * P])
                        mm = matmul3(pe, banks[i % 2][:, :], w, (xhi[:, c, tok], xlo[:, c, tok]), c == 0, c == KC - 1)
                    mm.then_inc(s_mm, 1)
                pe.wait_ge(s_id, 3)
                pe.wait_ge(s_raw, 2)
                for n in range(2):
                    for j in range(4):
                        a = (4 * n + j) * P
                        mm = pe.transpose(banks[2 + n][:, j * P:(j + 1) * P], kvraw[:, a:a + P], ident[:, :])
                    mm.then_inc(s_tr, 1)
                for acc in (acc0, acc1):
                    for j in range(4):
                        pe.matmul(acc[:, j * P:(j + 1) * P], zero[:, :], zero[:, :], start=(j == 0), stop=False,
                                  skip_group_check=True)
    return dict(qa=qa, qb=qb, kv=kv, cs=cs, acc=(acc0, acc1))


def attention0_heads(nc, k, io, g, lat):
    qa, qb, kv, cs, acc = lat["qa"], lat["qb"], lat["kv"], lat["cs"], lat["acc"]
    ident = g["ident"]
    NS, NPAIR = NB * NH, 2 * NH
    with ExitStack() as ctx:
        t = Kit(nc, ctx, "h")
        w = t.sb("w", [P, W0])
        wk = w[:, 2 * P:2 * P + KVL]
        rope = w[:, 2 * P + KVL:2 * P + KVL + 2 * ROPE].rearrange("p (a n) -> p a n", a=2)
        bcols = w[:, W0 - 2:W0]
        wv = t.sb("wv", [P, VH])
        wvs = (t.sb("wv_hi", [P, VH], F32R), t.sb("wv_lo", [P, VH], F32R))
        gm = t.sb("gm", [P, 2, P])
        gms = (t.sb("gm_hi", [P, 2, P], F32R), t.sb("gm_lo", [P, 2, P], F32R))
        gb = t.sb("gb", [P, 1])
        q = [(t.sb(f"q{i}_hi", [P, HALF], F32R), t.sb(f"q{i}_lo", [P, HALF], F32R)) for i in range(2)]
        o = [(t.sb(f"o{i}_hi", [P, HALF], F32R), t.sb(f"o{i}_lo", [P, HALF], F32R)) for i in range(2)]
        pr = [t.sb(f"pr{i}", [P, 2, S]) for i in range(NB)]
        pt = [(t.sb(f"pt{i}_hi", [P, 2, S], F32R), t.sb(f"pt{i}_lo", [P, 2, S], F32R)) for i in range(NB)]
        nmax = [t.sb(f"nmax{i}", [P, 2]) for i in range(NB)]
        rsum = [t.sb(f"rsum{i}", [P, 2]) for i in range(NB)]
        rinv = [t.sb(f"rinv{i}", [P, 2]) for i in range(NB)]
        bq = t.ps("bq")
        bs = [t.ps(f"bs{i}") for i in range(2)]
        bt = [t.ps(f"bt{i}") for i in range(2)]
        bo = t.ps("bo")
        s_w, s_wv, s_tick = k.sem("w0_in"), k.sem("wv_in"), g["tick"]
        s_gmm, s_graw, s_gpool, s_ghi, s_glo = (k.sem(x) for x in ("g_mm", "g_raw", "g_pool", "g_hi", "g_lo"))
        s_qmm, s_qhi, s_qlo = k.sem("q_mm"), k.sem("q_hi"), k.sem("q_lo")
        s_smm, s_max, s_exp, s_inv, s_norm = (k.sem(x) for x in ("s_mm", "s_max", "s_exp", "s_inv", "s_norm"))
        s_tmm, s_thi, s_tlo = k.sem("t_mm"), k.sem("t_hi"), k.sem("t_lo")
        s_pv, s_ohi, s_olo = k.sem("pv"), k.sem("o_hi"), k.sem("o_lo")
        s_wvh, s_wvl, s_om = k.sem("wv_hi"), k.sem("wv_lo"), k.sem("om")

        def has(x, n):
            return not isinstance(x, int) or 0 <= x < n

        def sweep(round_):
            def head(h):
                for b in range(NB):
                    round_(h, b)

            head(0)
            head(1)
            return head

        def run(eng, round_):
            head = sweep(round_)
            with eng.Fori(2, NH - 1) as h:
                head(h)
            head(NH - 1)
            head(NH)
            round_(NH + 1, 0)

        with nc.Block() as block:
            @block.sync
            def _(sp):
                def fetch(h):
                    need(sp, s_graw, h)
                    need(sp, s_gpool, h)
                    sp.dma_start(w[:, :], io["w_head0"][bass.ds(h, 1), :, :].rearrange("a p n -> (a p) n"))\
                      .then_inc(s_w, 16)

                def fetch_wv(h):
                    need(sp, s_wvl, h)
                    sp.dma_start(wv[:, :], io["wv_head0"][bass.ds(h, 1), :, :].rearrange("a p n -> (a p) n"))\
                      .then_inc(s_wv, 16)

                def both(h):
                    fetch(h + 1)
                    fetch_wv(h)

                fetch(0)
                loop(sp, NH - 1, both)
                fetch_wv(NH - 1)

            @block.gpsimd
            def _(pool):
                def rope_part(h):
                    pool.wait_ge(s_w, 16 * h + 16)
                    need(pool, s_glo, h)
                    need(pool, s_qlo, 2 * h)
                    plain(pool, s_tick)
                    pool.tensor_scalar(gm[:, :, KVL:P], rope, SCALE0, None, ALU.mult)
                    pool.tensor_scalar(gb[:, :], bcols[:, 1:2], SCALE0, None, ALU.mult).then_inc(s_gpool, 1)

                def split_wv(h):
                    pool.wait_ge(s_wv, 16 * h + 16)
                    need(pool, s_om, 2 * h)
                    plain(pool, s_tick)
                    pool.tensor_copy(wvs[0][:, :], wv[:, :]).then_inc(s_wvh, 1)
                    pool.wait_ge(s_wvh, h + 1)
                    pool.tensor_tensor(wvs[1][:, :], wv[:, :], f32(wvs[0][:, :]), ALU.subtract).then_inc(s_wvl, 1)

                def norm(s, b):
                    pool.wait_ge(s_inv, s + 1)
                    pool.tensor_tensor(pr[b][:, :, :], pr[b][:, :, :],
                                       rinv[b][:, :][:, :, None].to_broadcast([P, 2, S]), ALU.mult)\
                        .then_inc(s_norm, 1)

                def round_(h, b):
                    s = 4 * h + b
                    if has(s - 1, NS):
                        norm(s - 1, (b - 1) % 4)
                    if b == 0 and has(h + 1, NH):
                        rope_part(h + 1)
                    if b == 1 and has(h - 1, NH):
                        split_wv(h - 1)

                rope_part(0)
                run(pool, round_)

            @block.scalar
            def _(act):
                def merged(h):
                    act.wait_ge(s_graw, h + 1)
                    act.wait_ge(s_gpool, h + 1)
                    act.activation(gms[0][:, :, :], gm[:, :, :], ACT.Identity).then_inc(s_ghi, 1)

                def query(p, par):
                    act.wait_ge(s_qmm, p + 1)
                    act.activation(q[par][0][:, :], bq[:, :], ACT.Identity, bias=gb[:, :]).then_inc(s_qhi, 1)

                def exps(s, b):
                    act.wait_ge(s_max, s + 1)
                    for i in range(2):
                        m = act.activation(pr[b][:, i, :], bs[b % 2][:, i * S:(i + 1) * S], ACT.Exp,
                                           bias=nmax[b][:, i:i + 1], accum_out=rsum[b][:, i:i + 1])
                    m.then_inc(s_exp, 1)

                def probs(s, b):
                    act.wait_ge(s_tmm, s + 1)
                    act.activation(pt[b][0][:, :, :], bt[b % 2][:, :].rearrange("p (a n) -> p a n", a=2),
                                   ACT.Identity).then_inc(s_thi, 1)

                def outs(p, par):
                    act.wait_ge(s_pv, 2 * p + 2)
                    act.activation(o[par][0][:, :], bo[:, :], ACT.Identity).then_inc(s_ohi, 1)

                def round_(h, b):
                    s = 4 * h + b
                    if b == 0 and has(2 * h + 1, NPAIR) and not (isinstance(h, int) and h == 0):
                        query(2 * h + 1, 1)
                    if b == 2 and has(2 * h + 2, NPAIR):
                        query(2 * h + 2, 0)
                    if b % 2 and has(2 * h - 2 + b // 2, NPAIR):
                        outs(2 * h - 2 + b // 2, b // 2)
                    if has(s - 2, NS):
                        probs(s - 2, (b - 2) % 4)
                    if has(s, NS):
                        exps(s, b)
                    if b == 1 and has(h + 1, NH):
                        merged(h + 1)

                merged(0)
                query(0, 0)
                query(1, 1)
                run(act, round_)

            @block.vector
            def _(dve):
                def merged_raw(h):
                    dve.wait_ge(s_gmm, h + 1)
                    dve.tensor_scalar(gm[:, :, 0:KVL], bq[:, 0:2 * KVL].rearrange("p (a n) -> p a n", a=2), SCALE0,
                                      None, ALU.mult)
                    dve.wait_ge(s_gpool, h + 1)
                    dve.tensor_scalar(gb[0:KVL, :], bq[0:KVL, 2 * KVL:2 * KVL + 1], SCALE0, None,
                                      ALU.mult).then_inc(s_graw, 1)

                def merged_lo(h):
                    dve.wait_ge(s_ghi, h + 1)
                    dve.tensor_tensor(gms[1][:, :, :], gm[:, :, :], f32(gms[0][:, :, :]), ALU.subtract)\
                       .then_inc(s_glo, 1)

                def query(p, par):
                    dve.wait_ge(s_qhi, p + 1)
                    dve.scalar_tensor_tensor(out=q[par][1][:, :], in0=bq[:, :], scalar=gb[:, 0:1],
                                             in1=f32(q[par][0][:, :]), op0=ALU.add, op1=ALU.subtract)\
                       .then_inc(s_qlo, 1)

                def maxes(s, b):
                    dve.wait_ge(s_smm, s + 1)
                    dve.tensor_reduce(nmax[b][:, :], bs[b % 2][:, :].rearrange("p (a n) -> p a n", a=2), AX,
                                      ALU.max, negate=True).then_inc(s_max, 1)

                def inverse(s, b):
                    dve.wait_ge(s_exp, s + 1)
                    dve.reciprocal(rinv[b][:, :], rsum[b][:, :]).then_inc(s_inv, 1)

                def probs(s, b):
                    dve.wait_ge(s_thi, s + 1)
                    dve.tensor_tensor(pt[b][1][:, :, :], bt[b % 2][:, :].rearrange("p (a n) -> p a n", a=2),
                                      f32(pt[b][0][:, :, :]), ALU.subtract).then_inc(s_tlo, 1)

                def outs(p, par):
                    dve.wait_ge(s_ohi, p + 1)
                    dve.tensor_tensor(o[par][1][:, :], bo[:, :], f32(o[par][0][:, :]), ALU.subtract)\
                       .then_inc(s_olo, 1)

                def round_(h, b):
                    s = 4 * h + b
                    if has(s - 1, NS):
                        inverse(s - 1, (b - 1) % 4)
                    if has(s, NS):
                        maxes(s, b)
                    if b == 1 and has(h + 1, NH):
                        merged_raw(h + 1)
                    if b == 0 and has(2 * h + 1, NPAIR) and not (isinstance(h, int) and h == 0):
                        query(2 * h + 1, 1)
                    if b == 2 and has(2 * h + 2, NPAIR):
                        query(2 * h + 2, 0)
                    if b % 2 and has(2 * h - 2 + b // 2, NPAIR):
                        outs(2 * h - 2 + b // 2, b // 2)
                    if has(s - 2, NS):
                        probs(s - 2, (b - 2) % 4)
                    if b == 1 and has(h + 1, NH):
                        merged_lo(h + 1)

                merged_raw(0)
                merged_lo(0)
                query(0, 0)
                query(1, 1)
                run(dve, round_)

            @block.tensor
            def _(pe):
                def merge(h):
                    pe.wait_ge(s_w, 16 * h + 16)
                    need(pe, s_qlo, 2 * h)
                    for a in range(2):
                        pe.matmul(bq[:, a * KVL:(a + 1) * KVL], w[:, a * P:(a + 1) * P], wk, start=(a == 0),
                                  stop=True, skip_group_check=True)
                    pe.matmul(bq[0:KVL, 2 * KVL:2 * KVL + 1], wk, bcols[:, 0:1], start=False, stop=True,
                              skip_group_check=True).then_inc(s_gmm, 1)

                def query(h, p, c):
                    pe.wait_ge(s_glo, h + 1)
                    need(pe, s_qlo, p)
                    tok = slice(c * HALF, (c + 1) * HALF)
                    matmul3(pe, bq[:, :], (gms[0][:, 0, :], gms[1][:, 0, :]), (qa[0][:, tok], qa[1][:, tok]), True,
                            False)
                    pe.matmul(bq[:, :], gms[0][:, 1, :], qb[:, tok], start=False, stop=False, skip_group_check=True)
                    pe.matmul(bq[:, :], gms[1][:, 1, :], qb[:, tok], start=False, stop=True, skip_group_check=True)\
                      .then_inc(s_qmm, 1)

                def scores(s, p, b):
                    pe.wait_ge(s_qlo, p + 1)
                    need(pe, s_exp, s - 1)
                    par = b // 2
                    keys = slice(b * S, (b + 1) * S)
                    for i in range(2):
                        a = (b % 2) * S + i * P
                        m = matmul3(pe, bs[b % 2][:, i * S:(i + 1) * S],
                                    (q[par][0][:, a:a + P], q[par][1][:, a:a + P]),
                                    (kv[0][:, keys], kv[1][:, keys]), i == 0, i == 1)
                    m.then_inc(s_smm, 1)

                def turn(s, b):
                    pe.wait_ge(s_norm, s + 1)
                    need(pe, s_tlo, s - 1)
                    for kt in range(2):
                        for i in range(2):
                            m = pe.transpose(bt[b % 2][:, kt * S + i * P:kt * S + (i + 1) * P],
                                             pr[b][:, i, kt * P:(kt + 1) * P], ident[:, :])
                    m.then_inc(s_tmm, 1)

                def values(s, p, b):
                    pe.wait_ge(s_tlo, s + 1)
                    if b % 2 == 0:
                        need(pe, s_olo, p)
                    out = bo[:, (b % 2) * S:(b % 2 + 1) * S]
                    for kt in range(2):
                        for j in range(2):
                            m = pe.matmul(out, cs[:, 2 * b + kt, :], pt[b][j][:, kt, :],
                                          start=(b % 2 == 0 and kt == 0 and j == 0), stop=(kt == 1 and j == 1),
                                          skip_group_check=True)
                    m.then_inc(s_pv, 1)

                def project(h, p, c):
                    pe.wait_ge(s_olo, p + 1)
                    pe.wait_ge(s_wvl, h + 1)
                    matmul3(pe, acc[c][:, :], (wvs[0][:, :], wvs[1][:, :]), (o[c][0][:, :], o[c][1][:, :]), False,
                            False).then_inc(s_om, 1)

                def round_(h, b):
                    s = 4 * h + b
                    if has(s + 1, NS):
                        scores(s + 1, 2 * h + (b + 1) // 2, (b + 1) % 4)
                    if b == 3 and has(h + 1, NH):
                        query(h + 1, 2 * h + 3, 1)
                    if b == 0 and has(h - 2, NH):
                        project(h - 2, 2 * h - 3, 1)
                    if b == 2 and has(h - 1, NH):
                        project(h - 1, 2 * h - 2, 0)
                    if has(s - 1, NS):
                        turn(s - 1, (b - 1) % 4)
                    if has(s - 3, NS):
                        values(s - 3, 2 * h + (b - 3) // 2, (b - 3) % 4)
                    if b == 0 and has(h + 1, NH):
                        merge(h + 1)
                    if b == 1 and has(h + 1, NH):
                        query(h + 1, 2 * h + 2, 0)

                merge(0)
                query(0, 0, 0)
                query(0, 1, 1)
                scores(0, 0, 0)
                run(pe, round_)


def attention0_out(nc, k, io, g, lat):
    res, acc = g["res"], lat["acc"]
    with ExitStack() as ctx:
        t = Kit(nc, ctx, "o")
        wo = t.sb("wo", [P, HID])
        bv = t.sb("bv", [P, NH])
        bvs = t.sb("bvs", [P, 1])
        bo = t.sb("bo", [P, HID])
        os = t.sb("os", [P, T])
        banks = [t.ps(f"b{i}") for i in range(2)]
        s_in, s_b, s_os, s_pre, s_mm, s_add = (k.sem(x) for x in ("oo_in", "oo_b", "oo_os", "oo_pre", "oo_mm", "oo_add"))
        with nc.Block() as block:
            @block.sync
            def _(sp):
                sp.dma_start(bv[:, :], io["bv0"]).then_inc(s_in, 16)
                sp.dma_start(wo[:, :], io["wo0"]).then_inc(s_in, 16)
                sp.dma_start(bo[:, :], io["bo0"][None, :].to_broadcast([P, HID])).then_inc(s_in, 16)

            @block.gpsimd
            def _(pool):
                pool.wait_ge(s_in, 48)
                for j in range(NT):
                    pool.tensor_tensor(res[:, j, :], res[:, j, :], bo[:, :], ALU.add).then_inc(s_pre, 1)

            @block.vector
            def _(dve):
                dve.wait_ge(s_in, 48)
                dve.tensor_reduce(bvs[:, :], bv[:, :], AX, ALU.add).then_inc(s_b, 1)
                for j in range(NT):
                    dve.wait_ge(s_mm, j + 1)
                    dve.wait_ge(s_pre, j + 1)
                    dve.tensor_tensor(res[:, j, :], banks[j % 2][:, :], res[:, j, :], ALU.add).then_inc(s_add, 1)

            @block.scalar
            def _(act):
                act.wait_ge(s_b, 1)
                for c in range(2):
                    act.activation(os[:, c * HALF:(c + 1) * HALF], acc[c][:, :], ACT.Identity, bias=bvs[:, :])\
                       .then_inc(s_os, 1)

            @block.tensor
            def _(pe):
                pe.wait_ge(s_in, 48)
                for j in range(NT):
                    pe.wait_ge(s_os, j // 4 + 1)
                    need(pe, s_add, j - 1)
                    pe.matmul(banks[j % 2][:, :], os[:, j * P:(j + 1) * P], wo[:, :], start=True, stop=True)\
                      .then_inc(s_mm, 1)


def layernorm(nc, k, g, nth):
    res, ident = g["res"], g["ident"]
    xhi, xlo = g["xT"]
    st = k.sb("st", [P, 6])
    mv = k.sb("mv", [P, 2])
    rs = k.sb("rs", [P, 1])
    mh = k.sb("mh", [P, 1])
    xn = k.sb("xn", [P, 2, HID])
    banks = [k.ps(f"b{i}") for i in range(2)]
    s_tick = g["tick"]
    s_c, s_st, s_mv, s_add, s_rs, s_xn, s_cp, s_t, s_hi, s_lo = g["ln"].values()
    base = nth * NT
    with nc.Block() as block:
        @block.gpsimd
        def _(pool):
            pool.memset(mh[:, :], -0.5).then_inc(s_c, 1)
            pool.wait_ge(s_c, nth + 1)
            def round_(i):
                for u in range(2):
                    j = 2 * i + u
                    need(pool, s_add, base + j + 1)
                    pool.tensor_tensor(rs[:, :], mv[:, 1:2], mh[:, :], ALU.pow).then_inc(s_rs, 1)
                    need(pool, s_xn, base + j + 1)
                    plain(pool, s_tick)
                    pool.tensor_copy(res[:, bass.ds(j, 1), :].rearrange("p a n -> p (a n)"), xn[:, u, :])\
                        .then_inc(s_cp, 1)

            loop(pool, NT // 2, round_)

        @block.vector
        def _(dve):
            def round_(i):
                for u in range(2):
                    j = 2 * i + u
                    row = res[:, bass.ds(j, 1), :].rearrange("p a n -> p (a n)")
                    dve.bn_stats(st[:, :], row).then_inc(s_st, 1)
                    need(dve, s_st, base + j + 1)
                    plain(dve, s_tick)
                    dve.bn_aggr(mv[:, :], st[:, :]).then_inc(s_mv, 1)
                    need(dve, s_mv, base + j + 1)
                    dve.tensor_scalar(mv[:, 1:2], mv[:, 1:2], EPS, None, ALU.add).then_inc(s_add, 1)
                    need(dve, s_rs, base + j + 1)
                    need(dve, s_t, base + 2 * i)
                    need(dve, s_cp, base + 2 * i)
                    dve.tensor_scalar(xn[:, u, :], row, mv[:, 0:1], rs[:, 0:1], ALU.subtract, ALU.mult)\
                       .then_inc(s_xn, 1)
                    need(dve, s_hi, base + j + 1)
                    dve.tensor_tensor(xlo[:, :, bass.ds(j * P, P)], banks[u][:, :].rearrange("p (c n) -> p c n", c=KC),
                                      f32(xhi[:, :, bass.ds(j * P, P)]), ALU.subtract).then_inc(s_lo, 1)

            loop(dve, NT // 2, round_)

        @block.scalar
        def _(act):
            def round_(i):
                for u in range(2):
                    j = 2 * i + u
                    need(act, s_t, base + j + 1)
                    act.activation(xhi[:, :, bass.ds(j * P, P)], banks[u][:, :].rearrange("p (c n) -> p c n", c=KC),
                                   ACT.Identity).then_inc(s_hi, 1)

            loop(act, NT // 2, round_)

        @block.tensor
        def _(pe):
            def round_(i):
                for u in range(2):
                    j = 2 * i + u
                    need(pe, s_xn, base + j + 1)
                    need(pe, s_lo, base + 2 * i)
                    for c in range(KC):
                        m = pe.transpose(banks[u][:, c * P:(c + 1) * P], xn[:, u, c * P:(c + 1) * P], ident[:, :])
                    m.then_inc(s_t, 1)

            loop(pe, NT // 2, round_)


def ffn0(nc, k, io, g):
    res = g["res"]
    xhi, xlo = g["xT"]
    wi = k.sb("wi", [P, 3, HID], I32)
    ws = (k.sb("w_hi", [P, 3, HID], F32R), k.sb("w_lo", [P, 3, HID], F32R))
    gs = k.sb("gs", [P, NI])
    us = k.sb("us", [P, NI])
    ds = k.sb("ds", [P, HID])
    act_g = k.sb("act_g", [P, HALF])
    h = k.sb("h", [P, HALF])
    hs = (k.sb("h_hi", [P, HALF], F32R), k.sb("h_lo", [P, HALF], F32R))
    y = k.sb("y", [P, 2, HID])
    bg, bu = k.ps("bg"), k.ps("bu")
    bd = [k.ps(f"bd{i}") for i in range(4)]
    s_sc = k.sem("sc_in")
    s_in = [k.sem(f"w{i}_in") for i in range(3)]
    s_whi = [k.sem(f"w{i}_hi") for i in range(3)]
    s_wlo = [k.sem(f"w{i}_lo") for i in range(3)]
    s_mm = [k.sem(f"mm{i}") for i in range(3)]
    s_sg, s_h, s_hhi, s_hlo, s_y, s_res = (k.sem(x) for x in ("sg", "h", "h_hi", "h_lo", "y", "res"))
    N = 2 * NI

    with nc.Block() as block:
        @block.sync
        def _(sp):
            sp.dma_start(gs[:, :], io["gate_scale"]).then_inc(s_sc, 16)
            sp.dma_start(us[:, :], io["up_scale"]).then_inc(s_sc, 16)
            sp.dma_start(ds[:, :], io["down_scale"][None, :].to_broadcast([P, HID])).then_inc(s_sc, 16)
            for c in range(2):
                def round_(i):
                    n = c * NI + i
                    for j in range(3):
                        need(sp, s_wlo[j], n)
                        sp.dma_start(wi[:, j, :], io["w_ffn0"][bass.ds(i, 1), :, j * HID:(j + 1) * HID]
                                     .rearrange("a p n -> (a p) n")).then_inc(s_in[j], 16)

                loop(sp, NI, round_)

        @block.scalar
        def _(act):
            act.preload_act_table(ACT.Silu)
            act.wait_ge(s_sc, 48)

            def whi(j, n):
                act.wait_ge(s_in[j], 16 * n + 16)
                need(act, s_mm[j], n)
                act.activation(ws[0][:, j, :], wi[:, j, :], ACT.Identity).then_inc(s_whi[j], 1)

            for c in range(2):
                def round_(i):
                    n = c * NI + i
                    whi(0, n)
                    whi(1, n)
                    need(act, s_mm[0], n + 1)
                    need(act, s_h, n)
                    act.activation(act_g[:, :], bg[:, :], ACT.Silu, scale=gs[:, bass.ds(i, 1)]).then_inc(s_sg, 1)
                    need(act, s_h, n + 1)
                    need(act, s_mm[2], n)
                    act.activation(hs[0][:, :], h[:, :], ACT.Identity).then_inc(s_hhi, 1)
                    whi(2, n)

                loop(act, NI, round_)

        @block.vector
        def _(dve):
            dve.wait_ge(s_sc, 48)

            def wlo(j, n):
                dve.wait_ge(s_whi[j], n + 1)
                dve.tensor_tensor(ws[1][:, j, :], wi[:, j, :], f32(ws[0][:, j, :]), ALU.subtract).then_inc(s_wlo[j], 1)

            for c in range(2):
                def round_(i):
                    n = c * NI + i
                    wlo(0, n)
                    wlo(1, n)
                    need(dve, s_sg, n + 1)
                    need(dve, s_mm[1], n + 1)
                    need(dve, s_hlo, n)
                    dve.scalar_tensor_tensor(out=h[:, :], in0=bu[:, :], scalar=us[:, bass.ds(i, 1)], in1=act_g[:, :],
                                             op0=ALU.mult, op1=ALU.mult).then_inc(s_h, 1)
                    need(dve, s_hhi, n + 1)
                    dve.tensor_tensor(hs[1][:, :], h[:, :], f32(hs[0][:, :]), ALU.subtract).then_inc(s_hlo, 1)
                    wlo(2, n)

                loop(dve, NI, round_)
                dve.wait_ge(s_mm[2], (c + 1) * NI)
                for j in range(4):
                    if c or j >= 2:
                        dve.wait_ge(s_res, 4 * c + j - 1)
                    dve.tensor_tensor(y[:, j % 2, :], bd[j][:, :], ds[:, :], ALU.mult).then_inc(s_y, 1)

        @block.gpsimd
        def _(pool):
            for c in range(2):
                for j in range(4):
                    pool.wait_ge(s_y, 4 * c + j + 1)
                    pool.tensor_tensor(res[:, 4 * c + j, :], y[:, j % 2, :], res[:, 4 * c + j, :], ALU.add)\
                        .then_inc(s_res, 1)

        @block.tensor
        def _(pe):
            def wide(j, bank, n, tok):
                pe.wait_ge(s_wlo[j], n + 1)
                for kc in range(KC):
                    w = tuple(x[:, j, kc * P:(kc + 1) * P] for x in ws)
                    m = matmul3(pe, bank[:, :], w, (xhi[:, kc, tok], xlo[:, kc, tok]), kc == 0, kc == KC - 1)
                m.then_inc(s_mm[j], 1)

            def down(n, first):
                pe.wait_ge(s_hlo, n + 1)
                pe.wait_ge(s_wlo[2], n + 1)
                for j in range(4):
                    hh = tuple(x[:, j * P:(j + 1) * P] for x in hs)
                    m = matmul3(pe, bd[j][:, :], hh, (ws[0][:, 2, :], ws[1][:, 2, :]), first, False)
                m.then_inc(s_mm[2], 1)

            for c in range(2):
                tok = slice(c * HALF, (c + 1) * HALF)

                def step(i, first=False, second=False):
                    n = c * NI + i
                    need(pe, s_sg, n)
                    wide(0, bg, n, tok)
                    need(pe, s_h, n)
                    wide(1, bu, n, tok)
                    if not first:
                        down(n - 1, second)

                step(0, first=True)
                if c:
                    pe.wait_ge(s_y, 4)
                step(1, second=True)
                with pe.Fori(2, NI) as i:
                    step(i)
                down(c * NI + NI - 1, False)


def attention1(nc, k, io, g):
    res, ident = g["res"], g["ident"]
    xhi, xlo = g["xT"]
    PIECES = [("q0", 512), ("k0", 512), ("q1", 512), ("k1", 512), ("v", 1024), ("o", 1024)]
    off, a = {}, 0
    for name, n in PIECES:
        off[name] = a
        a += n
    raw = {n: k.sb(f"raw_{n}", [P, m]) for n, m in PIECES}
    ws = {n: (k.sb(f"w{n}_hi", [P, m], F32R), k.sb(f"w{n}_lo", [P, m], F32R)) for n, m in PIECES}
    qk = [(k.sb(f"qk{i}_hi", [P, 4, HALF], F32R), k.sb(f"qk{i}_lo", [P, 4, HALF], F32R)) for i in range(2)]
    v = [(k.sb(f"v{i}_hi", [P, 4, 2 * DV], F32R), k.sb(f"v{i}_lo", [P, 4, 2 * DV], F32R)) for i in range(2)]
    oT = [(k.sb(f"oT{i}_hi", [P, 2, HALF], F32R), k.sb(f"oT{i}_lo", [P, 2, HALF], F32R)) for i in range(2)]
    pr = k.sb("pr", [P, 3 * P])
    pt = (k.sb("pt_hi", [P, 3 * P], F32R), k.sb("pt_lo", [P, 3 * P], F32R))
    mask = k.sb("mask", [P, P])
    nmax, rsum, rinv = k.sb("nmax", [P, 2]), k.sb("rsum", [P, 2]), k.sb("rinv", [P, 2])
    bj = [k.ps(f"bj{i}") for i in range(3)]
    bs = [k.ps(f"bs{i}") for i in range(2)]
    bt = k.ps("bt")
    bo = [k.ps(f"bo{i}") for i in range(2)]
    s_in = {n: k.sem(f"in_{n}") for n, _ in PIECES}
    s_whi = {n: k.sem(f"whi_{n}") for n, _ in PIECES}
    s_wlo = {n: k.sem(f"wlo_{n}") for n, _ in PIECES}
    s_mask, s_tick = k.sem("mask"), g["tick"]
    s_jmm = [k.sem(f"jmm{i}") for i in range(3)]
    s_jhi = [k.sem(f"jhi{i}") for i in range(3)]
    s_jlo = [k.sem(f"jlo{i}") for i in range(3)]
    s_smm, s_mk, s_max, s_exp, s_inv, s_norm = (k.sem(x) for x in ("smm", "mk", "max", "exp", "inv", "norm"))
    s_tmm, s_thi, s_tlo, s_pv, s_ohi, s_olo = (k.sem(x) for x in ("tmm", "thi", "tlo", "pv", "ohi", "olo"))
    QK = ("q0", "k0", "q1", "k1")

    def sweep(eng, prologue, body, epilogue):
        for t in range(4):
            prologue(t)
        body(0, True, False)
        with eng.Fori(1, NG - 1) as gr:
            body(gr, False, False)
        body(NG - 1, False, True)
        epilogue()

    with nc.Block() as block:
        @block.sync
        def _(sp):
            def round_(gr):
                for n in ("q0", "k0", "v", "q1", "k1", "o"):
                    m = dict(PIECES)[n]
                    need(sp, s_wlo[n], gr)
                    sp.dma_start(raw[n][:, :], io["w_attn1"][bass.ds(gr, 1), :, off[n]:off[n] + m]
                                 .rearrange("a p n -> (a p) n")).then_inc(s_in[n], 16)

            loop(sp, NG, round_)

        @block.gpsimd
        def _(pool):
            pool.memset(mask[:, :], 0.0).then_inc(s_mask, 1)
            pool.wait_ge(s_mask, 1)
            pool.affine_select(out=mask[:, :], in_=mask[:, :], compare_op=ALU.is_ge, fill=-1e30, base=0,
                               pattern=[[-1, P]], channel_multiplier=1).then_inc(s_mask, 1)

            def split(n, gr, used):
                pool.wait_ge(s_in[n], 16 * gr + 16)
                for sem, value in used:
                    need(pool, sem, value)
                plain(pool, s_tick)
                pool.tensor_copy(ws[n][0][:, :], raw[n][:, :]).then_inc(s_whi[n], 1)
                pool.wait_ge(s_whi[n], gr + 1)
                pool.tensor_tensor(ws[n][1][:, :], raw[n][:, :], f32(ws[n][0][:, :]), ALU.subtract)\
                    .then_inc(s_wlo[n], 1)

            def body(gr, last):
                r = 4 + 8 * gr
                if not last:
                    split("q0", gr + 1, [(s_jmm[0], r + 1)])
                    split("k0", gr + 1, [(s_jmm[0], r + 2)])
                    split("v", gr + 1, [(s_jmm[2], r + 2)])
                    split("q1", gr + 1, [(s_jmm[0], r + 3)])
                    split("k1", gr + 1, [(s_jmm[0], r + 4)])
                split("o", gr, [(s_jmm[2], r + 4)])

            for n in ("q0", "k0", "v", "q1", "k1"):
                split(n, 0, [])
            def round_(gr):
                body(gr, False)

            loop(pool, NG - 1, round_)
            body(NG - 1, True)

        def proj_kinds(t, has_next, has_prev):
            kinds = [("qk", 0)] if has_next else []
            if t < 2 and has_next:
                kinds += [("v", 1), ("v", 2)]
            if t >= 2 and has_prev:
                kinds += [("o", 1), ("o", 2)]
            return kinds

        @block.tensor
        def _(pe):
            def project(kind, bank, r, gr, t, c):
                need(pe, s_jlo[bank], r)
                if kind == "qk":
                    n = QK[t]
                    pe.wait_ge(s_wlo[n], gr + 1)
                    for kc in range(KC):
                        w = tuple(x[:, kc * P:(kc + 1) * P] for x in ws[n])
                        tok = slice(c * HALF, (c + 1) * HALF)
                        m = matmul3(pe, bj[0][:, :], w, (xhi[:, kc, tok], xlo[:, kc, tok]), kc == 0, kc == KC - 1)
                elif kind == "v":
                    pe.wait_ge(s_wlo["v"], gr + 1)
                    a = c * HALF + (2 * t + bank - 1) * P
                    for kc in range(KC):
                        x = (xhi[:, kc, a:a + P], xlo[:, kc, a:a + P])
                        w = tuple(y[:, kc * 2 * DV:(kc + 1) * 2 * DV] for y in ws["v"])
                        m = matmul3(pe, bj[bank][:, 0:2 * DV], x, w, kc == 0, kc == KC - 1)
                else:
                    pe.wait_ge(s_wlo["o"], gr + 1)
                    a = (2 * (t - 2) + bank - 1) * P
                    for hd in range(2):
                        o = tuple(x[:, hd, a:a + P] for x in oT[c])
                        w = tuple(x[:, hd * HID:(hd + 1) * HID] for x in ws["o"])
                        m = matmul3(pe, bj[bank][:, :], o, w, hd == 0, hd == 1)
                m.then_inc(s_jmm[bank], 1)

            def skip(bank, r):
                need(pe, s_jlo[bank], r)
                pe.sem_inc(s_jmm[bank], 1)

            def step(s, r, gr, c, t, has_next, has_prev, attend=True):
                b, hd = t // 2, t % 2
                par = c
                nxt = (gr, 1) if c == 0 else (gr + 1, 0)
                prv = (gr - 1, 1) if c == 0 else (gr, 0)
                kinds = dict((bank, kind) for kind, bank in proj_kinds(t, has_next, has_prev))
                if not attend:
                    nxt = (0, 0)
                if attend:
                    if t == 0:
                        need(pe, s_jlo[0], r)
                        need(pe, s_jlo[2], r)
                    need(pe, s_exp, s - 1)
                    q = [tuple(x[:, 2 * hd, b * S + i * P:b * S + (i + 1) * P] for x in qk[par]) for i in range(2)]
                    kk = [tuple(x[:, 2 * hd + 1, b * S:b * S + (i + 1) * P] for x in qk[par]) for i in range(2)]
                    matmul3(pe, bs[t % 2][:, 0:P], q[0], kk[0], True, False)
                    matmul3(pe, bs[t % 2][:, P:3 * P], q[1], kk[1], False, True).then_inc(s_smm, 1)
                for bank in range(3):
                    if bank == 1 and attend:
                        pe.wait_ge(s_norm, s + 1)
                        need(pe, s_tlo, s)
                        for i in range(3):
                            m = pe.transpose(bt[:, i * P:(i + 1) * P], pr[:, i * P:(i + 1) * P], ident[:, :])
                        m.then_inc(s_tmm, 1)
                    if bank in kinds:
                        project(kinds[bank], bank, r, *(prv if kinds[bank] == "o" else nxt)[:1], t,
                                (prv if kinds[bank] == "o" else nxt)[1])
                    else:
                        skip(bank, r)
                if attend:
                    pe.wait_ge(s_tlo, s + 1)
                    need(pe, s_olo, s - 1)
                    out = bo[t % 2]
                    for kt in range(2):
                        vv = tuple(x[:, 2 * b + kt, hd * DV:(hd + 1) * DV] for x in v[par])
                        p = tuple(x[:, 2 * kt * P:(2 + kt) * P] for x in pt)
                        m = matmul3(pe, out[:, kt * P:2 * P], vv, p, kt == 0, kt == 1)
                    m.then_inc(s_pv, 1)

            def body(gr, first, last):
                for c in range(2):
                    for t in range(4):
                        s = 8 * gr + 4 * c + t
                        step(s, s + 4, gr, c, t, not (last and c == 1), not (first and c == 0))

            def epilogue():
                for t in (2, 3):
                    r = 8 * NG + 4 + t - 2
                    for bank in (1, 2):
                        if t == 2:
                            pe.wait_ge(s_olo, 8 * NG)
                        project("o", bank, r, NG - 1, t, 1)

            sweep(pe, lambda t: step(None, t, 0, 0, t, True, False, attend=False), body, epilogue)

        @block.scalar
        def _(act):
            def spill(kind, bank, r, t, c):
                act.wait_ge(s_jmm[bank], r + 1)
                if kind == "qk":
                    act.activation(qk[c][0][:, t, :], bj[0][:, :], ACT.Identity,
                                   scale=SCALE1 if t % 2 == 0 else 1.0).then_inc(s_jhi[0], 1)
                elif kind == "v":
                    act.activation(v[c][0][:, 2 * t + bank - 1, :], bj[bank][:, 0:2 * DV], ACT.Identity)\
                       .then_inc(s_jhi[bank], 1)

            def step(s, r, c, t, has_next, has_prev, attend=True):
                hd = t % 2
                if attend:
                    if not (isinstance(s, int) and s == 0):
                        outs(s - 1, (t - 1) % 4, c if t else 1 - c)
                    act.wait_ge(s_max, s + 1)
                    for i in range(2):
                        m = act.activation(pr[:, i * P:(2 * i + 1) * P], bs[t % 2][:, i * P:(2 * i + 1) * P], ACT.Exp,
                                           bias=nmax[:, i:i + 1], accum_out=rsum[:, i:i + 1])
                    m.then_inc(s_exp, 1)
                kinds = proj_kinds(t, has_next, has_prev)
                nc_ = 1 - c if attend else 0
                for kind, bank in kinds:
                    if bank == 0:
                        spill(kind, bank, r, t, nc_)
                if attend:
                    act.wait_ge(s_tmm, s + 1)
                    act.activation(pt[0][:, :], bt[:, 0:3 * P], ACT.Identity).then_inc(s_thi, 1)
                for kind, bank in kinds:
                    if kind == "v":
                        spill(kind, bank, r, t, nc_)

            def outs(s, t, c):
                act.wait_ge(s_pv, s + 1)
                b, hd = t // 2, t % 2
                act.activation(oT[c][0][:, hd, b * S:(b + 1) * S], bo[t % 2][:, 0:S], ACT.Identity)\
                   .then_inc(s_ohi, 1)

            def body(gr, first, last):
                for c in range(2):
                    for t in range(4):
                        s = 8 * gr + 4 * c + t
                        step(s, s + 4, c, t, not (last and c == 1), not (first and c == 0))

            sweep(act, lambda t: step(None, t, 0, t, True, False, attend=False), body,
                  lambda: outs(8 * NG - 1, 3, 1))

        @block.vector
        def _(dve):
            hi_count = {0: 0, 1: 0, 2: 0}

            def store(kind, bank, r, gr, t, c):
                if kind == "qk":
                    dve.wait_ge(s_jhi[0], r + 1)
                    if t % 2 == 0:
                        m = dve.scalar_tensor_tensor(out=qk[c][1][:, t, :], in0=bj[0][:, :], scalar=SCALE1,
                                                     in1=f32(qk[c][0][:, t, :]), op0=ALU.mult, op1=ALU.subtract)
                    else:
                        m = dve.tensor_tensor(qk[c][1][:, t, :], bj[0][:, :], f32(qk[c][0][:, t, :]), ALU.subtract)
                elif kind == "v":
                    dve.wait_ge(s_jhi[bank], (r - t) // 2 + t + 1)
                    j = 2 * t + bank - 1
                    m = dve.tensor_tensor(v[c][1][:, j, :], bj[bank][:, 0:2 * DV], f32(v[c][0][:, j, :]),
                                          ALU.subtract)
                else:
                    dve.wait_ge(s_jmm[bank], r + 1)
                    j = 4 * c + 2 * (t - 2) + bank - 1
                    m = dve.tensor_tensor(res[:, j, :], bj[bank][:, :], res[:, j, :], ALU.add)
                m.then_inc(s_jlo[bank], 1)

            def outs(s, t, c):
                dve.wait_ge(s_ohi, s + 1)
                b, hd = t // 2, t % 2
                dve.tensor_tensor(oT[c][1][:, hd, b * S:(b + 1) * S], bo[t % 2][:, 0:S],
                                  f32(oT[c][0][:, hd, b * S:(b + 1) * S]), ALU.subtract).then_inc(s_olo, 1)

            def step(s, r, c, t, has_next, has_prev, attend=True):
                kinds = dict((bank, kind) for kind, bank in proj_kinds(t, has_next, has_prev))
                if attend:
                    if not (isinstance(s, int) and s == 0):
                        outs(s - 1, (t - 1) % 4, c if t else 1 - c)
                    dve.wait_ge(s_smm, s + 1)
                    sc = bs[t % 2][:, :].rearrange("p (a n) -> p a n", n=S)
                    both = mask[:, :][:, None, :].to_broadcast([P, 2, P])
                    dve.tensor_tensor(sc[:, :, 0:P], sc[:, :, 0:P], both, ALU.add).then_inc(s_mk, 1)
                    dve.wait_ge(s_mk, s + 1)
                    dve.tensor_reduce(nmax[:, 0:1], bs[t % 2][:, 0:P], AX, ALU.max, negate=True)
                    dve.tensor_reduce(nmax[:, 1:2], bs[t % 2][:, P:3 * P], AX, ALU.max, negate=True)\
                       .then_inc(s_max, 1)
                    dve.wait_ge(s_exp, s + 1)
                    dve.reciprocal(rinv[:, :], rsum[:, :]).then_inc(s_inv, 1)
                    dve.wait_ge(s_inv, s + 1)
                    dve.tensor_scalar(pr[:, 0:P], pr[:, 0:P], rinv[:, 0:1], None, ALU.mult)
                    dve.tensor_scalar(pr[:, P:3 * P], pr[:, P:3 * P], rinv[:, 1:2], None, ALU.mult)\
                       .then_inc(s_norm, 1)
                for bank in range(3):
                    if bank == 1 and attend:
                        dve.wait_ge(s_thi, s + 1)
                        dve.tensor_tensor(pt[1][:, :], bt[:, 0:3 * P], f32(pt[0][:, :]), ALU.subtract)\
                           .then_inc(s_tlo, 1)
                    if bank in kinds:
                        kind = kinds[bank]
                        store(kind, bank, r, None, t, (1 - c) if attend else 0)
                    else:
                        dve.wait_ge(s_jmm[bank], r + 1)
                        dve.sem_inc(s_jlo[bank], 1)

            def body(gr, first, last):
                for c in range(2):
                    for t in range(4):
                        s = 8 * gr + 4 * c + t
                        step(s, s + 4, c, t, not (last and c == 1), not (first and c == 0))

            def epilogue():
                outs(8 * NG - 1, 3, 1)
                for t in (2, 3):
                    for bank in (1, 2):
                        store("o", bank, 8 * NG + 4 + t - 2, None, t, 1)

            dve.wait_ge(s_mask, 2)
            sweep(dve, lambda t: step(None, t, 0, t, True, False, attend=False), body, epilogue)


def ffn1(nc, k, io, g):
    res, ident = g["res"], g["ident"]
    NW = KC * W1F
    wraw = k.sb("wraw", [P, KC, W1F])
    ws = (k.sb("w_hi", [P, KC, W1F], F32R), k.sb("w_lo", [P, KC, W1F], F32R))
    braw = k.sb("braw", [P, HID])
    bm = (k.sb("bm_hi", [P, HID], F32R), k.sb("bm_lo", [P, HID], F32R))
    bb = k.sb("bb", [P, HID])
    mh = k.sb("mh", [P, 1])
    st, mv, rs = k.sb("st", [P, 6]), k.sb("mv", [P, 2]), k.sb("rs", [P, 1])
    st2, mv2, rs2 = k.sb("st2", [P, 6]), k.sb("mv2", [P, 2]), k.sb("rs2", [P, 1])
    x = k.sb("x", [P, HID])
    xb = k.sb("xb", [P, HID])
    xT = (k.sb("xT_hi", [P, HID], F32R), k.sb("xT_lo", [P, HID], F32R))
    qs = k.sb("qs", [P, E * DK])
    prod = k.sb("prod", [P, E * DK])
    sc, nm, nms, ex = k.sb("sc", [P, E]), k.sb("nm", [P, 1]), k.sb("nms", [P, 1]), k.sb("ex", [P, E])
    sm, ri = k.sb("sm", [P, 1]), k.sb("ri", [P, 1])
    gate = k.sb("gate", [P, E])
    wh = k.sb("wh", [P, E, R])
    whT = (k.sb("whT_hi", [P, P], F32R), k.sb("whT_lo", [P, P], F32R))
    y = k.sb("y", [P, HID])
    yo = k.sb("yo", [P, HID])
    bx, bqk, bh, br, bw = (k.ps(n) for n in ("bx", "bqk", "bh", "br", "bw"))
    s_in, s_whi, s_wlo, s_c = (k.sem(n) for n in ("in", "whi", "wlo", "c"))
    s_tick = g["tick"]
    s_v, s_rs, s_x, s_xb, s_tx, s_xhi, s_xlo = (k.sem(n) for n in ("v", "rs", "x", "xb", "tx", "xhi", "xlo"))
    s_qk, s_h, s_r, s_q, s_d, s_ex, s_wh, s_tw, s_whT, s_whl, s_y, s_rs2, s_yo, s_out = (
        k.sem(n) for n in ("qk", "h", "r", "q", "d", "ex", "wh", "tw", "whT", "whl", "y", "rs2", "yo", "out"))
    inv = float(DK) ** -0.5
    out = io["out"].rearrange("(t p) n -> t p n", p=P)
    ND = 12
    with nc.Block() as block:
        @block.sync
        def _(sp):
            sp.dma_start(wraw[:, :, :], io["w_ffn1"].rearrange("(c p) n -> p c n", p=P)).then_inc(s_in, 16)
            sp.dma_start(braw[:, :], io["bm1"]).then_inc(s_in, 16)
            sp.dma_start(bb[:, :], io["b1"][None, :].to_broadcast([P, HID])).then_inc(s_in, 16)
            def round_(i):
                need(sp, s_yo, i + 1)
                sp.dma_start(out[bass.ds(i, 1), :, :].rearrange("a p n -> (a p) n"), yo[:, :]).then_inc(s_out, 16)

            loop(sp, NT, round_)
            sp.wait_ge(s_out, 16 * NT)

        @block.gpsimd
        def _(pool):
            pool.memset(mh[:, :], -0.5).then_inc(s_c, 1)
            pool.wait_ge(s_c, 1)
            pool.wait_ge(s_in, 48)
            def round_(i):
                need(pool, s_v, 2 * i + 1)
                pool.tensor_tensor(rs[:, :], mv[:, 1:2], mh[:, :], ALU.pow).then_inc(s_rs, 1)
                need(pool, s_x, i + 1)
                pool.tensor_tensor(xb[:, :], x[:, :], bb[:, :], ALU.add).then_inc(s_xb, 1)
                need(pool, s_v, 2 * i + 2)
                pool.tensor_tensor(rs2[:, :], mv2[:, 1:2], mh[:, :], ALU.pow).then_inc(s_rs2, 1)

            loop(pool, NT, round_)

        @block.scalar
        def _(act):
            act.preload_act_table(ACT.Exp)
            act.wait_ge(s_in, 48)
            for c in range(KC):
                act.activation(ws[0][:, c, :], wraw[:, c, :], ACT.Identity).then_inc(s_whi, 1)
            act.activation(bm[0][:, :], braw[:, :], ACT.Identity).then_inc(s_whi, 1)
            def round_(i):
                need(act, s_tx, i + 1)
                act.activation(xT[0][:, :], bx[:, :], ACT.Identity).then_inc(s_xhi, 1)
                need(act, s_qk, i + 1)
                act.activation(qs[:, :], bqk[:, 0:E * DK], ACT.Identity).then_inc(s_q, 1)
                need(act, s_d, ND * i + 7)
                act.activation(ex[:, :], sc[:, :], ACT.Exp, bias=nms[:, :], scale=inv, accum_out=sm[:, :])\
                   .then_inc(s_ex, 1)
                need(act, s_tw, i + 1)
                act.activation(whT[0][:, :], bw[:, 0:P], ACT.Identity).then_inc(s_whT, 1)

            loop(act, NT, round_)

        @block.vector
        def _(dve):
            for c in range(KC):
                dve.wait_ge(s_whi, c + 1)
                dve.tensor_tensor(ws[1][:, c, :], wraw[:, c, :], f32(ws[0][:, c, :]), ALU.subtract).then_inc(s_wlo, 1)
            dve.wait_ge(s_whi, KC + 1)
            dve.tensor_tensor(bm[1][:, :], braw[:, :], f32(bm[0][:, :]), ALU.subtract).then_inc(s_wlo, 1)
            def round_(i):
                n = [0]

                def chain(m):
                    n[0] += 1
                    m.then_inc(s_d, 1)
                    need(dve, s_d, ND * i + n[0])
                    plain(dve, s_tick)

                row = res[:, bass.ds(i, 1), :].rearrange("p a n -> p (a n)")
                chain(dve.bn_stats(st[:, :], row))
                chain(dve.bn_aggr(mv[:, :], st[:, :]))
                dve.tensor_scalar(mv[:, 1:2], mv[:, 1:2], EPS, None, ALU.add).then_inc(s_v, 1)
                need(dve, s_rs, i + 1)
                need(dve, s_xb, i)
                dve.tensor_scalar(x[:, :], row, mv[:, 0:1], rs[:, 0:1], ALU.subtract, ALU.mult).then_inc(s_x, 1)
                need(dve, s_xhi, i + 1)
                dve.tensor_tensor(xT[1][:, :], bx[:, :], f32(xT[0][:, :]), ALU.subtract).then_inc(s_xlo, 1)
                need(dve, s_q, i + 1)
                chain(dve.tensor_tensor(prod[:, :], bqk[:, E * DK:2 * E * DK], qs[:, :], ALU.mult))
                chain(dve.tensor_reduce(sc[:, :], prod[:, :].rearrange("p (e d) -> p e d", e=E), AX, ALU.add))
                chain(dve.tensor_reduce(nm[:, :], sc[:, :], AX, ALU.max, negate=True))
                chain(dve.tensor_scalar(nms[:, :], nm[:, :], inv, None, ALU.mult))
                chain(dve.tensor_copy(nm[:, :], nms[:, :]))
                need(dve, s_ex, i + 1)
                chain(dve.reciprocal(ri[:, :], sm[:, :]))
                chain(dve.tensor_scalar(gate[:, :], ex[:, :], ri[:, 0:1], None, ALU.mult))
                need(dve, s_h, i + 1)
                dve.tensor_tensor(wh[:, :, :], bh[:, 0:P].rearrange("p (e r) -> p e r", e=E),
                                  gate[:, :][:, :, None].to_broadcast([P, E, R]), ALU.mult).then_inc(s_wh, 1)
                need(dve, s_whT, i + 1)
                dve.tensor_tensor(whT[1][:, :], bw[:, 0:P], f32(whT[0][:, :]), ALU.subtract).then_inc(s_whl, 1)
                need(dve, s_r, i + 1)
                need(dve, s_xb, i + 1)
                chain(dve.tensor_tensor(y[:, :], br[:, :], xb[:, :], ALU.add))
                chain(dve.bn_stats(st2[:, :], y[:, :]))
                chain(dve.bn_aggr(mv2[:, :], st2[:, :]))
                dve.tensor_scalar(mv2[:, 1:2], mv2[:, 1:2], EPS, None, ALU.add).then_inc(s_v, 1)
                need(dve, s_rs2, i + 1)
                need(dve, s_out, 16 * i)
                dve.tensor_scalar(yo[:, :], y[:, :], mv2[:, 0:1], rs2[:, 0:1], ALU.subtract, ALU.mult)\
                   .then_inc(s_yo, 1)

            loop(dve, NT, round_)

        @block.tensor
        def _(pe):
            pe.wait_ge(s_wlo, KC + 1)

            def wide(bank, a, n, stop):
                for c in range(KC):
                    m = matmul3(pe, bank[:, 0:n], tuple(z[:, c * P:(c + 1) * P] for z in xT),
                                tuple(z[:, c, a:a + n] for z in ws), c == 0, stop and c == KC - 1)
                return m

            def round_(i):
                need(pe, s_x, i + 1)
                for c in range(KC):
                    m = pe.transpose(bx[:, c * P:(c + 1) * P], x[:, c * P:(c + 1) * P], ident[:, :])
                m.then_inc(s_tx, 1)
                need(pe, s_xlo, i + 1)
                wide(bqk, HID, 2 * E * DK, True).then_inc(s_qk, 1)
                wide(bh, HID + 2 * E * DK, E * R, True).then_inc(s_h, 1)
                wide(br, 0, HID, False)
                need(pe, s_wh, i + 1)
                pe.transpose(bw[:, 0:P], wh[:, :, :].rearrange("p e r -> p (e r)"), ident[:, :]).then_inc(s_tw, 1)
                need(pe, s_whl, i + 1)
                matmul3(pe, br[:, :], (whT[0][:, :], whT[1][:, :]), (bm[0][:, :], bm[1][:, :]), False, True)\
                    .then_inc(s_r, 1)
                need(pe, s_yo, i + 1)

            loop(pe, NT, round_)


def _lay_out(i):
    c = np.ascontiguousarray
    f = np.float32
    a = {n: np.asarray(x) for n, x in i.items()}
    x = a["L0_attn_hidden_size"].reshape(T, HID)
    wqc, wkc = a["L0_attn_Wq_c"], a["L0_attn_Wkv_c"]
    bqc, bkc = a["L0_attn_bq_c"], a["L0_attn_bkv_c"]
    o = {"x": x, "xT": x.T}
    o["w_down0"] = np.concatenate([wqc.T, wqc[P:].T, wkc.T], 1)
    o["b_down0"] = np.stack([bqc[:P], np.concatenate([bqc[P:], bqc[P:]]), bkc], 1)
    wq = a["L0_attn_Wq_up"].reshape(NH, NOPE + ROPE, QL)
    bq = a["L0_attn_bq_up"].reshape(NH, NOPE + ROPE)
    wkv = a["L0_attn_Wkv_up"].reshape(NH, NOPE + VH, KVL)
    bkv = a["L0_attn_bkv_up"].reshape(NH, NOPE + VH)
    nope, rope = wq[:, :NOPE], wq[:, NOPE:].transpose(0, 2, 1)
    bias = np.zeros((NH, P, 2), f)
    bias[:, :, 0] = bq[:, :NOPE]
    bias[:, KVL:, 1] = bq[:, NOPE:]
    o["w_head0"] = np.concatenate([nope, nope[:, :, P:], wkv[:, :NOPE], rope[:, :P], np.concatenate(
        [rope[:, P:], rope[:, P:]], 1), bias], 2)
    wv = wkv[:, NOPE:].transpose(0, 2, 1)
    o["wv_head0"] = np.concatenate([wv, wv], 1)
    o["bv0"] = bkv[:, NOPE:].T
    o["wo0"] = a["L0_attn_Wo"].T
    o["bo0"] = a["L0_attn_bo"]

    gw, uw, dw = (a[f"L0_ffn_{n}_wq"] for n in ("gate", "up", "down"))
    blocks = np.zeros((NI, P, 3 * HID), gw.dtype)
    pad = np.zeros((NI * P, HID), gw.dtype)
    for j, w in enumerate((gw, uw)):
        pad[:INTER] = w
        blocks[:, :, j * HID:(j + 1) * HID] = pad.reshape(NI, P, KC, P).transpose(0, 3, 2, 1).reshape(NI, P, HID)
    pad[:INTER] = dw.T
    blocks[:, :, 2 * HID:] = pad.reshape(NI, P, HID)
    o["w_ffn0"] = blocks
    for n in ("gate", "up"):
        s = np.zeros(NI * P, f)
        s[:INTER] = a[f"L0_ffn_{n}_scale"]
        o[f"{n}_scale"] = s.reshape(NI, P).T
    o["down_scale"] = a["L0_ffn_down_scale"]

    wq1 = a["L1_attn_wq"].reshape(KC, P, NG, 2, DN + DR)[..., :DN]
    wkv1 = a["L1_attn_wkv"]
    wk1 = wkv1[:, :NH * DN].reshape(KC, P, NG, 2, DN)
    wv1 = wkv1[:, NH * DN:NH * (DN + DV)].reshape(KC, P, NG, 2 * DV)
    wo1 = a["L1_attn_wo"].reshape(NG, 2, P, HID)
    piece = lambda w: w.transpose(2, 1, 0, 3).reshape(NG, P, -1)
    o["w_attn1"] = np.concatenate([piece(wq1[:, :, :, 0]), piece(wk1[:, :, :, 0]), piece(wq1[:, :, :, 1]),
                                   piece(wk1[:, :, :, 1]), piece(wv1),
                                   wo1.transpose(0, 2, 1, 3).reshape(NG, P, -1)], 2)
    o["w_ffn1"] = np.concatenate([a["L1_ffn_W"].T, a["L1_ffn_Wq"].T, a["L1_ffn_Wk"].T,
                                  a["L1_ffn_A"].reshape(E * R, HID).T], 1)
    o["bm1"] = a["L1_ffn_Bm"].transpose(0, 2, 1).reshape(E * R, HID)
    o["b1"] = a["L1_ffn_b"]
    return {n: c(x) for n, x in o.items()}


def kernel(**inputs):
    import concourse.bacc as _bacc
    from concourse.bass_utils import run_bass_kernel_spmd as _run

    nc = _bacc.Bacc("TRN2", target_bir_lowering=False, num_devices=1)
    arrays = {f"in_{n}": x for n, x in _lay_out(inputs).items()}
    io = {n[3:]: nc.dram_tensor(n, x.shape, mybir.dt.from_np(x.dtype), kind="ExternalInput").ap()
          for n, x in arrays.items()}
    io["out"] = nc.dram_tensor("out", (T, HID), F32, kind="ExternalOutput").ap()
    build(nc, io)
    r = _run(nc, [arrays], core_ids=[0])
    return r.results[0]["out"].reshape(NB, S, HID)
```

```python
from contextlib import ExitStack

import numpy as np

import concourse.bass as bass
from concourse import mybir

F32 = mybir.dt.float32
F32R = mybir.dt.float32r
I32 = mybir.dt.int32
ALU = mybir.AluOpType
ACT = mybir.ActivationFunctionType
AX = mybir.AxisListType.X

P = 128
NB, S, HID = 4, 256, 512
T = NB * S
NT = T // P
KC = HID // P
HALF = 512
EPS = 1e-5

NH = 32
QL, KVL, NOPE, ROPE, VH = 192, 64, 128, 64, 128
SCALE0 = float(NOPE + ROPE) ** -0.5
W0 = 2 * P + KVL + 2 * ROPE + 2

INTER = 1376
NI = -(-INTER // P)

DN, DR, DV = 128, 64, 128
SCALE1 = float(DN + DR) ** -0.5
NG = NH // 2

E, DK, R = 8, 32, 16
W1F = HID + 2 * E * DK + E * R


def f32(ap):
    return ap.bitcast(F32)


def need(eng, sem, value):
    if isinstance(value, int) and value <= 0:
        return
    eng.wait_ge(sem, value)


def loop(eng, n, body):
    body(0)
    with eng.Fori(1, n) as i:
        body(i)


def plain(eng, sem):
    eng.sem_inc(sem, 1)


def has(x, n):
    return not isinstance(x, int) or 0 <= x < n


def matmul3(pe, out, w, x, start, stop):
    pe.matmul(out, w[0], x[0], start=start, stop=False, skip_group_check=True)
    pe.matmul(out, w[0], x[1], start=False, stop=False, skip_group_check=True)
    return pe.matmul(out, w[1], x[0], start=False, stop=stop, skip_group_check=True)


class Kit:

    def __init__(self, nc, ctx, tag):
        self.nc, self.ctx, self.tag = nc, ctx, tag

    def sb(self, name, shape, dt=F32):
        return self.ctx.enter_context(self.nc.sbuf_tensor(f"{self.tag}_{name}", shape, dt))

    def ps(self, name):
        return self.ctx.enter_context(self.nc.psum_tensor(f"{self.tag}_{name}", [P, 512], F32))

    def sem(self, name):
        return self.ctx.enter_context(self.nc.semaphore(f"{self.tag}_{name}"))


def build(nc, io):
    with ExitStack() as ctx:
        k = Kit(nc, ctx, "g")
        g = {
            "res": k.sb("res", [P, NT, HID]),
            "xT": (k.sb("xT_hi", [P, KC, T], F32R), k.sb("xT_lo", [P, KC, T], F32R)),
            "ident": k.sb("ident", [P, P]),
            "tick": k.sem("tick"),
            "ln": {n: k.sem(n) for n in ("c", "st", "mv", "add", "rs", "xn", "t", "hi", "lo")},
        }
        sems = ctx.enter_context(ExitStack())

        def kit(tag, memory):
            new = Kit(nc, memory, tag)
            new.sem = Kit(nc, sems, tag).sem
            return new

        with ExitStack() as m:
            a = kit("a", m)
            latent = attention0_prepare(nc, a, io, g)
            attention0_heads(nc, a, io, g, latent)
            attention0_out(nc, a, io, g, latent)
        with ExitStack() as m:
            f = FFN0(nc, kit("f", m), io, g)
            with ExitStack() as m2:
                layernorm(nc, kit("n0", m2), g, 0, f)
            f.run()
        with ExitStack() as m:
            e = kit("e", m)
            raw = ffn1_raw(e)
            with ExitStack() as m2:
                b = Attention1(nc, kit("b", m2), io, g, raw)
                with ExitStack() as m3:
                    layernorm(nc, kit("n1", m3), g, 1, b)
                b.run()
            ffn1(nc, e, io, g, raw)


def attention0_prepare(nc, k, io, g):
    res, ident = g["res"], g["ident"]
    xhi, xlo = g["xT"]
    qa = (k.sb("qa_hi", [P, T], F32R), k.sb("qa_lo", [P, T], F32R))
    qb = k.sb("qb", [P, T], F32R)
    kv = (k.sb("kv_hi", [P, T], F32R), k.sb("kv_lo", [P, T], F32R))
    cs = k.sb("cs", [P, NT, P], F32R)
    acc0 = k.ps("acc0")
    acc1 = k.ps("acc1")
    with ExitStack() as ctx:
        t = Kit(nc, ctx, "p")
        xraw = t.sb("xraw", [P, KC, T])
        wraw = t.sb("wraw", [P, KC, 3 * P])
        whi = t.sb("whi", [P, KC, 3 * P], F32R)
        wlo = t.sb("wlo", [P, KC, 3 * P], F32R)
        kvraw = t.sb("kvraw", [P, T])
        bias = t.sb("bias", [P, 3])
        zero = t.sb("zero", [P, P])
        banks = [t.ps(f"b{i}") for i in range(4)]
        s_x, s_w = k.sem("x_in"), k.sem("w_in")
        s_xk = [k.sem(f"xk{i}") for i in range(KC)]
        s_res = k.sem("res_in")
        s_id, s_whi, s_wlo = k.sem("ident"), k.sem("whi"), k.sem("wlo")
        s_xhi, s_xlo = k.sem("xhi"), k.sem("xlo")
        s_mm, s_hi, s_lo = k.sem("p_mm"), k.sem("p_hi"), k.sem("p_lo")
        s_raw, s_tr, s_chi, s_clo = k.sem("p_raw"), k.sem("p_tr"), k.sem("p_chi"), k.sem("p_clo")
        chunks = [(m, n) for m in (2, 0, 1) for n in range(2)]
        with nc.Block() as block:
            @block.sync
            def _(sp):
                sp.dma_start(wraw[:, :, :], io["w_down0"].rearrange("(c p) n -> p c n", p=P)).then_inc(s_w, 16)
                for c in range(KC):
                    sp.dma_start(xraw[:, c, :], io["xT"][c * P:(c + 1) * P, :]).then_inc(s_xk[c], 16)
                sp.dma_start(bias[:, :], io["b_down0"]).then_inc(s_x, 16)
                sp.dma_start(res[:, :, :], io["x"].rearrange("(t p) n -> p t n", p=P)).then_inc(s_res, 16)
                sp.wait_ge(s_res, 16)

            @block.gpsimd
            def _(pool):
                pool.memset(ident[:, :], 0.0).then_inc(s_id, 1)
                pool.memset(zero[:, :], 0.0).then_inc(s_id, 1)
                pool.wait_ge(s_id, 2)
                pool.affine_select(out=ident[:, :], in_=ident[:, :], compare_op=ALU.not_equal, fill=1.0, base=0,
                                   pattern=[[-1, P]], channel_multiplier=1).then_inc(s_id, 1)

            @block.scalar
            def _(act):
                act.wait_ge(s_w, 16)
                act.activation(whi[:, :, :], wraw[:, :, :], ACT.Identity).then_inc(s_whi, 1)
                for c in range(KC):
                    act.wait_ge(s_xk[c], 16)
                    act.activation(xhi[:, c, :], xraw[:, c, :], ACT.Identity).then_inc(s_xhi, 1)
                act.wait_ge(s_x, 16)
                for i, (m, n) in enumerate(chunks):
                    tok = slice(n * HALF, (n + 1) * HALF)
                    act.wait_ge(s_mm, i + 1)
                    if m == 2:
                        act.activation(kvraw[:, tok], banks[i % 2][:, :], ACT.Identity,
                                       bias=bias[:, m:m + 1]).then_inc(s_raw, 1)
                        act.wait_ge(s_raw, n + 1)
                        act.activation(kv[0][:, tok], kvraw[:, tok], ACT.Identity).then_inc(s_hi, 1)
                    else:
                        out = qa[0] if m == 0 else qb
                        act.activation(out[:, tok], banks[i % 2][:, :], ACT.Identity,
                                       bias=bias[:, m:m + 1]).then_inc(s_hi, 1)
                for n in range(2):
                    act.wait_ge(s_tr, n + 1)
                    src = banks[2 + n][:, :].rearrange("p (t l) -> p t l", l=P)
                    act.activation(cs[:, 4 * n:4 * n + 4, 0:KVL], src[:, :, 0:KVL], ACT.Identity).then_inc(s_chi, 1)

            @block.vector
            def _(dve):
                dve.wait_ge(s_whi, 1)
                dve.tensor_tensor(wlo[:, :, :], wraw[:, :, :], f32(whi[:, :, :]), ALU.subtract).then_inc(s_wlo, 1)
                for c in range(KC):
                    dve.wait_ge(s_xhi, c + 1)
                    dve.tensor_tensor(xlo[:, c, :], xraw[:, c, :], f32(xhi[:, c, :]), ALU.subtract).then_inc(s_xlo, 1)
                dve.wait_ge(s_x, 16)
                for i, (m, n) in enumerate(chunks):
                    tok = slice(n * HALF, (n + 1) * HALF)
                    dve.wait_ge(s_hi, i + 1)
                    if m == 2:
                        dve.tensor_tensor(kv[1][:, tok], kvraw[:, tok], f32(kv[0][:, tok]),
                                          ALU.subtract).then_inc(s_lo, 1)
                    else:
                        r = slice(0, P) if m == 0 else slice(QL - P, P)
                        hi, lo = (qa[0], qa[1]) if m == 0 else (qb, qb)
                        dve.scalar_tensor_tensor(out=lo[r, tok], in0=banks[i % 2][r, :], scalar=bias[r, m:m + 1],
                                                 in1=f32(hi[r, tok]), op0=ALU.add, op1=ALU.subtract).then_inc(s_lo, 1)
                for n in range(2):
                    dve.wait_ge(s_chi, n + 1)
                    src = banks[2 + n][:, :].rearrange("p (t l) -> p t l", l=P)
                    dve.tensor_tensor(cs[:, 4 * n:4 * n + 4, KVL:P], src[:, :, 0:KVL],
                                      f32(cs[:, 4 * n:4 * n + 4, 0:KVL]), ALU.subtract).then_inc(s_clo, 1)

            @block.tensor
            def _(pe):
                pe.wait_ge(s_wlo, 1)
                for i, (m, n) in enumerate(chunks):
                    need(pe, s_lo, i - 1)
                    tok = slice(n * HALF, (n + 1) * HALF)
                    for c in range(KC):
                        if i == 0:
                            pe.wait_ge(s_xlo, c + 1)
                        w = (whi[:, c, m * P:(m + 1) * P], wlo[:, c, m * P:(m + 1) * P])
                        mm = matmul3(pe, banks[i % 2][:, :], w, (xhi[:, c, tok], xlo[:, c, tok]), c == 0, c == KC - 1)
                    mm.then_inc(s_mm, 1)
                pe.wait_ge(s_id, 3)
                pe.wait_ge(s_raw, 2)
                for n in range(2):
                    for j in range(4):
                        a = (4 * n + j) * P
                        mm = pe.transpose(banks[2 + n][:, j * P:(j + 1) * P], kvraw[:, a:a + P], ident[:, :])
                    mm.then_inc(s_tr, 1)
                for acc in (acc0, acc1):
                    for j in range(4):
                        pe.matmul(acc[:, j * P:(j + 1) * P], zero[:, :], zero[:, :], start=(j == 0), stop=False,
                                  skip_group_check=True)
    return dict(qa=qa, qb=qb, kv=kv, cs=cs, acc=(acc0, acc1))


def attention0_heads(nc, k, io, g, lat):
    qa, qb, kv, cs, acc = lat["qa"], lat["qb"], lat["kv"], lat["cs"], lat["acc"]
    ident = g["ident"]
    NS, NPAIR = NB * NH, 2 * NH
    with ExitStack() as ctx:
        t = Kit(nc, ctx, "h")
        w = t.sb("w", [P, W0])
        wk = w[:, 2 * P:2 * P + KVL]
        rope = w[:, 2 * P + KVL:2 * P + KVL + 2 * ROPE].rearrange("p (a n) -> p a n", a=2)
        bcols = w[:, W0 - 2:W0]
        wv = t.sb("wv", [P, VH])
        wvs = (t.sb("wv_hi", [P, VH], F32R), t.sb("wv_lo", [P, VH], F32R))
        gm = t.sb("gm", [P, 2, P])
        gms = (t.sb("gm_hi", [P, 2, P], F32R), t.sb("gm_lo", [P, 2, P], F32R))
        gb = t.sb("gb", [P, 1])
        q = [(t.sb(f"q{i}_hi", [P, HALF], F32R), t.sb(f"q{i}_lo", [P, HALF], F32R)) for i in range(2)]
        o = [(t.sb(f"o{i}_hi", [P, HALF], F32R), t.sb(f"o{i}_lo", [P, HALF], F32R)) for i in range(2)]
        pr = [t.sb(f"pr{i}", [P, 2, S]) for i in range(NB)]
        pt = [(t.sb(f"pt{i}_hi", [P, 2, S], F32R), t.sb(f"pt{i}_lo", [P, 2, S], F32R)) for i in range(NB)]
        nmax = [t.sb(f"nmax{i}", [P, 2]) for i in range(NB)]
        rsum = [t.sb(f"rsum{i}", [P, 2]) for i in range(NB)]
        rinv = [t.sb(f"rinv{i}", [P, 2]) for i in range(NB)]
        bq = t.ps("bq")
        bs = [t.ps(f"bs{i}") for i in range(2)]
        bt = [t.ps(f"bt{i}") for i in range(2)]
        bo = t.ps("bo")
        s_w, s_wv, s_tick = k.sem("w0_in"), k.sem("wv_in"), g["tick"]
        s_gmm, s_graw, s_gpool, s_ghi, s_glo = (k.sem(x) for x in ("g_mm", "g_raw", "g_pool", "g_hi", "g_lo"))
        s_qmm, s_qhi, s_qlo = k.sem("q_mm"), k.sem("q_hi"), k.sem("q_lo")
        s_smm, s_max, s_exp, s_inv, s_norm = (k.sem(x) for x in ("s_mm", "s_max", "s_exp", "s_inv", "s_norm"))
        s_tmm, s_thi, s_tlo = k.sem("t_mm"), k.sem("t_hi"), k.sem("t_lo")
        s_pv, s_ohi, s_olo = k.sem("pv"), k.sem("o_hi"), k.sem("o_lo")
        s_wvh, s_wvl, s_om = k.sem("wv_hi"), k.sem("wv_lo"), k.sem("om")

        def run(eng, round_):
            def head(h):
                for b in range(NB):
                    round_(h, b)

            head(0)
            head(1)
            with eng.Fori(2, NH - 1) as h:
                head(h)
            head(NH - 1)
            head(NH)
            round_(NH + 1, 0)

        with nc.Block() as block:
            @block.sync
            def _(sp):
                def fetch(h):
                    need(sp, s_graw, h)
                    need(sp, s_gpool, h)
                    sp.dma_start(w[:, :], io["w_head0"][bass.ds(h, 1), :, :].rearrange("a p n -> (a p) n"))\
                      .then_inc(s_w, 16)

                def fetch_wv(h):
                    need(sp, s_wvl, h)
                    sp.dma_start(wv[:, :], io["wv_head0"][bass.ds(h, 1), :, :].rearrange("a p n -> (a p) n"))\
                      .then_inc(s_wv, 16)

                def both(h):
                    fetch(h + 1)
                    fetch_wv(h)

                fetch(0)
                loop(sp, NH - 1, both)
                fetch_wv(NH - 1)

            @block.gpsimd
            def _(pool):
                def rope_part(h):
                    pool.wait_ge(s_w, 16 * h + 16)
                    need(pool, s_glo, h)
                    need(pool, s_qlo, 2 * h)
                    plain(pool, s_tick)
                    pool.tensor_scalar(gm[:, :, KVL:P], rope, SCALE0, None, ALU.mult)
                    pool.tensor_scalar(gb[:, :], bcols[:, 1:2], SCALE0, None, ALU.mult).then_inc(s_gpool, 1)

                def split_wv(h):
                    pool.wait_ge(s_wv, 16 * h + 16)
                    need(pool, s_om, 2 * h)
                    plain(pool, s_tick)
                    pool.tensor_copy(wvs[0][:, :], wv[:, :]).then_inc(s_wvh, 1)
                    pool.wait_ge(s_wvh, h + 1)
                    pool.tensor_tensor(wvs[1][:, :], wv[:, :], f32(wvs[0][:, :]), ALU.subtract).then_inc(s_wvl, 1)

                def norm(s, b):
                    pool.wait_ge(s_inv, s + 1)
                    pool.tensor_tensor(pr[b][:, :, :], pr[b][:, :, :],
                                       rinv[b][:, :][:, :, None].to_broadcast([P, 2, S]), ALU.mult)\
                        .then_inc(s_norm, 1)

                def round_(h, b):
                    s = 4 * h + b
                    if has(s - 1, NS):
                        norm(s - 1, (b - 1) % 4)
                    if b == 0 and has(h + 1, NH):
                        rope_part(h + 1)
                    if b == 1 and has(h - 1, NH):
                        split_wv(h - 1)

                rope_part(0)
                run(pool, round_)

            @block.scalar
            def _(act):
                def merged(h):
                    act.wait_ge(s_graw, h + 1)
                    act.wait_ge(s_gpool, h + 1)
                    act.activation(gms[0][:, :, :], gm[:, :, :], ACT.Identity).then_inc(s_ghi, 1)

                def query(p, par):
                    act.wait_ge(s_qmm, p + 1)
                    act.activation(q[par][0][:, :], bq[:, :], ACT.Identity, bias=gb[:, :]).then_inc(s_qhi, 1)

                def exps(s, b):
                    act.wait_ge(s_max, s + 1)
                    for i in range(2):
                        m = act.activation(pr[b][:, i, :], bs[b % 2][:, i * S:(i + 1) * S], ACT.Exp,
                                           bias=nmax[b][:, i:i + 1], accum_out=rsum[b][:, i:i + 1])
                    m.then_inc(s_exp, 1)

                def probs(s, b):
                    act.wait_ge(s_tmm, s + 1)
                    act.activation(pt[b][0][:, :, :], bt[b % 2][:, :].rearrange("p (a n) -> p a n", a=2),
                                   ACT.Identity).then_inc(s_thi, 1)

                def outs(p, par):
                    act.wait_ge(s_pv, 2 * p + 2)
                    act.activation(o[par][0][:, :], bo[:, :], ACT.Identity).then_inc(s_ohi, 1)

                def round_(h, b):
                    s = 4 * h + b
                    if b == 0 and has(2 * h + 1, NPAIR) and not (isinstance(h, int) and h == 0):
                        query(2 * h + 1, 1)
                    if b == 2 and has(2 * h + 2, NPAIR):
                        query(2 * h + 2, 0)
                    if b % 2 and has(2 * h - 2 + b // 2, NPAIR):
                        outs(2 * h - 2 + b // 2, b // 2)
                    if b == 1 and has(h + 1, NH):
                        merged(h + 1)
                    if has(s - 2, NS):
                        probs(s - 2, (b - 2) % 4)
                    if has(s, NS):
                        exps(s, b)

                merged(0)
                query(0, 0)
                query(1, 1)
                run(act, round_)

            @block.vector
            def _(dve):
                def merged_raw(h):
                    dve.wait_ge(s_gmm, h + 1)
                    dve.tensor_scalar(gm[:, :, 0:KVL], bq[:, 0:2 * KVL].rearrange("p (a n) -> p a n", a=2), SCALE0,
                                      None, ALU.mult)
                    dve.wait_ge(s_gpool, h + 1)
                    dve.tensor_scalar(gb[0:KVL, :], bq[0:KVL, 2 * KVL:2 * KVL + 1], SCALE0, None,
                                      ALU.mult).then_inc(s_graw, 1)

                def merged_lo(h):
                    dve.wait_ge(s_ghi, h + 1)
                    dve.tensor_tensor(gms[1][:, :, :], gm[:, :, :], f32(gms[0][:, :, :]), ALU.subtract)\
                       .then_inc(s_glo, 1)

                def query(p, par):
                    dve.wait_ge(s_qhi, p + 1)
                    dve.scalar_tensor_tensor(out=q[par][1][:, :], in0=bq[:, :], scalar=gb[:, 0:1],
                                             in1=f32(q[par][0][:, :]), op0=ALU.add, op1=ALU.subtract)\
                       .then_inc(s_qlo, 1)

                def maxes(s, b):
                    dve.wait_ge(s_smm, s + 1)
                    dve.tensor_reduce(nmax[b][:, :], bs[b % 2][:, :].rearrange("p (a n) -> p a n", a=2), AX,
                                      ALU.max, negate=True).then_inc(s_max, 1)

                def inverse(s, b):
                    dve.wait_ge(s_exp, s + 1)
                    dve.reciprocal(rinv[b][:, :], rsum[b][:, :]).then_inc(s_inv, 1)

                def probs(s, b):
                    dve.wait_ge(s_thi, s + 1)
                    dve.tensor_tensor(pt[b][1][:, :, :], bt[b % 2][:, :].rearrange("p (a n) -> p a n", a=2),
                                      f32(pt[b][0][:, :, :]), ALU.subtract).then_inc(s_tlo, 1)

                def outs(p, par):
                    dve.wait_ge(s_ohi, p + 1)
                    dve.tensor_tensor(o[par][1][:, :], bo[:, :], f32(o[par][0][:, :]), ALU.subtract)\
                       .then_inc(s_olo, 1)

                def round_(h, b):
                    s = 4 * h + b
                    if has(s - 1, NS):
                        inverse(s - 1, (b - 1) % 4)
                    if has(s, NS):
                        maxes(s, b)
                    if b == 1 and has(h + 1, NH):
                        merged_raw(h + 1)
                    if b == 0 and has(2 * h + 1, NPAIR) and not (isinstance(h, int) and h == 0):
                        query(2 * h + 1, 1)
                    if b == 2 and has(2 * h + 2, NPAIR):
                        query(2 * h + 2, 0)
                    if b % 2 and has(2 * h - 2 + b // 2, NPAIR):
                        outs(2 * h - 2 + b // 2, b // 2)
                    if b == 1 and has(h + 1, NH):
                        merged_lo(h + 1)
                    if has(s - 2, NS):
                        probs(s - 2, (b - 2) % 4)

                merged_raw(0)
                merged_lo(0)
                query(0, 0)
                query(1, 1)
                run(dve, round_)

            @block.tensor
            def _(pe):
                def merge(h):
                    pe.wait_ge(s_w, 16 * h + 16)
                    need(pe, s_qlo, 2 * h)
                    for a in range(2):
                        pe.matmul(bq[:, a * KVL:(a + 1) * KVL], w[:, a * P:(a + 1) * P], wk, start=(a == 0),
                                  stop=True, skip_group_check=True)
                    pe.matmul(bq[0:KVL, 2 * KVL:2 * KVL + 1], wk, bcols[:, 0:1], start=False, stop=True,
                              skip_group_check=True).then_inc(s_gmm, 1)

                def query(h, p, c):
                    pe.wait_ge(s_glo, h + 1)
                    need(pe, s_qlo, p)
                    tok = slice(c * HALF, (c + 1) * HALF)
                    matmul3(pe, bq[:, :], (gms[0][:, 0, :], gms[1][:, 0, :]), (qa[0][:, tok], qa[1][:, tok]), True,
                            False)
                    pe.matmul(bq[:, :], gms[0][:, 1, :], qb[:, tok], start=False, stop=False, skip_group_check=True)
                    pe.matmul(bq[:, :], gms[1][:, 1, :], qb[:, tok], start=False, stop=True, skip_group_check=True)\
                      .then_inc(s_qmm, 1)

                def scores(s, p, b):
                    pe.wait_ge(s_qlo, p + 1)
                    need(pe, s_exp, s - 1)
                    par = b // 2
                    keys = slice(b * S, (b + 1) * S)
                    for i in range(2):
                        a = (b % 2) * S + i * P
                        m = matmul3(pe, bs[b % 2][:, i * S:(i + 1) * S],
                                    (q[par][0][:, a:a + P], q[par][1][:, a:a + P]),
                                    (kv[0][:, keys], kv[1][:, keys]), i == 0, i == 1)
                    m.then_inc(s_smm, 1)

                def turn(s, b):
                    pe.wait_ge(s_norm, s + 1)
                    need(pe, s_tlo, s - 1)
                    for kt in range(2):
                        for i in range(2):
                            m = pe.transpose(bt[b % 2][:, kt * S + i * P:kt * S + (i + 1) * P],
                                             pr[b][:, i, kt * P:(kt + 1) * P], ident[:, :])
                    m.then_inc(s_tmm, 1)

                def values(s, p, b):
                    pe.wait_ge(s_tlo, s + 1)
                    if b % 2 == 0:
                        need(pe, s_olo, p)
                    out = bo[:, (b % 2) * S:(b % 2 + 1) * S]
                    for kt in range(2):
                        for j in range(2):
                            m = pe.matmul(out, cs[:, 2 * b + kt, :], pt[b][j][:, kt, :],
                                          start=(b % 2 == 0 and kt == 0 and j == 0), stop=(kt == 1 and j == 1),
                                          skip_group_check=True)
                    m.then_inc(s_pv, 1)

                def project(h, p, c):
                    pe.wait_ge(s_olo, p + 1)
                    pe.wait_ge(s_wvl, h + 1)
                    matmul3(pe, acc[c][:, :], (wvs[0][:, :], wvs[1][:, :]), (o[c][0][:, :], o[c][1][:, :]), False,
                            False).then_inc(s_om, 1)

                def round_(h, b):
                    s = 4 * h + b
                    if has(s + 1, NS):
                        scores(s + 1, 2 * h + (b + 1) // 2, (b + 1) % 4)
                    if b == 3 and has(h + 1, NH):
                        query(h + 1, 2 * h + 3, 1)
                    if b == 0 and has(h - 2, NH):
                        project(h - 2, 2 * h - 3, 1)
                    if b == 2 and has(h - 1, NH):
                        project(h - 1, 2 * h - 2, 0)
                    if has(s - 1, NS):
                        turn(s - 1, (b - 1) % 4)
                    if has(s - 3, NS):
                        values(s - 3, 2 * h + (b - 3) // 2, (b - 3) % 4)
                    if b == 0 and has(h + 1, NH):
                        merge(h + 1)
                    if b == 1 and has(h + 1, NH):
                        query(h + 1, 2 * h + 2, 0)

                merge(0)
                query(0, 0, 0)
                query(0, 1, 1)
                scores(0, 0, 0)
                run(pe, round_)


def attention0_out(nc, k, io, g, lat):
    res, acc = g["res"], lat["acc"]
    with ExitStack() as ctx:
        t = Kit(nc, ctx, "o")
        wo = t.sb("wo", [P, HID])
        bv = t.sb("bv", [P, NH])
        bvs = t.sb("bvs", [P, 1])
        bo = t.sb("bo", [P, HID])
        os = t.sb("os", [P, T])
        banks = [t.ps(f"b{i}") for i in range(2)]
        s_in, s_b, s_os, s_pre, s_mm, s_add = (k.sem(x) for x in ("oo_in", "oo_b", "oo_os", "oo_pre", "oo_mm", "oo_add"))
        with nc.Block() as block:
            @block.sync
            def _(sp):
                sp.dma_start(bv[:, :], io["bv0"]).then_inc(s_in, 16)
                sp.dma_start(wo[:, :], io["wo0"]).then_inc(s_in, 16)
                sp.dma_start(bo[:, :], io["bo0"][None, :].to_broadcast([P, HID])).then_inc(s_in, 16)

            @block.gpsimd
            def _(pool):
                pool.wait_ge(s_in, 48)
                for j in range(NT):
                    pool.tensor_tensor(res[:, j, :], res[:, j, :], bo[:, :], ALU.add).then_inc(s_pre, 1)

            @block.vector
            def _(dve):
                dve.wait_ge(s_in, 48)
                dve.tensor_reduce(bvs[:, :], bv[:, :], AX, ALU.add).then_inc(s_b, 1)
                for j in range(NT):
                    dve.wait_ge(s_mm, j + 1)
                    dve.wait_ge(s_pre, j + 1)
                    dve.tensor_tensor(res[:, j, :], banks[j % 2][:, :], res[:, j, :], ALU.add).then_inc(s_add, 1)

            @block.scalar
            def _(act):
                act.wait_ge(s_b, 1)
                for c in range(2):
                    act.activation(os[:, c * HALF:(c + 1) * HALF], acc[c][:, :], ACT.Identity, bias=bvs[:, :])\
                       .then_inc(s_os, 1)

            @block.tensor
            def _(pe):
                pe.wait_ge(s_in, 48)
                for j in range(NT):
                    pe.wait_ge(s_os, j // 4 + 1)
                    need(pe, s_add, j - 1)
                    pe.matmul(banks[j % 2][:, :], os[:, j * P:(j + 1) * P], wo[:, :], start=True, stop=True)\
                      .then_inc(s_mm, 1)


def moments(dve, pool, g, m, nth):
    base = nth * NT
    for q in range(2):
        js = range(4 * q, 4 * q + 4)
        if dve:
            for j in js:
                dve.bn_stats(m["st"][:, j, :], g["res"][:, j, :]).then_inc(g["ln"]["st"], 1)
            dve.wait_ge(g["ln"]["st"], base + 4 * q + 4)
            for j in js:
                dve.bn_aggr(m["mv"][:, j, :], m["st"][:, j, :]).then_inc(g["ln"]["mv"], 1)
            dve.wait_ge(g["ln"]["mv"], base + 4 * q + 4)
            var = m["mv"][:, 4 * q:4 * q + 4, 1]
            dve.tensor_scalar(var, var, EPS, None, ALU.add).then_inc(g["ln"]["add"], 1)
        if pool:
            if q == 0:
                pool.memset(m["mh"][:, :], -0.5).then_inc(g["ln"]["c"], 1)
                pool.wait_ge(g["ln"]["c"], nth + 1)
            pool.wait_ge(g["ln"]["add"], 2 * nth + q + 1)
            pool.tensor_tensor(m["rs"][:, 4 * q:4 * q + 4], m["mv"][:, 4 * q:4 * q + 4, 1], m["mh"][:, :], ALU.pow)\
                .then_inc(g["ln"]["rs"], 1)


def moment_memory(k):
    return {"st": k.sb("st", [P, NT, 6]), "mv": k.sb("mv", [P, NT, 2]), "rs": k.sb("rs", [P, NT]),
            "mh": k.sb("mh", [P, 4])}


def layernorm(nc, k, g, nth, after):
    res, ident = g["res"], g["ident"]
    xhi, xlo = g["xT"]
    m = moment_memory(k)
    banks = [k.ps(f"b{i}") for i in range(2)]
    s_rs, s_xn, s_t, s_hi, s_lo = (g["ln"][n] for n in ("rs", "xn", "t", "hi", "lo"))
    base = nth * NT

    def by_chunk(bank):
        return bank[:, :].rearrange("p (c n) -> p c n", c=KC)

    with nc.Block() as block:
        @block.sync
        def _(sp):
            after.first_loads(sp)

        @block.gpsimd
        def _(pool):
            moments(None, pool, g, m, nth)
            after.first_splits(pool)

        @block.vector
        def _(dve):
            def lo(j):
                dve.wait_ge(s_hi, base + j + 1)
                cols = slice(j * P, (j + 1) * P)
                dve.tensor_tensor(xlo[:, :, cols], by_chunk(banks[j % 2]), f32(xhi[:, :, cols]), ALU.subtract)\
                   .then_inc(s_lo, 1)

            moments(dve, None, g, m, nth)
            for j in range(NT):
                dve.wait_ge(s_rs, 2 * nth + j // 4 + 1)
                dve.tensor_scalar(res[:, j, :], res[:, j, :], m["mv"][:, j, 0:1], m["rs"][:, j:j + 1], ALU.subtract,
                                  ALU.mult).then_inc(s_xn, 1)
                if j:
                    lo(j - 1)
            lo(NT - 1)

        @block.scalar
        def _(act):
            for j in range(NT):
                act.wait_ge(s_t, base + j + 1)
                act.activation(xhi[:, :, j * P:(j + 1) * P], by_chunk(banks[j % 2]), ACT.Identity).then_inc(s_hi, 1)

        @block.tensor
        def _(pe):
            for j in range(NT):
                pe.wait_ge(s_xn, base + j + 1)
                need(pe, s_lo, base + j - 1)
                for c in range(KC):
                    t = pe.transpose(banks[j % 2][:, c * P:(c + 1) * P], res[:, j, c * P:(c + 1) * P], ident[:, :])
                t.then_inc(s_t, 1)


class FFN0:

    def __init__(self, nc, k, io, g):
        self.nc, self.io, self.g = nc, io, g
        self.wi = k.sb("wi", [P, 3, HID], I32)
        self.ws = (k.sb("w_hi", [P, 3, HID], F32R), k.sb("w_lo", [P, 3, HID], F32R))
        self.gs, self.us, self.ds = k.sb("gs", [P, NI]), k.sb("us", [P, NI]), k.sb("ds", [P, HID])
        self.sg, self.h = k.sb("sg", [P, HALF]), k.sb("h", [P, HALF])
        self.hs = (k.sb("h_hi", [P, HALF], F32R), k.sb("h_lo", [P, HALF], F32R))
        self.y = k.sb("y", [P, 2, HID])
        self.k = k
        self.s_sc = k.sem("sc_in")
        self.s_in = [k.sem(f"w{i}_in") for i in range(3)]
        self.s_whi = [k.sem(f"w{i}_hi") for i in range(3)]
        self.s_wlo = [k.sem(f"w{i}_lo") for i in range(3)]
        self.s_mm = [k.sem(f"mm{i}") for i in range(3)]

    def load(self, sp, n, i):
        for j in range(3):
            need(sp, self.s_wlo[j], n)
            sp.dma_start(self.wi[:, j, :], self.io["w_ffn0"][bass.ds(i, 1), :, j * HID:(j + 1) * HID]
                         .rearrange("a p n -> (a p) n")).then_inc(self.s_in[j], 16)

    def first_loads(self, sp):
        self.load(sp, 0, 0)
        sp.dma_start(self.gs[:, :], self.io["gate_scale"]).then_inc(self.s_sc, 16)
        sp.dma_start(self.us[:, :], self.io["up_scale"]).then_inc(self.s_sc, 16)
        sp.dma_start(self.ds[:, :], self.io["down_scale"][None, :].to_broadcast([P, HID])).then_inc(self.s_sc, 16)

    def first_splits(self, pool):
        pass

    def run(self):
        nc, k, g = self.nc, self.k, self.g
        wi, ws, gs, us, ds = self.wi, self.ws, self.gs, self.us, self.ds
        sg, h, hs, y = self.sg, self.h, self.hs, self.y
        s_sc, s_in, s_whi, s_wlo, s_mm = self.s_sc, self.s_in, self.s_whi, self.s_wlo, self.s_mm
        res = g["res"]
        xhi, xlo = g["xT"]
        bg, bu = k.ps("bg"), k.ps("bu")
        bd = [k.ps(f"bd{i}") for i in range(4)]
        s_sg, s_h, s_hhi, s_hlo, s_y, s_res = (k.sem(x) for x in ("sg", "h", "h_hi", "h_lo", "y", "res"))
        N = 2 * NI

        def rounds(eng, round_, peel):
            for c in range(2):
                lo, hi = c * NI, (c + 1) * NI
                first = [n for n in range(lo, hi) if n in peel and n < lo + 3]
                last = [n for n in range(lo, hi) if n in peel and n >= lo + 3]
                for n in first:
                    round_(n, n - lo)
                with eng.Fori(lo + len(first), hi - len(last)) as n:
                    round_(n, n - lo)
                for n in last:
                    round_(n, n - lo)

        with nc.Block() as block:
            @block.sync
            def _(sp):
                rounds(sp, lambda n, i: self.load(sp, n, i) if not (isinstance(n, int) and n == 0) else None, {0})

            @block.scalar
            def _(act):
                act.preload_act_table(ACT.Silu)
                act.wait_ge(s_sc, 48)

                def whi(j, n):
                    act.wait_ge(s_in[j], 16 * n + 16)
                    need(act, s_mm[j], n)
                    act.activation(ws[0][:, j, :], wi[:, j, :], ACT.Identity).then_inc(s_whi[j], 1)

                def hhi(n):
                    act.wait_ge(s_h, n + 1)
                    need(act, s_mm[2], n)
                    act.activation(hs[0][:, :], h[:, :], ACT.Identity).then_inc(s_hhi, 1)

                def round_(n, i):
                    if has(n - 1, N):
                        hhi(n - 1)
                        whi(2, n - 1)
                    if has(n, N):
                        act.wait_ge(s_mm[0], n + 1)
                        act.activation(sg[:, :], bg[:, :], ACT.Silu, scale=gs[:, bass.ds(i, 1)]).then_inc(s_sg, 1)
                        if has(n + 1, N):
                            whi(0, n + 1)
                            whi(1, n + 1)

                whi(0, 0)
                whi(1, 0)
                rounds(act, round_, {0, N - 1})
                round_(N, None)

            @block.vector
            def _(dve):
                dve.wait_ge(s_sc, 48)

                def wlo(j, n):
                    dve.wait_ge(s_whi[j], n + 1)
                    dve.tensor_tensor(ws[1][:, j, :], wi[:, j, :], f32(ws[0][:, j, :]), ALU.subtract)\
                       .then_inc(s_wlo[j], 1)

                def take(c):
                    dve.wait_ge(s_mm[2], (c + 1) * NI)
                    for j in range(4):
                        need(dve, s_res, 4 * c + j - 1)
                        dve.tensor_tensor(y[:, j % 2, :], bd[j][:, :], ds[:, :], ALU.mult).then_inc(s_y, 1)

                def round_(n, i):
                    if has(n - 1, N):
                        dve.wait_ge(s_hhi, n)
                        dve.tensor_tensor(hs[1][:, :], h[:, :], f32(hs[0][:, :]), ALU.subtract).then_inc(s_hlo, 1)
                        wlo(2, n - 1)
                    if isinstance(n, int) and n == NI + 1:
                        take(0)
                    if has(n, N):
                        if has(n + 1, N):
                            wlo(0, n + 1)
                        dve.wait_ge(s_sg, n + 1)
                        dve.wait_ge(s_mm[1], n + 1)
                        need(dve, s_hlo, n)
                        dve.scalar_tensor_tensor(out=h[:, :], in0=bu[:, :], scalar=us[:, bass.ds(i, 1)], in1=sg[:, :],
                                                 op0=ALU.mult, op1=ALU.mult).then_inc(s_h, 1)
                        if has(n + 1, N):
                            wlo(1, n + 1)

                wlo(0, 0)
                wlo(1, 0)
                rounds(dve, round_, {0, NI, NI + 1, N - 1})
                round_(N, None)
                take(1)

            @block.gpsimd
            def _(pool):
                for c in range(2):
                    for j in range(4):
                        pool.wait_ge(s_y, 4 * c + j + 1)
                        pool.tensor_tensor(res[:, 4 * c + j, :], y[:, j % 2, :], res[:, 4 * c + j, :], ALU.add)\
                            .then_inc(s_res, 1)

            @block.tensor
            def _(pe):
                def wide(j, bank, n, tok):
                    pe.wait_ge(s_wlo[j], n + 1)
                    for kc in range(KC):
                        w = tuple(x[:, j, kc * P:(kc + 1) * P] for x in ws)
                        m = matmul3(pe, bank[:, :], w, (xhi[:, kc, tok], xlo[:, kc, tok]), kc == 0, kc == KC - 1)
                    m.then_inc(s_mm[j], 1)

                def down(n):
                    first = isinstance(n, int) and n % NI == 0
                    pe.wait_ge(s_hlo, n + 1)
                    pe.wait_ge(s_wlo[2], n + 1)
                    for j in range(4):
                        hh = tuple(x[:, j * P:(j + 1) * P] for x in hs)
                        m = matmul3(pe, bd[j][:, :], hh, (ws[0][:, 2, :], ws[1][:, 2, :]), first, False)
                    m.then_inc(s_mm[2], 1)

                half = [0]

                def round_(n, i):
                    if isinstance(n, int):
                        half[0] = n // NI
                    tok = slice(half[0] * HALF, (half[0] + 1) * HALF)
                    need(pe, s_sg, n)
                    wide(0, bg, n, tok)
                    need(pe, s_h, n)
                    wide(1, bu, n, tok)
                    if isinstance(n, int) and n == NI + 1:
                        pe.wait_ge(s_y, 4)
                    if has(n - 1, N):
                        down(n - 1)

                rounds(pe, round_, {0, 1, NI, NI + 1})
                down(N - 1)


class Attention1:
    PIECES = {"q0": 512, "k0": 512, "v": 1024, "q1": 512, "k1": 512, "o": 1024}
    QK = ("q0", "k0", "q1", "k1")

    def __init__(self, nc, k, io, g, ffn_raw):
        self.nc, self.k, self.io, self.g, self.ffn_raw = nc, k, io, g, ffn_raw
        self.off, a = {}, 0
        for n in ("q0", "k0", "q1", "k1", "v", "o"):
            self.off[n] = a
            a += self.PIECES[n]
        self.raw = {n: k.sb(f"raw_{n}", [P, m]) for n, m in self.PIECES.items()}
        self.ws = {n: (k.sb(f"w{n}_hi", [P, m], F32R), k.sb(f"w{n}_lo", [P, m], F32R)) for n, m in self.PIECES.items()}
        self.mask = k.sb("mask", [P, P])
        self.s_in = {n: k.sem(f"in_{n}") for n in self.PIECES}
        self.s_whi = {n: k.sem(f"whi_{n}") for n in self.PIECES}
        self.s_wlo = {n: k.sem(f"wlo_{n}") for n in self.PIECES}
        self.s_mask = k.sem("mask")

    def load(self, sp, gr):
        for n, m in self.PIECES.items():
            need(sp, self.s_wlo[n], gr)
            a = self.off[n]
            sp.dma_start(self.raw[n][:, :], self.io["w_attn1"][bass.ds(gr, 1), :, a:a + m]
                         .rearrange("a p n -> (a p) n")).then_inc(self.s_in[n], 16)

    def split(self, pool, n, gr, used=()):
        pool.wait_ge(self.s_in[n], 16 * gr + 16)
        for sem, value in used:
            pool.wait_ge(sem, value)
        plain(pool, self.g["tick"])
        hi, lo = self.ws[n]
        pool.tensor_copy(hi[:, :], self.raw[n][:, :]).then_inc(self.s_whi[n], 1)
        pool.wait_ge(self.s_whi[n], gr + 1)
        pool.tensor_tensor(lo[:, :], self.raw[n][:, :], f32(hi[:, :]), ALU.subtract).then_inc(self.s_wlo[n], 1)

    def first_loads(self, sp):
        self.load(sp, 0)
        ffn1_first_loads(sp, self.io, self.ffn_raw)

    def first_splits(self, pool):
        pool.memset(self.mask[:, :], 0.0).then_inc(self.s_mask, 1)
        pool.wait_ge(self.s_mask, 1)
        pool.affine_select(out=self.mask[:, :], in_=self.mask[:, :], compare_op=ALU.is_ge, fill=-1e30, base=0,
                           pattern=[[-1, P]], channel_multiplier=1).then_inc(self.s_mask, 1)
        for n in ("q0", "k0", "v", "q1", "k1"):
            self.split(pool, n, 0)

    def run(self):
        nc, k, g = self.nc, self.k, self.g
        raw, ws, mask, QK = self.raw, self.ws, self.mask, self.QK
        s_wlo, s_mask = self.s_wlo, self.s_mask
        res, ident = g["res"], g["ident"]
        xhi, xlo = g["xT"]
        NSTEP = 8 * NG
        qk = [(k.sb(f"qk{i}_hi", [P, 4, HALF], F32R), k.sb(f"qk{i}_lo", [P, 4, HALF], F32R)) for i in range(2)]
        v = [(k.sb(f"v{i}_hi", [P, 4, 2 * DV], F32R), k.sb(f"v{i}_lo", [P, 4, 2 * DV], F32R)) for i in range(2)]
        oT = [(k.sb(f"oT{i}_hi", [P, 2, HALF], F32R), k.sb(f"oT{i}_lo", [P, 2, HALF], F32R)) for i in range(2)]
        pr = [k.sb(f"pr{i}", [P, 3 * P]) for i in range(2)]
        pt = (k.sb("pt_hi", [P, 3 * P], F32R), k.sb("pt_lo", [P, 3 * P], F32R))
        nmax = [k.sb(f"nmax{i}", [P, 2]) for i in range(2)]
        rsum = [k.sb(f"rsum{i}", [P, 2]) for i in range(2)]
        rinv = [k.sb(f"rinv{i}", [P, 2]) for i in range(2)]
        bj = [k.ps(f"bj{i}") for i in range(3)]
        bs = [k.ps(f"bs{i}") for i in range(2)]
        bt = k.ps("bt")
        bo = [k.ps(f"bo{i}") for i in range(2)]
        s_jmm = [k.sem(f"jmm{i}") for i in range(3)]
        s_jhi = [k.sem(f"jhi{i}") for i in range(3)]
        s_jlo = [k.sem(f"jlo{i}") for i in range(3)]
        s_smm, s_mk, s_max, s_exp, s_inv, s_norm = (k.sem(x) for x in ("smm", "mk", "max", "exp", "inv", "norm"))
        s_tmm, s_thi, s_tlo, s_pv, s_ohi, s_olo = (k.sem(x) for x in ("tmm", "thi", "tlo", "pv", "ohi", "olo"))

        def work(r, t):
            todo = {}
            if has(r, NSTEP):
                todo[0] = "qk"
                if t < 2:
                    todo[1] = todo[2] = "v"
            if t >= 2 and has(r - 8, NSTEP):
                todo[1] = todo[2] = "o"
            return todo

        def sweep(eng, prologue, step):
            def group(gr):
                for c in range(2):
                    for t in range(4):
                        step(gr, c, t)

            for t in range(4):
                prologue(t)
            group(0)
            with eng.Fori(1, NG - 1) as gr:
                group(gr)
            group(NG - 1)
            for t in range(4):
                step(NG, 0, t)

        with nc.Block() as block:
            @block.sync
            def _(sp):
                with sp.Fori(1, NG) as gr:
                    self.load(sp, gr)

            @block.gpsimd
            def _(pool):
                def group(gr):
                    r = 4 + 8 * gr
                    if has(gr + 1, NG):
                        self.split(pool, "q0", gr + 1, [(s_jmm[0], r + 1)])
                        self.split(pool, "k0", gr + 1, [(s_jmm[0], r + 2)])
                        self.split(pool, "v", gr + 1, [(s_jmm[2], r + 2)])
                        self.split(pool, "q1", gr + 1, [(s_jmm[0], r + 3)])
                        self.split(pool, "k1", gr + 1, [(s_jmm[0], r + 4)])
                    self.split(pool, "o", gr, [(s_jmm[2], r + 4)])

                with pool.Fori(0, NG - 1) as gr:
                    group(gr)
                group(NG - 1)

            @block.scalar
            def _(act):
                act.preload_act_table(ACT.Exp)

                def exps(s, t):
                    act.wait_ge(s_max, s + 1)
                    for i in range(2):
                        cols = slice(i * P, (2 * i + 1) * P)
                        m = act.activation(pr[t % 2][:, cols], bs[t % 2][:, cols], ACT.Exp, bias=nmax[t % 2][:, i:i + 1],
                                           accum_out=rsum[t % 2][:, i:i + 1])
                    m.then_inc(s_exp, 1)

                def probs(s):
                    act.wait_ge(s_tmm, s + 1)
                    act.activation(pt[0][:, :], bt[:, 0:3 * P], ACT.Identity).then_inc(s_thi, 1)

                def outs(s, c, t):
                    act.wait_ge(s_pv, s + 1)
                    b, hd = t // 2, t % 2
                    act.activation(oT[c][0][:, hd, b * S:(b + 1) * S], bo[t % 2][:, 0:S], ACT.Identity)\
                       .then_inc(s_ohi, 1)

                def spill(todo, banks, r, c, t):
                    for bank in banks:
                        if todo.get(bank) == "qk":
                            act.wait_ge(s_jmm[0], r + 1)
                            act.activation(qk[c][0][:, t, :], bj[0][:, :], ACT.Identity,
                                           scale=SCALE1 if t % 2 == 0 else 1.0).then_inc(s_jhi[0], 1)
                        if todo.get(bank) == "v":
                            act.wait_ge(s_jmm[bank], r + 1)
                            act.activation(v[c][0][:, 2 * t + bank - 1, :], bj[bank][:, 0:2 * DV], ACT.Identity)\
                               .then_inc(s_jhi[bank], 1)

                def prologue(t):
                    spill(work(t, t), (0, 1, 2), t, 0, t)
                    if t == 3:
                        exps(0, 0)

                def step(gr, c, t):
                    s = 8 * gr + 4 * c + t
                    if has(s - 1, NSTEP):
                        outs(s - 1, c if t else 1 - c, (t - 1) % 4)
                    if has(s, NSTEP):
                        probs(s)
                    if has(s + 1, NSTEP):
                        exps(s + 1, (t + 1) % 4)
                    spill(work(s + 4, t), (0, 1, 2), s + 4, 1 - c, t)

                sweep(act, prologue, step)

            @block.vector
            def _(dve):
                def softmax_a(s, t):
                    dve.wait_ge(s_smm, s + 1)
                    bank = bs[t % 2]
                    diagonal = bank[:, :].rearrange("p (a n) -> p a n", n=S)[:, :, 0:P]
                    dve.tensor_tensor(diagonal, diagonal, mask[:, :][:, None, :].to_broadcast([P, 2, P]), ALU.add)\
                       .then_inc(s_mk, 1)
                    dve.wait_ge(s_mk, s + 1)
                    dve.tensor_reduce(nmax[t % 2][:, 0:1], bank[:, 0:P], AX, ALU.max, negate=True)
                    dve.tensor_reduce(nmax[t % 2][:, 1:2], bank[:, P:3 * P], AX, ALU.max, negate=True)\
                       .then_inc(s_max, 1)

                def softmax_b(s, t):
                    dve.wait_ge(s_exp, s + 1)
                    dve.reciprocal(rinv[t % 2][:, :], rsum[t % 2][:, :]).then_inc(s_inv, 1)
                    dve.wait_ge(s_inv, s + 1)
                    x = pr[t % 2]
                    dve.tensor_scalar(x[:, 0:P], x[:, 0:P], rinv[t % 2][:, 0:1], None, ALU.mult)
                    dve.tensor_scalar(x[:, P:3 * P], x[:, P:3 * P], rinv[t % 2][:, 1:2], None, ALU.mult)\
                       .then_inc(s_norm, 1)

                def probs(s):
                    dve.wait_ge(s_thi, s + 1)
                    dve.tensor_tensor(pt[1][:, :], bt[:, 0:3 * P], f32(pt[0][:, :]), ALU.subtract).then_inc(s_tlo, 1)

                def outs(s, c, t):
                    dve.wait_ge(s_ohi, s + 1)
                    b, hd = t // 2, t % 2
                    dve.tensor_tensor(oT[c][1][:, hd, b * S:(b + 1) * S], bo[t % 2][:, 0:S],
                                      f32(oT[c][0][:, hd, b * S:(b + 1) * S]), ALU.subtract).then_inc(s_olo, 1)

                def store(todo, banks, r, c, t):
                    for bank in banks:
                        kind = todo.get(bank)
                        if kind == "qk":
                            dve.wait_ge(s_jhi[0], r + 1)
                            hi, lo = (x[:, t, :] for x in qk[c])
                            if t % 2 == 0:
                                m = dve.scalar_tensor_tensor(out=lo, in0=bj[0][:, :], scalar=SCALE1, in1=f32(hi),
                                                             op0=ALU.mult, op1=ALU.subtract)
                            else:
                                m = dve.tensor_tensor(lo, bj[0][:, :], f32(hi), ALU.subtract)
                            m.then_inc(s_jlo[0], 1)
                        elif kind == "v":
                            dve.wait_ge(s_jhi[bank], (r - t) // 2 + t + 1)
                            hi, lo = (x[:, 2 * t + bank - 1, :] for x in v[c])
                            dve.tensor_tensor(lo, bj[bank][:, 0:2 * DV], f32(hi), ALU.subtract).then_inc(s_jlo[bank], 1)
                        elif kind == "o":
                            dve.wait_ge(s_jmm[bank], r + 1)
                            j = 4 * c + 2 * (t - 2) + bank - 1
                            dve.tensor_tensor(res[:, j, :], bj[bank][:, :], res[:, j, :], ALU.add)\
                               .then_inc(s_jlo[bank], 1)
                        else:
                            dve.wait_ge(s_jmm[bank], r + 1)
                            dve.sem_inc(s_jlo[bank], 1)

                def prologue(t):
                    store(work(t, t), (0, 1, 2), t, 0, t)
                    if t == 3:
                        dve.wait_ge(s_mask, 2)
                        softmax_a(0, 0)
                        softmax_b(0, 0)

                def step(gr, c, t):
                    s = 8 * gr + 4 * c + t
                    todo = work(s + 4, t)
                    if has(s + 1, NSTEP):
                        softmax_a(s + 1, (t + 1) % 4)
                    if has(s - 1, NSTEP):
                        outs(s - 1, c if t else 1 - c, (t - 1) % 4)
                    if has(s, NSTEP):
                        probs(s)
                    if has(s + 1, NSTEP):
                        softmax_b(s + 1, (t + 1) % 4)
                    store(todo, (0, 1, 2), s + 4, 1 - c, t)

                sweep(dve, prologue, step)

            @block.tensor
            def _(pe):
                def project(todo, bank, r, gr, c, t):
                    need(pe, s_jlo[bank], r)
                    kind = todo.get(bank)
                    if kind == "qk":
                        n = QK[t]
                        pe.wait_ge(s_wlo[n], gr + 1)
                        tok = slice(c * HALF, (c + 1) * HALF)
                        for kc in range(KC):
                            w = tuple(x[:, kc * P:(kc + 1) * P] for x in ws[n])
                            m = matmul3(pe, bj[0][:, :], w, (xhi[:, kc, tok], xlo[:, kc, tok]), kc == 0, kc == KC - 1)
                    elif kind == "v":
                        pe.wait_ge(s_wlo["v"], gr + 1)
                        a = c * HALF + (2 * t + bank - 1) * P
                        for kc in range(KC):
                            x = (xhi[:, kc, a:a + P], xlo[:, kc, a:a + P])
                            w = tuple(y[:, kc * 2 * DV:(kc + 1) * 2 * DV] for y in ws["v"])
                            m = matmul3(pe, bj[bank][:, 0:2 * DV], x, w, kc == 0, kc == KC - 1)
                    elif kind == "o":
                        pe.wait_ge(s_wlo["o"], gr)
                        a = (2 * (t - 2) + bank - 1) * P
                        for hd in range(2):
                            o = tuple(x[:, hd, a:a + P] for x in oT[c])
                            w = tuple(x[:, hd * HID:(hd + 1) * HID] for x in ws["o"])
                            m = matmul3(pe, bj[bank][:, :], o, w, hd == 0, hd == 1)
                    else:
                        pe.sem_inc(s_jmm[bank], 1)
                        return
                    m.then_inc(s_jmm[bank], 1)

                def scores(s, c, t):
                    b, hd = t // 2, t % 2
                    need(pe, s_exp, s - 1)
                    q = [tuple(x[:, 2 * hd, b * S + i * P:b * S + (i + 1) * P] for x in qk[c]) for i in range(2)]
                    kk = [tuple(x[:, 2 * hd + 1, b * S:b * S + (i + 1) * P] for x in qk[c]) for i in range(2)]
                    matmul3(pe, bs[t % 2][:, 0:P], q[0], kk[0], True, False)
                    matmul3(pe, bs[t % 2][:, P:3 * P], q[1], kk[1], False, True).then_inc(s_smm, 1)

                def turn(s, t):
                    pe.wait_ge(s_norm, s + 1)
                    need(pe, s_tlo, s)
                    for i in range(3):
                        cols = slice(i * P, (i + 1) * P)
                        m = pe.transpose(bt[:, cols], pr[t % 2][:, cols], ident[:, :])
                    m.then_inc(s_tmm, 1)

                def values(s, c, t):
                    b, hd = t // 2, t % 2
                    pe.wait_ge(s_tlo, s + 1)
                    need(pe, s_olo, s - 1)
                    for kt in range(2):
                        vv = tuple(x[:, 2 * b + kt, hd * DV:(hd + 1) * DV] for x in v[c])
                        p = tuple(x[:, 2 * kt * P:(2 + kt) * P] for x in pt)
                        m = matmul3(pe, bo[t % 2][:, kt * P:2 * P], vv, p, kt == 0, kt == 1)
                    m.then_inc(s_pv, 1)

                def prologue(t):
                    for bank in range(3):
                        project(work(t, t), bank, t, 0, 0, t)
                    if t == 3:
                        pe.wait_ge(s_jlo[0], 2)
                        scores(0, 0, 0)

                def step(gr, c, t):
                    s = 8 * gr + 4 * c + t
                    r = s + 4
                    todo = work(r, t)
                    if has(s + 1, NSTEP):
                        if t == 3:
                            pe.wait_ge(s_jlo[0], r - 1)
                        if t == 0:
                            pe.wait_ge(s_jlo[0], r)
                        scores(s + 1, c if t < 3 else 1 - c, (t + 1) % 4)
                    if has(s, NSTEP):
                        turn(s, t)
                    unit = (gr, 1) if c == 0 else (gr + 1, 0)
                    for bank in range(3):
                        if todo.get(bank) == "o":
                            if t == 2 and bank == 1:
                                pe.wait_ge(s_olo, s - 2)
                        project(todo, bank, r, *unit, t)
                    if has(s, NSTEP):
                        if t == 0:
                            pe.wait_ge(s_jlo[1], r)
                            pe.wait_ge(s_jlo[2], r)
                        values(s, c, t)

                sweep(pe, prologue, step)


def ffn1_raw(k):
    return {"w": k.sb("wraw", [P, KC, W1F]), "bm": k.sb("braw", [P, HID]), "b": k.sb("bb", [P, HID]),
            "in": k.sem("in")}


def ffn1_first_loads(sp, io, raw):
    sp.dma_start(raw["w"][:, :, :], io["w_ffn1"].rearrange("(c p) n -> p c n", p=P)).then_inc(raw["in"], 16)
    sp.dma_start(raw["bm"][:, :], io["bm1"]).then_inc(raw["in"], 16)
    sp.dma_start(raw["b"][:, :], io["b1"][None, :].to_broadcast([P, HID])).then_inc(raw["in"], 16)


def ffn1(nc, k, io, g, raw):
    res, ident = g["res"], g["ident"]
    ws = (k.sb("w_hi", [P, KC, W1F], F32R), k.sb("w_lo", [P, KC, W1F], F32R))
    bm = (k.sb("bm_hi", [P, HID], F32R), k.sb("bm_lo", [P, HID], F32R))
    m = moment_memory(k)
    st, mv, rs = k.sb("st2", [P, 6]), k.sb("mv2", [P, 2]), k.sb("rs2", [P, 1])
    x = [k.sb(f"x{i}", [P, HID]) for i in range(2)]
    xb = [k.sb(f"xb{i}", [P, HID]) for i in range(2)]
    xT = [(k.sb(f"xT{i}_hi", [P, HID], F32R), k.sb(f"xT{i}_lo", [P, HID], F32R)) for i in range(2)]
    qs = k.sb("qs", [P, E * DK])
    prod = k.sb("prod", [P, E * DK])
    sc, nm, nms, ex = k.sb("sc", [P, E]), k.sb("nm", [P, 1]), k.sb("nms", [P, 1]), k.sb("ex", [P, E])
    sm, ri = k.sb("sm", [P, 1]), k.sb("ri", [P, 1])
    gate = k.sb("gate", [P, E])
    wh = k.sb("wh", [P, E, R])
    whT = (k.sb("whT_hi", [P, P], F32R), k.sb("whT_lo", [P, P], F32R))
    y = k.sb("y", [P, HID])
    yo = [k.sb(f"yo{i}", [P, HID]) for i in range(2)]
    bx, bqk, bh, br, bw = (k.ps(n) for n in ("bx", "bqk", "bh", "br", "bw"))
    s_in, s_whi, s_wlo = raw["in"], k.sem("whi"), k.sem("wlo")
    s_x, s_xb, s_tx, s_xhi, s_xlo = (k.sem(n) for n in ("x", "xb", "tx", "xhi", "xlo"))
    s_qk, s_h, s_r, s_q, s_gate, s_ex, s_wh, s_tw, s_whT, s_whl = (
        k.sem(n) for n in ("qk", "h", "r", "q", "gate", "ex", "wh", "tw", "whT", "whl"))
    s_end, s_var, s_rs, s_yo = (k.sem(n) for n in ("end", "var", "rs", "yo"))
    s_out = [k.sem(f"out{i}") for i in range(2)]
    inv = float(DK) ** -0.5
    out = io["out"].rearrange("(t p) n -> t p n", p=P)
    NGATE, NEND = 6, 3

    def rounds(eng, round_):
        for t in (0, 1):
            round_(t, t, 0)
        with eng.Fori(1, NT // 2 - 1) as i:
            for u in range(2):
                round_(2 * i + u, u, i)
        for t in (NT - 2, NT - 1, NT):
            round_(t, t % 2, t // 2)

    with nc.Block() as block:
        @block.sync
        def _(sp):
            def store(t, u, i):
                if has(t, NT):
                    sp.wait_ge(s_yo, t + 1)
                    sp.dma_start(out[bass.ds(t, 1), :, :].rearrange("a p n -> (a p) n"), yo[u][:, :])\
                      .then_inc(s_out[u], 16)

            for free in s_out:
                sp.sem_inc(free, 16)
            rounds(sp, store)
            for stored in s_out:
                sp.wait_ge(stored, 16 * (NT // 2 + 1))

        @block.gpsimd
        def _(pool):
            moments(None, pool, g, m, 2)
            pool.wait_ge(s_in, 48)

            def with_bias(t, u):
                pool.wait_ge(s_x, t + 1)
                need(pool, s_end, NEND * (t - 1))
                pool.tensor_tensor(xb[u][:, :], x[u][:, :], raw["b"][:, :], ALU.add).then_inc(s_xb, 1)

            def round_(t, u, i):
                if has(t + 1, NT):
                    with_bias(t + 1, 1 - u)
                if has(t - 1, NT):
                    pool.wait_ge(s_var, t)
                    pool.tensor_tensor(rs[:, :], mv[:, 1:2], m["mh"][:, 0:1], ALU.pow).then_inc(s_rs, 1)

            with_bias(0, 0)
            rounds(pool, round_)

        @block.scalar
        def _(act):
            act.preload_act_table(ACT.Exp)
            act.wait_ge(s_in, 48)
            for c in range(KC):
                act.activation(ws[0][:, c, :], raw["w"][:, c, :], ACT.Identity).then_inc(s_whi, 1)
            act.activation(bm[0][:, :], raw["bm"][:, :], ACT.Identity).then_inc(s_whi, 1)

            def xhi(t, u):
                act.wait_ge(s_tx, t + 1)
                act.activation(xT[u][0][:, :], bx[:, :], ACT.Identity).then_inc(s_xhi, 1)

            def round_(t, u, i):
                if has(t, NT):
                    act.wait_ge(s_qk, t + 1)
                    act.activation(qs[:, :], bqk[:, 0:E * DK], ACT.Identity).then_inc(s_q, 1)
                    act.wait_ge(s_gate, NGATE * t + 4)
                    act.activation(ex[:, :], sc[:, :], ACT.Exp, bias=nms[:, :], scale=inv, accum_out=sm[:, :])\
                       .then_inc(s_ex, 1)
                if has(t + 1, NT):
                    xhi(t + 1, 1 - u)
                if has(t, NT):
                    act.wait_ge(s_tw, t + 1)
                    act.activation(whT[0][:, :], bw[:, 0:P], ACT.Identity).then_inc(s_whT, 1)

            xhi(0, 0)
            rounds(act, round_)

        @block.vector
        def _(dve):
            def begin(t, u):
                need(dve, s_tx, t - 1)
                need(dve, s_xb, t - 1)
                row = res[:, bass.ds(t, 1), :].rearrange("p a n -> p (a n)")
                mean = m["mv"][:, bass.ds(t, 1), 0]
                dve.tensor_scalar(x[u][:, :], row, mean, m["rs"][:, bass.ds(t, 1)], ALU.subtract, ALU.mult)\
                   .then_inc(s_x, 1)

            def xlo(t, u):
                dve.wait_ge(s_xhi, t + 1)
                dve.tensor_tensor(xT[u][1][:, :], bx[:, :], f32(xT[u][0][:, :]), ALU.subtract).then_inc(s_xlo, 1)

            def chained(sem, count):
                def link(ins):
                    count[0] = count[0] + 1
                    ins.then_inc(sem, 1)
                    dve.wait_ge(sem, count[0])
                    plain(dve, g["tick"])
                return link

            def end_a(t, u):
                dve.wait_ge(s_r, t + 1)
                dve.wait_ge(s_xb, t + 1)
                link = chained(s_end, [NEND * t])
                link(dve.tensor_tensor(y[:, :], br[:, :], xb[u][:, :], ALU.add))
                link(dve.bn_stats(st[:, :], y[:, :]))
                link(dve.bn_aggr(mv[:, :], st[:, :]))
                dve.tensor_scalar(mv[:, 1:2], mv[:, 1:2], EPS, None, ALU.add).then_inc(s_var, 1)

            def end_b(t, u, before):
                dve.wait_ge(s_rs, t + 1)
                dve.wait_ge(s_out[u], 16 * before)
                dve.tensor_scalar(yo[u][:, :], y[:, :], mv[:, 0:1], rs[:, 0:1], ALU.subtract, ALU.mult)\
                   .then_inc(s_yo, 1)

            def gates(t):
                dve.wait_ge(s_q, t + 1)
                link = chained(s_gate, [NGATE * t])
                link(dve.tensor_tensor(prod[:, :], bqk[:, E * DK:2 * E * DK], qs[:, :], ALU.mult))
                link(dve.tensor_reduce(sc[:, :], prod[:, :].rearrange("p (e d) -> p e d", e=E), AX, ALU.add))
                link(dve.tensor_reduce(nm[:, :], sc[:, :], AX, ALU.max, negate=True))
                link(dve.tensor_scalar(nms[:, :], nm[:, :], inv, None, ALU.mult))
                dve.wait_ge(s_ex, t + 1)
                link(dve.reciprocal(ri[:, :], sm[:, :]))
                link(dve.tensor_scalar(gate[:, :], ex[:, :], ri[:, 0:1], None, ALU.mult))
                dve.wait_ge(s_h, t + 1)
                dve.tensor_tensor(wh[:, :, :], bh[:, 0:P].rearrange("p (e r) -> p e r", e=E),
                                  gate[:, :][:, :, None].to_broadcast([P, E, R]), ALU.mult).then_inc(s_wh, 1)

            def round_(t, u, i):
                if has(t - 1, NT):
                    end_a(t - 1, 1 - u)
                if has(t + 1, NT):
                    begin(t + 1, 1 - u)
                if has(t - 1, NT):
                    end_b(t - 1, 1 - u, i + u)
                if has(t, NT):
                    gates(t)
                if has(t + 1, NT):
                    xlo(t + 1, 1 - u)
                if has(t, NT):
                    dve.wait_ge(s_whT, t + 1)
                    dve.tensor_tensor(whT[1][:, :], bw[:, 0:P], f32(whT[0][:, :]), ALU.subtract).then_inc(s_whl, 1)

            moments(dve, None, g, m, 2)
            dve.wait_ge(g["ln"]["rs"], 6)
            begin(0, 0)
            for c in range(KC):
                dve.wait_ge(s_whi, c + 1)
                dve.tensor_tensor(ws[1][:, c, :], raw["w"][:, c, :], f32(ws[0][:, c, :]), ALU.subtract)\
                   .then_inc(s_wlo, 1)
            dve.wait_ge(s_whi, KC + 1)
            dve.tensor_tensor(bm[1][:, :], raw["bm"][:, :], f32(bm[0][:, :]), ALU.subtract).then_inc(s_wlo, 1)
            xlo(0, 0)
            rounds(dve, round_)

        @block.tensor
        def _(pe):
            def wide(bank, u, a, n, stop):
                for c in range(KC):
                    i = matmul3(pe, bank[:, 0:n], tuple(z[:, c * P:(c + 1) * P] for z in xT[u]),
                                tuple(z[:, c, a:a + n] for z in ws), c == 0, stop and c == KC - 1)
                return i

            def turn(t, u):
                pe.wait_ge(s_x, t + 1)
                need(pe, s_xlo, t)
                for c in range(KC):
                    i = pe.transpose(bx[:, c * P:(c + 1) * P], x[u][:, c * P:(c + 1) * P], ident[:, :])
                i.then_inc(s_tx, 1)

            def round_(t, u, i):
                if not has(t, NT):
                    return
                pe.wait_ge(s_xlo, t + 1)
                wide(bqk, u, HID, 2 * E * DK, True).then_inc(s_qk, 1)
                wide(bh, u, HID + 2 * E * DK, E * R, True).then_inc(s_h, 1)
                need(pe, s_end, NEND * (t - 1) + 1)
                wide(br, u, 0, HID, False)
                if has(t + 1, NT):
                    turn(t + 1, 1 - u)
                pe.wait_ge(s_wh, t + 1)
                pe.transpose(bw[:, 0:P], wh[:, :, :].rearrange("p e r -> p (e r)"), ident[:, :]).then_inc(s_tw, 1)
                pe.wait_ge(s_whl, t + 1)
                matmul3(pe, br[:, :], (whT[0][:, :], whT[1][:, :]), (bm[0][:, :], bm[1][:, :]), False, True)\
                    .then_inc(s_r, 1)

            turn(0, 0)
            pe.wait_ge(s_wlo, KC + 1)
            rounds(pe, round_)


def _lay_out(i):
    c = np.ascontiguousarray
    f = np.float32
    a = {n: np.asarray(x) for n, x in i.items()}
    x = a["L0_attn_hidden_size"].reshape(T, HID)
    wqc, wkc = a["L0_attn_Wq_c"], a["L0_attn_Wkv_c"]
    bqc, bkc = a["L0_attn_bq_c"], a["L0_attn_bkv_c"]
    o = {"x": x, "xT": x.T}
    o["w_down0"] = np.concatenate([wqc.T, wqc[P:].T, wkc.T], 1)
    o["b_down0"] = np.stack([bqc[:P], np.concatenate([bqc[P:], bqc[P:]]), bkc], 1)
    wq = a["L0_attn_Wq_up"].reshape(NH, NOPE + ROPE, QL)
    bq = a["L0_attn_bq_up"].reshape(NH, NOPE + ROPE)
    wkv = a["L0_attn_Wkv_up"].reshape(NH, NOPE + VH, KVL)
    bkv = a["L0_attn_bkv_up"].reshape(NH, NOPE + VH)
    nope, rope = wq[:, :NOPE], wq[:, NOPE:].transpose(0, 2, 1)
    bias = np.zeros((NH, P, 2), f)
    bias[:, :, 0] = bq[:, :NOPE]
    bias[:, KVL:, 1] = bq[:, NOPE:]
    o["w_head0"] = np.concatenate([nope, nope[:, :, P:], wkv[:, :NOPE], rope[:, :P], np.concatenate(
        [rope[:, P:], rope[:, P:]], 1), bias], 2)
    wv = wkv[:, NOPE:].transpose(0, 2, 1)
    o["wv_head0"] = np.concatenate([wv, wv], 1)
    o["bv0"] = bkv[:, NOPE:].T
    o["wo0"] = a["L0_attn_Wo"].T
    o["bo0"] = a["L0_attn_bo"]

    gw, uw, dw = (a[f"L0_ffn_{n}_wq"] for n in ("gate", "up", "down"))
    blocks = np.zeros((NI, P, 3 * HID), gw.dtype)
    pad = np.zeros((NI * P, HID), gw.dtype)
    for j, w in enumerate((gw, uw)):
        pad[:INTER] = w
        blocks[:, :, j * HID:(j + 1) * HID] = pad.reshape(NI, P, KC, P).transpose(0, 3, 2, 1).reshape(NI, P, HID)
    pad[:INTER] = dw.T
    blocks[:, :, 2 * HID:] = pad.reshape(NI, P, HID)
    o["w_ffn0"] = blocks
    for n in ("gate", "up"):
        s = np.zeros(NI * P, f)
        s[:INTER] = a[f"L0_ffn_{n}_scale"]
        o[f"{n}_scale"] = s.reshape(NI, P).T
    o["down_scale"] = a["L0_ffn_down_scale"]

    wq1 = a["L1_attn_wq"].reshape(KC, P, NG, 2, DN + DR)[..., :DN]
    wkv1 = a["L1_attn_wkv"]
    wk1 = wkv1[:, :NH * DN].reshape(KC, P, NG, 2, DN)
    wv1 = wkv1[:, NH * DN:NH * (DN + DV)].reshape(KC, P, NG, 2 * DV)
    wo1 = a["L1_attn_wo"].reshape(NG, 2, P, HID)
    piece = lambda w: w.transpose(2, 1, 0, 3).reshape(NG, P, -1)
    o["w_attn1"] = np.concatenate([piece(wq1[:, :, :, 0]), piece(wk1[:, :, :, 0]), piece(wq1[:, :, :, 1]),
                                   piece(wk1[:, :, :, 1]), piece(wv1),
                                   wo1.transpose(0, 2, 1, 3).reshape(NG, P, -1)], 2)
    o["w_ffn1"] = np.concatenate([a["L1_ffn_W"].T, a["L1_ffn_Wq"].T, a["L1_ffn_Wk"].T,
                                  a["L1_ffn_A"].reshape(E * R, HID).T], 1)
    o["bm1"] = a["L1_ffn_Bm"].transpose(0, 2, 1).reshape(E * R, HID)
    o["b1"] = a["L1_ffn_b"]
    return {n: c(x) for n, x in o.items()}


def kernel(**inputs):
    import concourse.bacc as _bacc
    from concourse.bass_utils import run_bass_kernel_spmd as _run

    nc = _bacc.Bacc("TRN2", target_bir_lowering=False, num_devices=1)
    arrays = {f"in_{n}": x for n, x in _lay_out(inputs).items()}
    io = {n[3:]: nc.dram_tensor(n, x.shape, mybir.dt.from_np(x.dtype), kind="ExternalInput").ap()
          for n, x in arrays.items()}
    io["out"] = nc.dram_tensor("out", (T, HID), F32, kind="ExternalOutput").ap()
    build(nc, io)
    r = _run(nc, [arrays], core_ids=[0])
    return r.results[0]["out"].reshape(NB, S, HID)
```

```python
from contextlib import ExitStack

import numpy as np

import concourse.bass as bass
from concourse import mybir

F32 = mybir.dt.float32
F32R = mybir.dt.float32r
I32 = mybir.dt.int32
ALU = mybir.AluOpType
ACT = mybir.ActivationFunctionType
AX = mybir.AxisListType.X

P = 128
NB, S, HID = 4, 256, 512
T = NB * S
NT = T // P
KC = HID // P
HALF = 512
EPS = 1e-5

NH = 32
QL, KVL, NOPE, ROPE, VH = 192, 64, 128, 64, 128
SCALE0 = float(NOPE + ROPE) ** -0.5
W0 = 2 * P + KVL + 2 * ROPE + 2

INTER = 1376
EXACT = 256
NI = -(-INTER // P)

DN, DR, DV = 128, 64, 128
SCALE1 = float(DN + DR) ** -0.5
NG = NH // 2

E, DK, R = 8, 32, 16
W1H = E * DK + E * R // 2
W1F = HID + 2 * W1H


def f32(ap):
    return ap.bitcast(F32)


def need(eng, sem, value):
    if isinstance(value, int) and value <= 0:
        return
    eng.wait_ge(sem, value)


def loop(eng, n, body):
    body(0)
    with eng.Fori(1, n) as i:
        body(i)


def plain(eng, sem):
    eng.sem_inc(sem, 1)


def has(x, n):
    return not isinstance(x, int) or 0 <= x < n


def matmul3(pe, out, w, x, start, stop):
    pe.matmul(out, w[0], x[0], start=start, stop=False, skip_group_check=True)
    pe.matmul(out, w[0], x[1], start=False, stop=False, skip_group_check=True)
    return pe.matmul(out, w[1], x[0], start=False, stop=stop, skip_group_check=True)


class Kit:

    def __init__(self, nc, ctx, tag):
        self.nc, self.ctx, self.tag = nc, ctx, tag

    def sb(self, name, shape, dt=F32):
        return self.ctx.enter_context(self.nc.sbuf_tensor(f"{self.tag}_{name}", shape, dt))

    def ps(self, name):
        return self.ctx.enter_context(self.nc.psum_tensor(f"{self.tag}_{name}", [P, 512], F32))

    def sem(self, name):
        return self.ctx.enter_context(self.nc.semaphore(f"{self.tag}_{name}"))


def build(nc, io):
    with ExitStack() as ctx:
        k = Kit(nc, ctx, "g")
        g = {
            "res": k.sb("res", [P, NT, HID]),
            "xT": (k.sb("xT_hi", [P, KC, T], F32R), k.sb("xT_lo", [P, KC, T], F32R)),
            "ident": k.sb("ident", [P, P]),
            "y": k.sb("y", [P, 4, HID]),
            "wo": k.sb("wo", [P, HID]),
            "bvs": k.sb("bvs", [P, 1]),
            "mag": k.sb("mag", [P, NH]),
            "mag1": k.sb("mag1", [P, 1]),
            "largest": k.sb("largest", [1, 1], I32),
            "tick": k.sem("tick"),
            "ln": {n: k.sem(n) for n in ("st", "mv", "add", "rs", "xn", "t", "hi", "lo")},
            "m": {"st": k.sb("st", [P, NT, 6]), "mv": k.sb("mv", [P, NT, 2]), "rs": k.sb("rs", [P, NT]),
                  "mh": k.sb("mh", [P, 4])},
        }
        sems = ctx.enter_context(ExitStack())

        def kit(tag, memory):
            new = Kit(nc, memory, tag)
            new.sem = Kit(nc, sems, tag).sem
            return new

        norm0, norm1, norm2 = (Norm(g, n) for n in range(3))
        accs = ctx.enter_context(ExitStack())
        acc = [kit("a", accs).ps(f"acc{c}") for c in range(2)]
        with ExitStack() as m:
            a = kit("a", m)
            first = head_weights(a)
            latent = attention0_prepare(nc, a, io, g, acc, first)
            attention0_heads(nc, a, io, g, latent, acc, first)
        with ExitStack() as later:
            raw = ffn1_raw(kit("e", later))
            attn1 = Attention1(nc, kit("b", later), io, g, raw)
            with ExitStack() as m:
                ffn0 = FFN0(nc, kit("f", m), io, g)
                with ExitStack() as m2:
                    attention0_out(nc, kit("o", m2), g, acc, norm0, ffn0)
                accs.close()
                ffn0.run(norm0, norm1, attn1)
            with ExitStack() as m:
                attn1.run(kit("c", m), norm1, norm2, ffn0.s_res)
            with ExitStack() as m:
                ffn1(nc, kit("e", m), io, g, raw, norm2)


def head_weights(k):
    return {"w": k.sb("w", [P, W0]), "wv": k.sb("wv", [P, VH]), "w_in": k.sem("w0_in"), "wv_in": k.sem("wv_in")}


def fetch_head(sp, io, first, h):
    sp.dma_start(first["w"][:, :], io["w_head0"][bass.ds(h, 1), :, :].rearrange("a p n -> (a p) n"))\
      .then_inc(first["w_in"], 16)


def attention0_prepare(nc, k, io, g, accs, first):
    res, ident = g["res"], g["ident"]
    xhi, xlo = g["xT"]
    qa = (k.sb("qa_hi", [P, T], F32R), k.sb("qa_lo", [P, T], F32R))
    qb = k.sb("qb", [P, T], F32R)
    kv = (k.sb("kv_hi", [P, T], F32R), k.sb("kv_lo", [P, T], F32R))
    cs = k.sb("cs", [P, NT, P], F32R)
    with ExitStack() as ctx:
        t = Kit(nc, ctx, "p")
        xraw = t.sb("xraw", [P, KC, T])
        wraw = t.sb("wraw", [P, KC, 3 * P])
        whi = t.sb("whi", [P, KC, 3 * P], F32R)
        wlo = t.sb("wlo", [P, KC, 3 * P], F32R)
        kvraw = t.sb("kvraw", [P, T])
        bias = t.sb("bias", [P, 3])
        zero = t.sb("zero", [P, P])
        bv = t.sb("bv", [P, NH])
        bo = t.sb("bo", [P, HID])
        banks = [t.ps(f"b{i}") for i in range(4)]
        s_x = k.sem("x_in")
        s_xk = [k.sem(f"xk{i}") for i in range(4)]
        s_wk = [k.sem(f"wk{i}") for i in range(2)]
        s_res, s_bv, s_bo, s_pre = k.sem("res_in"), k.sem("bv_in"), k.sem("bo_in"), k.sem("pre")
        s_id, s_whi, s_wlo = k.sem("ident"), k.sem("whi"), k.sem("wlo")
        s_xhi, s_xlo = k.sem("xhi"), k.sem("xlo")
        s_mm, s_hi, s_lo = k.sem("p_mm"), k.sem("p_hi"), k.sem("p_lo")
        s_raw, s_tr, s_chi, s_clo = k.sem("p_raw"), k.sem("p_tr"), k.sem("p_chi"), k.sem("p_clo")
        chunks = [(m, n) for n in range(2) for m in (2, 0, 1)]
        pieces = [(n, c) for n in range(2) for c in range(KC)]
        with nc.Block() as block:
            @block.sync
            def _(sp):
                for n, c in pieces:
                    if n == 0 and c % 2 == 0:
                        sp.dma_start(wraw[:, c:c + 2, :], io["w_down0"][c * P:(c + 2) * P, :]
                                     .rearrange("(c p) n -> p c n", p=P)).then_inc(s_wk[c // 2], 16)
                    tok = slice(n * HALF, (n + 1) * HALF)
                    if c % 2 == 0:
                        sp.dma_start(xraw[:, c:c + 2, tok], io["xT"][c * P:(c + 2) * P, tok]
                                     .rearrange("(c p) n -> p c n", p=P)).then_inc(s_xk[2 * n + c // 2], 16)
                sp.dma_start(bias[:, :], io["b_down0"]).then_inc(s_x, 16)
                fetch_head(sp, io, first, 0)
                sp.dma_start(bo[:, :], io["bo0"][None, :].to_broadcast([P, HID])).then_inc(s_bo, 16)
                sp.dma_start(res[:, :, :], io["x"].rearrange("(t p) n -> p t n", p=P)).then_inc(s_res, 16)
                sp.dma_start(bv[:, :], io["bv0"]).then_inc(s_bv, 16)
                sp.dma_start(g["wo"][:, :], io["wo0"]).then_inc(s_bv, 16)

            @block.gpsimd
            def _(pool):
                pool.memset(ident[:, :], 0.0).then_inc(s_id, 1)
                pool.memset(zero[:, :], 0.0).then_inc(s_id, 1)
                pool.wait_ge(s_id, 2)
                pool.affine_select(out=ident[:, :], in_=ident[:, :], compare_op=ALU.not_equal, fill=1.0, base=0,
                                   pattern=[[-1, P]], channel_multiplier=1).then_inc(s_id, 1)
                pool.memset(g["m"]["mh"][:, :], -0.5).then_inc(s_pre, 1)
                pool.wait_ge(s_bo, 16)
                pool.wait_ge(s_res, 16)
                for j in range(NT):
                    pool.tensor_tensor(res[:, j, :], res[:, j, :], bo[:, :], ALU.add).then_inc(s_pre, 1)

            @block.scalar
            def _(act):
                def x_hi(n):
                    tok = slice(n * HALF, (n + 1) * HALF)
                    for c in range(KC):
                        if n == 0 and c % 2 == 0:
                            act.wait_ge(s_wk[c // 2], 16)
                            act.activation(whi[:, c:c + 2, :], wraw[:, c:c + 2, :], ACT.Identity).then_inc(s_whi, 1)
                        act.wait_ge(s_xk[2 * n + c // 2], 16)
                        act.activation(xhi[:, c, tok], xraw[:, c, tok], ACT.Identity).then_inc(s_xhi, 1)

                x_hi(0)
                x_hi(1)
                act.wait_ge(s_x, 16)
                for i, (m, n) in enumerate(chunks):
                    tok = slice(n * HALF, (n + 1) * HALF)
                    act.wait_ge(s_mm, i + 1)
                    if m == 2:
                        act.activation(kvraw[:, tok], banks[i % 2][:, :], ACT.Identity,
                                       bias=bias[:, m:m + 1]).then_inc(s_raw, 1)
                        act.wait_ge(s_raw, n + 1)
                        act.activation(kv[0][:, tok], kvraw[:, tok], ACT.Identity).then_inc(s_hi, 1)
                    else:
                        out = qa[0] if m == 0 else qb
                        act.activation(out[:, tok], banks[i % 2][:, :], ACT.Identity,
                                       bias=bias[:, m:m + 1]).then_inc(s_hi, 1)
                for n in range(2):
                    act.wait_ge(s_tr, n + 1)
                    src = banks[2 + n][:, :].rearrange("p (t l) -> p t l", l=P)
                    act.activation(cs[:, 4 * n:4 * n + 4, 0:KVL], src[:, :, 0:KVL], ACT.Identity).then_inc(s_chi, 1)

            @block.vector
            def _(dve):
                for i, (n, c) in enumerate(pieces):
                    if n == 0 and c % 2 == 0:
                        dve.wait_ge(s_whi, c // 2 + 1)
                        dve.tensor_tensor(wlo[:, c:c + 2, :], wraw[:, c:c + 2, :], f32(whi[:, c:c + 2, :]),
                                          ALU.subtract).then_inc(s_wlo, 1)
                    tok = slice(n * HALF, (n + 1) * HALF)
                    dve.wait_ge(s_xhi, i + 1)
                    dve.tensor_tensor(xlo[:, c, tok], xraw[:, c, tok], f32(xhi[:, c, tok]), ALU.subtract)\
                       .then_inc(s_xlo, 1)
                dve.wait_ge(s_x, 16)
                for i, (m, n) in enumerate(chunks):
                    tok = slice(n * HALF, (n + 1) * HALF)
                    dve.wait_ge(s_hi, i + 1)
                    if m == 2:
                        dve.tensor_tensor(kv[1][:, tok], kvraw[:, tok], f32(kv[0][:, tok]),
                                          ALU.subtract).then_inc(s_lo, 1)
                    else:
                        r = slice(0, P) if m == 0 else slice(QL - P, P)
                        hi, lo = (qa[0], qa[1]) if m == 0 else (qb, qb)
                        dve.scalar_tensor_tensor(out=lo[r, tok], in0=banks[i % 2][r, :], scalar=bias[r, m:m + 1],
                                                 in1=f32(hi[r, tok]), op0=ALU.add, op1=ALU.subtract).then_inc(s_lo, 1)
                for n in range(2):
                    dve.wait_ge(s_chi, n + 1)
                    src = banks[2 + n][:, :].rearrange("p (t l) -> p t l", l=P)
                    dve.tensor_tensor(cs[:, 4 * n:4 * n + 4, KVL:P], src[:, :, 0:KVL],
                                      f32(cs[:, 4 * n:4 * n + 4, 0:KVL]), ALU.subtract).then_inc(s_clo, 1)
                dve.wait_ge(s_bv, 32)
                dve.tensor_reduce(g["bvs"][:, :], bv[:, :], AX, ALU.add).then_inc(s_clo, 1)

            @block.tensor
            def _(pe):
                for i, (m, n) in enumerate(chunks):
                    need(pe, s_lo, i - 1)
                    tok = slice(n * HALF, (n + 1) * HALF)
                    for c in range(KC):
                        if m == 2:
                            pe.wait_ge(s_wlo, c // 2 + 1)
                            pe.wait_ge(s_xlo, KC * n + c + 1)
                        w = (whi[:, c, m * P:(m + 1) * P], wlo[:, c, m * P:(m + 1) * P])
                        mm = matmul3(pe, banks[i % 2][:, :], w, (xhi[:, c, tok], xlo[:, c, tok]), c == 0, c == KC - 1)
                    mm.then_inc(s_mm, 1)
                pe.wait_ge(s_id, 3)
                pe.wait_ge(s_raw, 2)
                for n in range(2):
                    for j in range(4):
                        a = (4 * n + j) * P
                        mm = pe.transpose(banks[2 + n][:, j * P:(j + 1) * P], kvraw[:, a:a + P], ident[:, :])
                    mm.then_inc(s_tr, 1)
                for acc in accs:
                    for j in range(4):
                        pe.matmul(acc[:, j * P:(j + 1) * P], zero[:, :], zero[:, :], start=(j == 0), stop=False,
                                  skip_group_check=True)
    return dict(qa=qa, qb=qb, kv=kv, cs=cs)


def attention0_heads(nc, k, io, g, lat, acc, first):
    qa, qb, kv, cs = lat["qa"], lat["qb"], lat["kv"], lat["cs"]
    ident = g["ident"]
    NS, NPAIR = NB * NH, 2 * NH
    with ExitStack() as ctx:
        t = Kit(nc, ctx, "h")
        w, wv = first["w"], first["wv"]
        wk = w[:, 2 * P:2 * P + KVL]
        rope = w[:, 2 * P + KVL:2 * P + KVL + 2 * ROPE].rearrange("p (a n) -> p a n", a=2)
        bcols = w[:, W0 - 2:W0]
        part = t.sb("part", [P, NI * 3 * HID // NH], I32)
        parts = io["w_ffn0"].rearrange("i p n -> (i p n)").rearrange("(h q m) -> h q m", h=NH, q=P)
        s_part, s_mag = k.sem("part_in"), k.sem("mag")
        wvs = (t.sb("wv_hi", [P, VH], F32R), t.sb("wv_lo", [P, VH], F32R))
        gm = t.sb("gm", [P, 2, P])
        gms = (t.sb("gm_hi", [P, 2, P], F32R), t.sb("gm_lo", [P, 2, P], F32R))
        gb = t.sb("gb", [P, 1])
        q = [(t.sb(f"q{i}_hi", [P, HALF], F32R), t.sb(f"q{i}_lo", [P, HALF], F32R)) for i in range(2)]
        o = [(t.sb(f"o{i}_hi", [P, HALF], F32R), t.sb(f"o{i}_lo", [P, HALF], F32R)) for i in range(2)]
        pr = [t.sb(f"pr{i}", [P, 2, S]) for i in range(NB)]
        pt = [(t.sb(f"pt{i}_hi", [P, 2, S], F32R), t.sb(f"pt{i}_lo", [P, 2, S], F32R)) for i in range(NB)]
        nmax = [t.sb(f"nmax{i}", [P, 2]) for i in range(NB)]
        rsum = [t.sb(f"rsum{i}", [P, 2]) for i in range(NB)]
        rinv = [t.sb(f"rinv{i}", [P, 2]) for i in range(NB)]
        bq = t.ps("bq")
        bs = [t.ps(f"bs{i}") for i in range(2)]
        bt = [t.ps(f"bt{i}") for i in range(2)]
        bo = t.ps("bo")
        s_w, s_wv, s_tick = first["w_in"], first["wv_in"], g["tick"]
        s_gmm, s_graw, s_gpool, s_ghi, s_glo = (k.sem(x) for x in ("g_mm", "g_raw", "g_pool", "g_hi", "g_lo"))
        s_qmm, s_qhi, s_qlo = k.sem("q_mm"), k.sem("q_hi"), k.sem("q_lo")
        s_smm, s_max, s_exp, s_inv, s_norm = (k.sem(x) for x in ("s_mm", "s_max", "s_exp", "s_inv", "s_norm"))
        s_tmm, s_thi, s_tlo = k.sem("t_mm"), k.sem("t_hi"), k.sem("t_lo")
        s_pv, s_ohi, s_olo = k.sem("pv"), k.sem("o_hi"), k.sem("o_lo")
        s_wvh, s_wvl, s_om = k.sem("wv_hi"), k.sem("wv_lo"), k.sem("om")

        def run(eng, round_):
            def head(h):
                for b in range(NB):
                    round_(h, b)

            head(0)
            head(1)
            with eng.Fori(2, NH - 1) as h:
                head(h)
            head(NH - 1)
            head(NH)
            round_(NH + 1, 0)

        with nc.Block() as block:
            @block.sync
            def _(sp):
                def fetch(h):
                    need(sp, s_graw, h)
                    need(sp, s_gpool, h)
                    fetch_head(sp, io, first, h)

                def fetch_wv(h):
                    need(sp, s_wvl, h)
                    sp.dma_start(wv[:, :], io["wv_head0"][bass.ds(h, 1), :, :].rearrange("a p n -> (a p) n"))\
                      .then_inc(s_wv, 16)

                def fetch_part(h):
                    need(sp, s_mag, h)
                    sp.dma_start(part[:, :], parts[bass.ds(h, 1), :, :].rearrange("a p n -> (a p) n"))\
                      .then_inc(s_part, 16)

                def both(h):
                    fetch(h + 1)
                    fetch_wv(h)
                    fetch_part(h)

                loop(sp, NH - 1, both)
                fetch_wv(NH - 1)
                fetch_part(NH - 1)

            @block.gpsimd
            def _(pool):
                def rope_part(h):
                    pool.wait_ge(s_w, 16 * h + 16)
                    need(pool, s_glo, h)
                    need(pool, s_qlo, 2 * h)
                    plain(pool, s_tick)
                    pool.tensor_scalar(gm[:, :, KVL:P], rope, SCALE0, None, ALU.mult)
                    pool.tensor_scalar(gb[:, :], bcols[:, 1:2], SCALE0, None, ALU.mult).then_inc(s_gpool, 1)

                def split_wv(h):
                    pool.wait_ge(s_wv, 16 * h + 16)
                    need(pool, s_om, 2 * h)
                    plain(pool, s_tick)
                    pool.tensor_copy(wvs[0][:, :], wv[:, :]).then_inc(s_wvh, 1)
                    pool.wait_ge(s_wvh, h + 1)
                    pool.tensor_tensor(wvs[1][:, :], wv[:, :], f32(wvs[0][:, :]), ALU.subtract).then_inc(s_wvl, 1)

                def norm(s, b):
                    pool.wait_ge(s_inv, s + 1)
                    pool.tensor_tensor(pr[b][:, :, :], pr[b][:, :, :],
                                       rinv[b][:, :][:, :, None].to_broadcast([P, 2, S]), ALU.mult)\
                        .then_inc(s_norm, 1)

                def round_(h, b):
                    s = 4 * h + b
                    if has(s - 1, NS):
                        norm(s - 1, (b - 1) % 4)
                    if b == 0 and has(h + 1, NH):
                        rope_part(h + 1)
                    if b == 1 and has(h - 1, NH):
                        split_wv(h - 1)

                rope_part(0)
                run(pool, round_)

            @block.scalar
            def _(act):
                def merged(h):
                    act.wait_ge(s_graw, h + 1)
                    act.wait_ge(s_gpool, h + 1)
                    act.activation(gms[0][:, :, :], gm[:, :, :], ACT.Identity).then_inc(s_ghi, 1)

                def query(p, par):
                    act.wait_ge(s_qmm, p + 1)
                    act.activation(q[par][0][:, :], bq[:, :], ACT.Identity, bias=gb[:, :]).then_inc(s_qhi, 1)

                def exps(s, b):
                    act.wait_ge(s_max, s + 1)
                    for i in range(2):
                        m = act.activation(pr[b][:, i, :], bs[b % 2][:, i * S:(i + 1) * S], ACT.Exp,
                                           bias=nmax[b][:, i:i + 1], accum_out=rsum[b][:, i:i + 1])
                    m.then_inc(s_exp, 1)

                def probs(s, b):
                    act.wait_ge(s_tmm, s + 1)
                    act.activation(pt[b][0][:, :, :], bt[b % 2][:, :].rearrange("p (a n) -> p a n", a=2),
                                   ACT.Identity).then_inc(s_thi, 1)

                def outs(p, par):
                    act.wait_ge(s_pv, 2 * p + 2)
                    act.activation(o[par][0][:, :], bo[:, :], ACT.Identity).then_inc(s_ohi, 1)

                def round_(h, b):
                    s = 4 * h + b
                    if b == 0 and has(2 * h + 1, NPAIR) and not (isinstance(h, int) and h == 0):
                        query(2 * h + 1, 1)
                    if b == 2 and has(2 * h + 2, NPAIR):
                        query(2 * h + 2, 0)
                    if b % 2 and has(2 * h - 2 + b // 2, NPAIR):
                        outs(2 * h - 2 + b // 2, b // 2)
                    if b == 1 and has(h + 1, NH):
                        merged(h + 1)
                    if has(s - 2, NS):
                        probs(s - 2, (b - 2) % 4)
                    if has(s, NS):
                        exps(s, b)

                merged(0)
                query(0, 0)
                query(1, 1)
                run(act, round_)

            @block.vector
            def _(dve):
                def merged_raw(h):
                    dve.wait_ge(s_gmm, h + 1)
                    dve.tensor_scalar(gm[:, :, 0:KVL], bq[:, 0:2 * KVL].rearrange("p (a n) -> p a n", a=2), SCALE0,
                                      None, ALU.mult)
                    dve.wait_ge(s_gpool, h + 1)
                    dve.tensor_scalar(gb[0:KVL, :], bq[0:KVL, 2 * KVL:2 * KVL + 1], SCALE0, None,
                                      ALU.mult).then_inc(s_graw, 1)

                def merged_lo(h):
                    dve.wait_ge(s_ghi, h + 1)
                    dve.tensor_tensor(gms[1][:, :, :], gm[:, :, :], f32(gms[0][:, :, :]), ALU.subtract)\
                       .then_inc(s_glo, 1)

                def query(p, par):
                    dve.wait_ge(s_qhi, p + 1)
                    dve.scalar_tensor_tensor(out=q[par][1][:, :], in0=bq[:, :], scalar=gb[:, 0:1],
                                             in1=f32(q[par][0][:, :]), op0=ALU.add, op1=ALU.subtract)\
                       .then_inc(s_qlo, 1)

                def maxes(s, b):
                    dve.wait_ge(s_smm, s + 1)
                    dve.tensor_reduce(nmax[b][:, :], bs[b % 2][:, :].rearrange("p (a n) -> p a n", a=2), AX,
                                      ALU.max, negate=True).then_inc(s_max, 1)

                def inverse(s, b):
                    dve.wait_ge(s_exp, s + 1)
                    dve.reciprocal(rinv[b][:, :], rsum[b][:, :]).then_inc(s_inv, 1)

                def probs(s, b):
                    dve.wait_ge(s_thi, s + 1)
                    dve.tensor_tensor(pt[b][1][:, :, :], bt[b % 2][:, :].rearrange("p (a n) -> p a n", a=2),
                                      f32(pt[b][0][:, :, :]), ALU.subtract).then_inc(s_tlo, 1)

                def outs(p, par):
                    dve.wait_ge(s_ohi, p + 1)
                    dve.tensor_tensor(o[par][1][:, :], bo[:, :], f32(o[par][0][:, :]), ALU.subtract)\
                       .then_inc(s_olo, 1)

                def round_(h, b):
                    s = 4 * h + b
                    if has(s - 1, NS):
                        inverse(s - 1, (b - 1) % 4)
                    if has(s, NS):
                        maxes(s, b)
                    if b == 1 and has(h + 1, NH):
                        merged_raw(h + 1)
                    if b == 0 and has(2 * h + 1, NPAIR) and not (isinstance(h, int) and h == 0):
                        query(2 * h + 1, 1)
                    if b == 2 and has(2 * h + 2, NPAIR):
                        query(2 * h + 2, 0)
                    if b % 2 and has(2 * h - 2 + b // 2, NPAIR):
                        outs(2 * h - 2 + b // 2, b // 2)
                    if b == 1 and has(h + 1, NH):
                        merged_lo(h + 1)
                    if has(s - 2, NS):
                        probs(s - 2, (b - 2) % 4)
                    if b == 3 and has(h, NH):
                        dve.wait_ge(s_part, 16 * h + 16)
                        dve.tensor_reduce(g["mag"][:, bass.ds(h, 1)], part[:, :], AX, ALU.max,
                                          apply_absolute_value=True).then_inc(s_mag, 1)

                merged_raw(0)
                merged_lo(0)
                query(0, 0)
                query(1, 1)
                run(dve, round_)

            @block.tensor
            def _(pe):
                def merge(h):
                    pe.wait_ge(s_w, 16 * h + 16)
                    need(pe, s_qlo, 2 * h)
                    for a in range(2):
                        pe.matmul(bq[:, a * KVL:(a + 1) * KVL], w[:, a * P:(a + 1) * P], wk, start=(a == 0),
                                  stop=True, skip_group_check=True)
                    pe.matmul(bq[0:KVL, 2 * KVL:2 * KVL + 1], wk, bcols[:, 0:1], start=False, stop=True,
                              skip_group_check=True).then_inc(s_gmm, 1)

                def query(h, p, c):
                    pe.wait_ge(s_glo, h + 1)
                    need(pe, s_qlo, p)
                    tok = slice(c * HALF, (c + 1) * HALF)
                    matmul3(pe, bq[:, :], (gms[0][:, 0, :], gms[1][:, 0, :]), (qa[0][:, tok], qa[1][:, tok]), True,
                            False)
                    pe.matmul(bq[:, :], gms[0][:, 1, :], qb[:, tok], start=False, stop=False, skip_group_check=True)
                    pe.matmul(bq[:, :], gms[1][:, 1, :], qb[:, tok], start=False, stop=True, skip_group_check=True)\
                      .then_inc(s_qmm, 1)

                def scores(s, p, b):
                    pe.wait_ge(s_qlo, p + 1)
                    need(pe, s_exp, s - 1)
                    par = b // 2
                    keys = slice(b * S, (b + 1) * S)
                    for i in range(2):
                        a = (b % 2) * S + i * P
                        m = matmul3(pe, bs[b % 2][:, i * S:(i + 1) * S],
                                    (q[par][0][:, a:a + P], q[par][1][:, a:a + P]),
                                    (kv[0][:, keys], kv[1][:, keys]), i == 0, i == 1)
                    m.then_inc(s_smm, 1)

                def turn(s, b):
                    pe.wait_ge(s_norm, s + 1)
                    need(pe, s_tlo, s - 1)
                    for kt in range(2):
                        for i in range(2):
                            m = pe.transpose(bt[b % 2][:, kt * S + i * P:kt * S + (i + 1) * P],
                                             pr[b][:, i, kt * P:(kt + 1) * P], ident[:, :])
                    m.then_inc(s_tmm, 1)

                def values(s, p, b):
                    pe.wait_ge(s_tlo, s + 1)
                    if b % 2 == 0:
                        need(pe, s_olo, p)
                    out = bo[:, (b % 2) * S:(b % 2 + 1) * S]
                    for kt in range(2):
                        for j in range(2):
                            m = pe.matmul(out, cs[:, 2 * b + kt, :], pt[b][j][:, kt, :],
                                          start=(b % 2 == 0 and kt == 0 and j == 0), stop=(kt == 1 and j == 1),
                                          skip_group_check=True)
                    m.then_inc(s_pv, 1)

                def project(h, p, c):
                    pe.wait_ge(s_olo, p + 1)
                    pe.wait_ge(s_wvl, h + 1)
                    matmul3(pe, acc[c][:, :], (wvs[0][:, :], wvs[1][:, :]), (o[c][0][:, :], o[c][1][:, :]), False,
                            False).then_inc(s_om, 1)

                def round_(h, b):
                    s = 4 * h + b
                    if has(s + 1, NS):
                        scores(s + 1, 2 * h + (b + 1) // 2, (b + 1) % 4)
                    if b == 3 and has(h + 1, NH):
                        query(h + 1, 2 * h + 3, 1)
                    if b == 0 and has(h - 2, NH):
                        project(h - 2, 2 * h - 3, 1)
                    if b == 2 and has(h - 1, NH):
                        project(h - 1, 2 * h - 2, 0)
                    if has(s - 1, NS):
                        turn(s - 1, (b - 1) % 4)
                    if has(s - 3, NS):
                        values(s - 3, 2 * h + (b - 3) // 2, (b - 3) % 4)
                    if b == 0 and has(h + 1, NH):
                        merge(h + 1)
                    if b == 1 and has(h + 1, NH):
                        query(h + 1, 2 * h + 2, 0)

                merge(0)
                query(0, 0, 0)
                query(0, 1, 1)
                scores(0, 0, 0)
                run(pe, round_)


def attention0_out(nc, k, g, acc, norm, ffn):
    res, wo = g["res"], g["wo"]
    os = k.sb("os", [P, T])
    banks = [k.ps(f"b{i}") for i in range(4)]
    turned = [k.ps(f"t{i}") for i in range(2)]
    s_os, s_mm, s_add, s_y = (k.sem(x) for x in ("os", "mm", "add", "y"))
    s_mag, s_magT = k.sem("mag"), k.sem("magT")
    magT = k.sb("magT", [1, P])
    with nc.Block() as block:
        @block.sync
        def _(sp):
            ffn.first_loads(sp)

        @block.gpsimd
        def _(pool):
            norm.power(pool, 0)

        @block.vector
        def _(dve):
            dve.tensor_reduce(g["mag1"][:, :], g["mag"][:, :], AX, ALU.max).then_inc(s_mag, 1)
            for j in range(4):
                dve.wait_ge(s_mm, j + 1)
                dve.tensor_tensor(res[:, j, :], banks[j][:, :], res[:, j, :], ALU.add).then_inc(s_add, 1)
                norm.stats(dve, j, (s_add, j + 1))
                if j == 0:
                    dve.wait_ge(s_magT, 1)
                    dve.tensor_reduce(magT[:, 0:1], turned[1][0:1, 0:P], AX, ALU.max).then_inc(s_mag, 1)
                    dve.wait_ge(s_mag, 2)
                    dve.tensor_scalar(g["largest"][:, :], magT[:, 0:1], 1e6, None, ALU.min).then_inc(s_mag, 1)
            norm.spread(dve, 0)
            ffn.first_lo(dve)
            for j in range(4):
                norm.scale(dve, j)
            for j in range(4):
                norm.lo(dve, j, turned)

        @block.scalar
        def _(act):
            for c in range(2):
                act.activation(os[:, c * HALF:(c + 1) * HALF], acc[c][:, :], ACT.Identity, bias=g["bvs"][:, :])\
                   .then_inc(s_os, 1)
            act.preload_act_table(ACT.Silu)
            ffn.first_hi(act)
            for j in range(4):
                act.wait_ge(s_mm, 5 + j)
                act.activation(g["y"][:, j, :], banks[j][:, :], ACT.Identity).then_inc(s_y, 1)
            for j in range(4):
                norm.hi(act, j, turned)

        @block.tensor
        def _(pe):
            def out(j):
                pe.wait_ge(s_os, j // 4 + 1)
                need(pe, s_add, j - 3)
                pe.matmul(banks[j % 4][:, :], os[:, j * P:(j + 1) * P], wo[:, :], start=True, stop=True)\
                  .then_inc(s_mm, 1)

            pe.wait_ge(s_mag, 1)
            pe.transpose(turned[1][0:1, 0:P], g["mag1"][:, :], g["ident"][:, :]).then_inc(s_magT, 1)
            for j in range(NT):
                out(j)
            pe.wait_ge(s_mag, 2)
            for j in range(4):
                norm.turn(pe, j, turned)


class Norm:

    def __init__(self, g, nth):
        self.res, self.xT, self.ident, self.m, self.s = g["res"], g["xT"], g["ident"], g["m"], g["ln"]
        self.tiles, self.halves = nth * NT, nth * 2

    def stats(self, dve, j, ready):
        dve.wait_ge(*ready)
        dve.bn_stats(self.m["st"][:, j, :], self.res[:, j, :]).then_inc(self.s["st"], 1)

    def spread(self, dve, q):
        dve.wait_ge(self.s["st"], self.tiles + 4 * q + 4)
        for j in range(4 * q, 4 * q + 4):
            dve.bn_aggr(self.m["mv"][:, j, :], self.m["st"][:, j, :]).then_inc(self.s["mv"], 1)
        dve.wait_ge(self.s["mv"], self.tiles + 4 * q + 4)
        var = self.m["mv"][:, 4 * q:4 * q + 4, 1]
        dve.tensor_scalar(var, var, EPS, None, ALU.add).then_inc(self.s["add"], 1)

    def power(self, pool, q):
        pool.wait_ge(self.s["add"], self.halves + q + 1)
        pool.tensor_tensor(self.m["rs"][:, 4 * q:4 * q + 4], self.m["mv"][:, 4 * q:4 * q + 4, 1],
                           self.m["mh"][:, :], ALU.pow).then_inc(self.s["rs"], 1)

    def scale(self, dve, j):
        dve.wait_ge(self.s["rs"], self.halves + j // 4 + 1)
        dve.tensor_scalar(self.res[:, j, :], self.res[:, j, :], self.m["mv"][:, j, 0:1], self.m["rs"][:, j:j + 1],
                          ALU.subtract, ALU.mult).then_inc(self.s["xn"], 1)

    def turn(self, pe, j, banks):
        pe.wait_ge(self.s["xn"], self.tiles + j + 1)
        need(pe, self.s["lo"], self.tiles + j + 1 - len(banks))
        for c in range(KC):
            cols = slice(c * P, (c + 1) * P)
            i = pe.transpose(banks[j % len(banks)][:, cols], self.res[:, j, cols], self.ident[:, :])
        i.then_inc(self.s["t"], 1)

    def view(self, j, banks):
        return banks[j % len(banks)][:, :].rearrange("p (c n) -> p c n", c=KC)

    def hi(self, act, j, banks):
        act.wait_ge(self.s["t"], self.tiles + j + 1)
        act.activation(self.xT[0][:, :, j * P:(j + 1) * P], self.view(j, banks), ACT.Identity)\
           .then_inc(self.s["hi"], 1)

    def lo(self, dve, j, banks):
        dve.wait_ge(self.s["hi"], self.tiles + j + 1)
        cols = slice(j * P, (j + 1) * P)
        dve.tensor_tensor(self.xT[1][:, :, cols], self.view(j, banks), f32(self.xT[0][:, :, cols]), ALU.subtract)\
           .then_inc(self.s["lo"], 1)

    def split_until(self, j):
        return self.s["lo"], self.tiles + j + 1


class FFN0:

    def __init__(self, nc, k, io, g):
        self.nc, self.io, self.g = nc, io, g
        self.wi = k.sb("wi", [P, 3, HID], I32)
        self.ws = (k.sb("w_hi", [P, 3, HID], F32R), k.sb("w_lo", [P, 3, HID], F32R))
        self.gs, self.us, self.ds = k.sb("gs", [P, NI]), k.sb("us", [P, NI]), k.sb("ds", [P, HID])
        self.sg, self.h = k.sb("sg", [P, HALF]), k.sb("h", [P, HALF])
        self.hs = (k.sb("h_hi", [P, HALF], F32R), k.sb("h_lo", [P, HALF], F32R))
        self.k = k
        self.s_sc = k.sem("sc_in")
        self.s_in = [k.sem(f"w{i}_in") for i in range(3)]
        self.s_whi = [k.sem(f"w{i}_hi") for i in range(3)]
        self.s_wlo = [k.sem(f"w{i}_lo") for i in range(3)]
        self.s_mm = [k.sem(f"mm{i}") for i in range(3)]
        self.s_res = k.sem("res")

    def load(self, sp, n, i, pieces):
        for j in pieces:
            need(sp, self.s_wlo[j], n)
            sp.dma_start(self.wi[:, j, :], self.io["w_ffn0"][bass.ds(i, 1), :, j * HID:(j + 1) * HID]
                         .rearrange("a p n -> (a p) n")).then_inc(self.s_in[j], 16)

    def first_loads(self, sp):
        self.load(sp, 0, 0, (0, 1, 2))
        sp.dma_start(self.gs[:, :], self.io["gate_scale"]).then_inc(self.s_sc, 16)
        sp.dma_start(self.us[:, :], self.io["up_scale"]).then_inc(self.s_sc, 16)
        sp.dma_start(self.ds[:, :], self.io["down_scale"][None, :].to_broadcast([P, HID])).then_inc(self.s_sc, 16)

    def hi(self, act, j, n):
        act.wait_ge(self.s_in[j], 16 * n + 16)
        need(act, self.s_mm[j], n)
        act.activation(self.ws[0][:, j, :], self.wi[:, j, :], ACT.Identity).then_inc(self.s_whi[j], 1)

    def lo(self, dve, j, n):
        dve.wait_ge(self.s_whi[j], n + 1)
        dve.tensor_tensor(self.ws[1][:, j, :], self.wi[:, j, :], f32(self.ws[0][:, j, :]), ALU.subtract)\
           .then_inc(self.s_wlo[j], 1)

    def first_hi(self, act):
        self.hi(act, 0, 0)
        self.hi(act, 1, 0)

    def first_lo(self, dve):
        self.lo(dve, 0, 0)
        self.lo(dve, 1, 0)

    def run(self, before, after, attn1):
        nc, k, g = self.nc, self.k, self.g
        wi, ws, gs, us, ds = self.wi, self.ws, self.gs, self.us, self.ds
        sg, h, hs, y = self.sg, self.h, self.hs, g["y"]
        s_sc, s_wlo, s_mm, s_res = self.s_sc, self.s_wlo, self.s_mm, self.s_res
        res = g["res"]
        xhi, xlo = g["xT"]
        bg, bu = k.ps("bg"), k.ps("bu")
        bd = [k.ps(f"bd{i}") for i in range(4)]
        turned = [k.ps(f"t{i}") for i in range(2)]
        s_sg, s_h, s_hhi, s_hlo, s_y, s_add = (k.sem(x) for x in ("sg", "h", "h_hi", "h_lo", "y", "add"))
        N = 2 * NI
        peeled = {0, 1, 2, 3, 4, *range(NI, NI + 6), N - 1}
        first_round = {2: (before, 1), NI + 3: (after, 0)}

        def norm_part(n, part):
            for start, (norm, q) in first_round.items():
                if isinstance(n, int) and n == start + part:
                    return norm, q
            return None, None

        def norm_turns(pe, n):
            for part in range(2):
                norm, q = norm_part(n, part)
                if norm:
                    for i in range(2):
                        norm.turn(pe, 4 * q + 2 * part + i, turned)

        def norm_splits(split, eng, n):
            for part in range(2):
                norm, q = norm_part(n, part + 1)
                if norm:
                    for i in range(2):
                        j = 4 * q + 2 * part + i
                        if split == "hi":
                            norm.hi(eng, j, turned)
                        else:
                            norm.lo(eng, j, turned)

        def rounds(eng, round_):
            for c in range(2):
                lo, hi = c * NI, (c + 1) * NI
                a = lo
                while a in peeled:
                    round_(a, a - lo)
                    a += 1
                b = hi - 1 if hi - 1 in peeled else hi
                with eng.Fori(a, b) as n:
                    round_(n, n - lo)
                for n in range(b, hi):
                    round_(n, n - lo)

        with nc.Block() as block:
            @block.sync
            def _(sp):
                ahead = {2: ("q0", "k0"), 3: ("v",), 4: ("q1", "k1"), NI: ("o",)}

                def loads(n, i):
                    if isinstance(n, int) and n in ahead:
                        attn1.load(sp, 0, ahead[n])
                    if not isinstance(n, int) or n > 0:
                        self.load(sp, n, i, (0, 1))
                    if not isinstance(n, int) or n > 1:
                        self.load(sp, n - 1, NI - 1 if isinstance(n, int) and n == NI else i - 1, (2,))

                rounds(sp, loads)
                self.load(sp, N - 1, NI - 1, (2,))

            @block.scalar
            def _(act):
                act.wait_ge(s_sc, 48)

                def hhi(n):
                    act.wait_ge(s_h, n + 1)
                    need(act, s_mm[2], n)
                    act.activation(hs[0][:, :], h[:, :], ACT.Identity).then_inc(s_hhi, 1)

                def round_(n, i):
                    if has(n - 1, N):
                        hhi(n - 1)
                        self.hi(act, 2, n - 1)
                    norm_splits("hi", act, n)
                    if has(n, N):
                        act.wait_ge(s_mm[0], n + 1)
                        act.activation(sg[:, :], bg[:, :], ACT.Silu, scale=gs[:, bass.ds(i, 1)]).then_inc(s_sg, 1)
                        if has(n + 1, N):
                            self.hi(act, 0, n + 1)
                            self.hi(act, 1, n + 1)

                rounds(act, round_)
                round_(N, None)

            @block.vector
            def _(dve):
                dve.wait_ge(s_sc, 48)

                def take(c):
                    dve.wait_ge(s_mm[2], (c + 1) * NI)
                    need(dve, s_res, 4 * c)
                    for j in range(4):
                        dve.tensor_tensor(y[:, j, :], bd[j][:, :], ds[:, :], ALU.mult).then_inc(s_y, 1)

                def round_(n, i):
                    if has(n - 1, N):
                        dve.wait_ge(s_hhi, n)
                        dve.tensor_tensor(hs[1][:, :], h[:, :], f32(hs[0][:, :]), ALU.subtract).then_inc(s_hlo, 1)
                        self.lo(dve, 2, n - 1)
                    norm_splits("lo", dve, n)
                    if isinstance(n, int) and n == NI + 1:
                        take(0)
                    if isinstance(n, int) and n == NI + 2:
                        for j in range(4):
                            after.stats(dve, j, (s_res, j + 1))
                        after.spread(dve, 0)
                    norm, q = norm_part(n, 0)
                    if norm:
                        for j in range(4):
                            norm.scale(dve, 4 * q + j)
                    if isinstance(n, int) and n == 1:
                        for j in range(4):
                            before.stats(dve, 4 + j, (s_add, j + 1))
                        before.spread(dve, 1)
                    if has(n, N):
                        if has(n + 1, N):
                            self.lo(dve, 0, n + 1)
                        dve.wait_ge(s_sg, n + 1)
                        dve.wait_ge(s_mm[1], n + 1)
                        need(dve, s_hlo, n)
                        dve.scalar_tensor_tensor(out=h[:, :], in0=bu[:, :], scalar=us[:, bass.ds(i, 1)], in1=sg[:, :],
                                                 op0=ALU.mult, op1=ALU.mult).then_inc(s_h, 1)
                        if has(n + 1, N):
                            self.lo(dve, 1, n + 1)

                rounds(dve, round_)
                round_(N, None)
                take(1)

            @block.gpsimd
            def _(pool):
                for j in range(4):
                    pool.tensor_tensor(res[:, 4 + j, :], y[:, j, :], res[:, 4 + j, :], ALU.add).then_inc(s_add, 1)
                before.power(pool, 1)
                attn1.first_splits(pool)
                for j in range(4):
                    pool.wait_ge(s_y, j + 1)
                    pool.tensor_tensor(res[:, j, :], y[:, j, :], res[:, j, :], ALU.add).then_inc(s_res, 1)
                after.power(pool, 0)

            @block.tensor
            def _(pe):
                exact = [False]

                def products(out, w, x, w_is_moving, start, stop):
                    pairs = [(w[0], x[0]), (w[0], x[1])] + ([] if exact[0] else [(w[1], x[0])])
                    for i, (a, b) in enumerate(pairs):
                        a, b = (b, a) if w_is_moving else (a, b)
                        m = pe.matmul(out, a, b, start=start and i == 0, stop=stop and i == len(pairs) - 1,
                                      skip_group_check=True)
                    return m

                def wide(j, bank, n, tok):
                    pe.wait_ge(s_wlo[j], n + 1)
                    for kc in range(KC):
                        w = tuple(x[:, j, kc * P:(kc + 1) * P] for x in ws)
                        m = products(bank[:, :], w, (xhi[:, kc, tok], xlo[:, kc, tok]), False, kc == 0, kc == KC - 1)
                    m.then_inc(s_mm[j], 1)

                def down(n):
                    first = isinstance(n, int) and n % NI == 0
                    pe.wait_ge(s_hlo, n + 1)
                    pe.wait_ge(s_wlo[2], n + 1)
                    for j in range(4):
                        hh = tuple(x[:, j * P:(j + 1) * P] for x in hs)
                        m = products(bd[j][:, :], (ws[0][:, 2, :], ws[1][:, 2, :]), hh, True, first, False)
                    m.then_inc(s_mm[2], 1)

                half = [0]

                def round_(n, i):
                    if isinstance(n, int):
                        half[0] = n // NI
                    tok = slice(half[0] * HALF, (half[0] + 1) * HALF)
                    if isinstance(n, int) and n == NI:
                        pe.wait_ge(*before.split_until(NT - 1))
                    need(pe, s_sg, n)
                    wide(0, bg, n, tok)
                    need(pe, s_h, n)
                    wide(1, bu, n, tok)
                    if isinstance(n, int) and n == NI + 1:
                        pe.wait_ge(s_y, 4)
                    if has(n - 1, N):
                        down(n - 1)
                    norm_turns(pe, n)

                def all_rounds():
                    rounds(pe, round_)
                    down(N - 1)

                largest = pe.value_load(g["largest"][0:1, 0:1])
                with pe.If(largest > EXACT):
                    all_rounds()
                with pe.Else():
                    exact[0] = True
                    all_rounds()


class Attention1:
    PIECES = {"q0": 512, "k0": 512, "v": 1024, "q1": 512, "k1": 512, "o": 1024}
    QK = ("q0", "k0", "q1", "k1")

    def __init__(self, nc, k, io, g, ffn_raw):
        self.nc, self.k, self.io, self.g, self.ffn_raw = nc, k, io, g, ffn_raw
        self.off, a = {}, 0
        for n in ("q0", "k0", "q1", "k1", "v", "o"):
            self.off[n] = a
            a += self.PIECES[n]
        self.raw = {n: k.sb(f"raw_{n}", [P, m]) for n, m in self.PIECES.items()}
        at, used = {"qk": 2 * self.off["o"]}, 2 * self.off["o"] + 2 * 4 * HALF
        self.memory = k.sb("w", [P, used + 2 * self.PIECES["o"]], F32R)
        for n in self.PIECES:
            at[n] = used if n == "o" else 2 * self.off[n]

        def pair(start, m):
            return self.memory[:, start:start + m], self.memory[:, start + m:start + 2 * m]

        self.ws = {n: pair(at[n], m) for n, m in self.PIECES.items()}
        self.qk0 = self.memory[:, at["qk"]:used].rearrange("p (z a n) -> p z a n", z=2, a=4)
        assert used >= 2 * (KC * W1F + HID)
        ffn_raw["memory"] = self.memory
        self.mask = k.sb("mask", [P, P])
        self.s_in = {n: k.sem(f"in_{n}") for n in self.PIECES}
        self.s_whi = {n: k.sem(f"whi_{n}") for n in self.PIECES}
        self.s_wlo = {n: k.sem(f"wlo_{n}") for n in self.PIECES}
        self.s_mask = k.sem("mask")

    def load(self, sp, gr, pieces=tuple(PIECES)):
        for n in pieces:
            m = self.PIECES[n]
            need(sp, self.s_wlo[n], gr)
            a = self.off[n]
            sp.dma_start(self.raw[n][:, :], self.io["w_attn1"][bass.ds(gr, 1), :, a:a + m]
                         .rearrange("a p n -> (a p) n")).then_inc(self.s_in[n], 16)

    def split(self, pool, n, gr, used=()):
        pool.wait_ge(self.s_in[n], 16 * gr + 16)
        for sem, value in used:
            pool.wait_ge(sem, value)
        plain(pool, self.g["tick"])
        hi, lo = self.ws[n]
        pool.tensor_copy(hi[:, :], self.raw[n][:, :]).then_inc(self.s_whi[n], 1)
        pool.wait_ge(self.s_whi[n], gr + 1)
        pool.tensor_tensor(lo[:, :], self.raw[n][:, :], f32(hi[:, :]), ALU.subtract).then_inc(self.s_wlo[n], 1)

    def first_splits(self, pool):
        pool.memset(self.mask[:, :], 0.0).then_inc(self.s_mask, 1)
        pool.wait_ge(self.s_mask, 1)
        pool.affine_select(out=self.mask[:, :], in_=self.mask[:, :], compare_op=ALU.is_ge, fill=-1e30, base=0,
                           pattern=[[-1, P]], channel_multiplier=1).then_inc(self.s_mask, 1)
        for n in ("q0", "k0", "v", "q1", "k1"):
            self.split(pool, n, 0)

    def run(self, k, before, after, s_res):
        nc, g = self.nc, self.g
        raw, ws, mask, QK = self.raw, self.ws, self.mask, self.QK
        s_wlo, s_mask = self.s_wlo, self.s_mask
        res, ident = g["res"], g["ident"]
        xhi, xlo = g["xT"]
        NSTEP = 8 * NG
        qk_all = [self.qk0, k.sb("qk1", [P, 2, 4, HALF], F32R)[:, :, :, :]]
        qk = [(x[:, 0, :, :], x[:, 1, :, :]) for x in qk_all]
        v = [(k.sb(f"v{i}_hi", [P, 4, 2 * DV], F32R), k.sb(f"v{i}_lo", [P, 4, 2 * DV], F32R)) for i in range(2)]
        oT = [(k.sb(f"oT{i}_hi", [P, 2, HALF], F32R), k.sb(f"oT{i}_lo", [P, 2, HALF], F32R)) for i in range(2)]
        pr = [k.sb(f"pr{i}", [P, 3 * P]) for i in range(2)]
        s0 = k.sb("s0", [P, P])
        o1 = k.sb("o1", [P, P])
        pt_all = k.sb("pt", [P, 2, 3 * P], F32R)
        pt = (pt_all[:, 0, :], pt_all[:, 1, :])
        nmax = [k.sb(f"nmax{i}", [P, 2]) for i in range(2)]
        rsum = [k.sb(f"rsum{i}", [P, 2]) for i in range(2)]
        rinv = [k.sb(f"rinv{i}", [P, 2]) for i in range(2)]
        bj = [k.ps(f"bj{i}") for i in range(3)]
        bs = [k.ps(f"bs{i}") for i in range(2)]
        bt = k.ps("bt")
        bo = [k.ps(f"bo{i}") for i in range(2)]
        s_jmm = [k.sem(f"jmm{i}") for i in range(3)]
        s_jhi = [k.sem(f"jhi{i}") for i in range(3)]
        s_jlo = [k.sem(f"jlo{i}") for i in range(3)]
        s_smm, s_mk, s_max, s_exp, s_inv, s_norm = (k.sem(x) for x in ("smm", "mk", "max", "exp", "inv", "norm"))
        s_tmm, s_thi, s_tlo, s_pv, s_orest, s_osum, s_ohi, s_olo = (
            k.sem(x) for x in ("tmm", "thi", "tlo", "pv", "orest", "osum", "ohi", "olo"))

        def work(r, t):
            todo = {}
            if has(r, NSTEP):
                todo[0] = "qk"
                if t < 2:
                    todo[1] = todo[2] = "v"
            if t >= 2 and has(r - 8, NSTEP):
                todo[1] = todo[2] = "o"
            return todo

        def sweep(eng, prologue, step):
            def group(gr):
                for c in range(2):
                    for t in range(4):
                        step(gr, c, t)

            for t in range(4):
                prologue(t)
            group(0)
            with eng.Fori(1, NG - 1) as gr:
                group(gr)
            group(NG - 1)
            for t in range(4):
                step(NG, 0, t)

        turned = [bo[0], bo[1], bt, bs[1]]

        with nc.Block() as block:
            @block.sync
            def _(sp):
                ffn1_first_loads(sp, self.io, self.ffn_raw)
                with sp.Fori(1, NG) as gr:
                    self.load(sp, gr)

            @block.gpsimd
            def _(pool):
                for j in range(4):
                    pool.tensor_tensor(res[:, 4 + j, :], g["y"][:, j, :], res[:, 4 + j, :], ALU.add).then_inc(s_res, 1)
                before.power(pool, 1)

                def group(gr):
                    r = 4 + 8 * gr
                    if has(gr + 1, NG):
                        self.split(pool, "q0", gr + 1, [(s_jmm[0], r + 1)])
                        self.split(pool, "k0", gr + 1, [(s_jmm[0], r + 2)])
                        self.split(pool, "v", gr + 1, [(s_jmm[2], r + 2)])
                        self.split(pool, "q1", gr + 1, [(s_jmm[0], r + 3)])
                        self.split(pool, "k1", gr + 1, [(s_jmm[0], r + 4)])
                    self.split(pool, "o", gr, [(s_jmm[2], r + 4)])

                with pool.Fori(0, NG - 1) as gr:
                    group(gr)
                group(NG - 1)
                pool.wait_ge(s_smm, NSTEP - 4)
                ffn1_lo(pool, self.ffn_raw)
                after.power(pool, 0)

            @block.scalar
            def _(act):
                act.preload_act_table(ACT.Exp)

                def exps(s, t):
                    act.wait_ge(s_max, s + 1)
                    for i, scored in enumerate((s0[:, :], bs[t % 2][:, P:3 * P])):
                        m = act.activation(pr[t % 2][:, i * P:(2 * i + 1) * P], scored, ACT.Exp,
                                           bias=nmax[t % 2][:, i:i + 1], accum_out=rsum[t % 2][:, i:i + 1])
                    m.then_inc(s_exp, 1)

                def probs(s):
                    act.wait_ge(s_tmm, s + 1)
                    act.activation(pt[0], bt[:, 0:3 * P], ACT.Identity).then_inc(s_thi, 1)

                def out_rest(s, t):
                    act.wait_ge(s_pv, s + 1)
                    need(act, s_osum, s)
                    act.activation(o1[:, :], bo[t % 2][:, 2 * P:3 * P], ACT.Identity).then_inc(s_orest, 1)

                def outs(s, c, t):
                    act.wait_ge(s_osum, s + 1)
                    b, hd = t // 2, t % 2
                    act.activation(oT[c][0][:, hd, b * S:(b + 1) * S], bo[t % 2][:, 0:S], ACT.Identity)\
                       .then_inc(s_ohi, 1)

                def spill(todo, banks, r, c, t):
                    for bank in banks:
                        if todo.get(bank) == "qk":
                            act.wait_ge(s_jmm[0], r + 1)
                            act.activation(qk[c][0][:, t, :], bj[0][:, :], ACT.Identity,
                                           scale=SCALE1 if t % 2 == 0 else 1.0).then_inc(s_jhi[0], 1)
                        if todo.get(bank) == "v":
                            act.wait_ge(s_jmm[bank], r + 1)
                            act.activation(v[c][0][:, 2 * t + bank - 1, :], bj[bank][:, 0:2 * DV], ACT.Identity)\
                               .then_inc(s_jhi[bank], 1)

                def prologue(t):
                    if t == 3:
                        for j in range(4, NT):
                            before.hi(act, j, turned)
                    spill(work(t, t), (0, 1, 2), t, 0, t)
                    if t == 3:
                        exps(0, 0)

                def step(gr, c, t):
                    s = 8 * gr + 4 * c + t
                    if has(s - 1, NSTEP):
                        out_rest(s - 1, (t - 1) % 4)
                    if has(s, NSTEP):
                        probs(s)
                    if has(s - 1, NSTEP):
                        outs(s - 1, c if t else 1 - c, (t - 1) % 4)
                    if has(s + 1, NSTEP):
                        exps(s + 1, (t + 1) % 4)
                    spill(work(s + 4, t), (0, 1, 2), s + 4, 1 - c, t)
                    if isinstance(gr, int) and (gr, c) == (NG - 1, 1):
                        if t == 0:
                            for bank in range(3):
                                act.wait_ge(s_jmm[bank], NSTEP)
                        ffn1_hi(act, self.ffn_raw, t)

                sweep(act, prologue, step)

            @block.vector
            def _(dve):
                def softmax_a(s, t):
                    dve.wait_ge(s_smm, s + 1)
                    bank = bs[t % 2]
                    dve.tensor_tensor(s0[:, :], bank[:, 3 * P:4 * P], mask[:, :], ALU.add).then_inc(s_mk, 1)
                    dve.tensor_tensor(bank[:, 2 * P:3 * P], bank[:, 2 * P:3 * P], mask[:, :], ALU.add)\
                       .then_inc(s_mk, 1)
                    dve.wait_ge(s_mk, 3 * s + 1)
                    dve.tensor_tensor(s0[:, :], bank[:, 0:P], s0[:, :], ALU.add).then_inc(s_mk, 1)
                    dve.wait_ge(s_mk, 3 * s + 2)
                    dve.tensor_reduce(nmax[t % 2][:, 1:2], bank[:, P:3 * P], AX, ALU.max, negate=True)
                    dve.wait_ge(s_mk, 3 * s + 3)
                    dve.tensor_reduce(nmax[t % 2][:, 0:1], s0[:, :], AX, ALU.max, negate=True).then_inc(s_max, 1)

                def softmax_b(s, t):
                    dve.wait_ge(s_exp, s + 1)
                    dve.reciprocal(rinv[t % 2][:, :], rsum[t % 2][:, :]).then_inc(s_inv, 1)
                    dve.wait_ge(s_inv, s + 1)
                    x = pr[t % 2]
                    dve.tensor_scalar(x[:, 0:P], x[:, 0:P], rinv[t % 2][:, 0:1], None, ALU.mult)
                    dve.tensor_scalar(x[:, P:3 * P], x[:, P:3 * P], rinv[t % 2][:, 1:2], None, ALU.mult)\
                       .then_inc(s_norm, 1)

                def probs(s):
                    dve.wait_ge(s_thi, s + 1)
                    dve.tensor_tensor(pt[1], bt[:, 0:3 * P], f32(pt[0]), ALU.subtract).then_inc(s_tlo, 1)

                def out_sum(s, t):
                    dve.wait_ge(s_orest, s + 1)
                    out = bo[t % 2][:, P:2 * P]
                    dve.tensor_tensor(out, out, o1[:, :], ALU.add).then_inc(s_osum, 1)

                def outs(s, c, t):
                    dve.wait_ge(s_ohi, s + 1)
                    b, hd = t // 2, t % 2
                    dve.tensor_tensor(oT[c][1][:, hd, b * S:(b + 1) * S], bo[t % 2][:, 0:S],
                                      f32(oT[c][0][:, hd, b * S:(b + 1) * S]), ALU.subtract).then_inc(s_olo, 1)

                def store(todo, banks, r, c, t):
                    for bank in banks:
                        kind = todo.get(bank)
                        if kind == "qk":
                            dve.wait_ge(s_jhi[0], r + 1)
                            hi, lo = (x[:, t, :] for x in qk[c])
                            if t % 2 == 0:
                                m = dve.scalar_tensor_tensor(out=lo, in0=bj[0][:, :], scalar=SCALE1, in1=f32(hi),
                                                             op0=ALU.mult, op1=ALU.subtract)
                            else:
                                m = dve.tensor_tensor(lo, bj[0][:, :], f32(hi), ALU.subtract)
                            m.then_inc(s_jlo[0], 1)
                        elif kind == "v":
                            dve.wait_ge(s_jhi[bank], (r - t) // 2 + t + 1)
                            hi, lo = (x[:, 2 * t + bank - 1, :] for x in v[c])
                            dve.tensor_tensor(lo, bj[bank][:, 0:2 * DV], f32(hi), ALU.subtract).then_inc(s_jlo[bank], 1)
                        elif kind == "o":
                            dve.wait_ge(s_jmm[bank], r + 1)
                            j = 4 * c + 2 * (t - 2) + bank - 1
                            dve.tensor_tensor(res[:, j, :], bj[bank][:, :], res[:, j, :], ALU.add)\
                               .then_inc(s_jlo[bank], 1)
                        else:
                            dve.wait_ge(s_jmm[bank], r + 1)
                            dve.sem_inc(s_jlo[bank], 1)

                def prologue(t):
                    if t == 1:
                        for j in range(4, NT):
                            before.stats(dve, j, (s_res, j + 1))
                        before.spread(dve, 1)
                    if t == 2:
                        for j in range(4, NT):
                            before.scale(dve, j)
                    if t == 3:
                        for j in range(4, NT):
                            before.lo(dve, j, turned)
                    store(work(t, t), (0, 1, 2), t, 0, t)
                    if t == 3:
                        dve.wait_ge(s_mask, 2)
                        softmax_a(0, 0)
                        softmax_b(0, 0)

                def step(gr, c, t):
                    s = 8 * gr + 4 * c + t
                    todo = work(s + 4, t)
                    if has(s - 1, NSTEP):
                        out_sum(s - 1, (t - 1) % 4)
                    if has(s + 1, NSTEP):
                        softmax_a(s + 1, (t + 1) % 4)
                    if has(s - 1, NSTEP):
                        outs(s - 1, c if t else 1 - c, (t - 1) % 4)
                    if has(s, NSTEP):
                        probs(s)
                    if has(s + 1, NSTEP):
                        softmax_b(s + 1, (t + 1) % 4)
                    if isinstance(gr, int) and gr == NG and t >= 2:
                        for j in (2 * t - 4, 2 * t - 3):
                            after.stats(dve, j, (s_jlo[2], NSTEP + 4))
                        if t == 3:
                            after.spread(dve, 0)
                    store(todo, (0, 1, 2), s + 4, 1 - c, t)

                sweep(dve, prologue, step)

            @block.tensor
            def _(pe):
                def project(todo, bank, r, gr, c, t):
                    need(pe, s_jlo[bank], r)
                    kind = todo.get(bank)
                    if kind == "qk":
                        n = QK[t]
                        pe.wait_ge(s_wlo[n], gr + 1)
                        tok = slice(c * HALF, (c + 1) * HALF)
                        for kc in range(KC):
                            w = tuple(x[:, kc * P:(kc + 1) * P] for x in ws[n])
                            m = matmul3(pe, bj[0][:, :], w, (xhi[:, kc, tok], xlo[:, kc, tok]), kc == 0, kc == KC - 1)
                    elif kind == "v":
                        pe.wait_ge(s_wlo["v"], gr + 1)
                        a = c * HALF + (2 * t + bank - 1) * P
                        for kc in range(KC):
                            x = (xhi[:, kc, a:a + P], xlo[:, kc, a:a + P])
                            w = tuple(y[:, kc * 2 * DV:(kc + 1) * 2 * DV] for y in ws["v"])
                            m = matmul3(pe, bj[bank][:, 0:2 * DV], x, w, kc == 0, kc == KC - 1)
                    elif kind == "o":
                        pe.wait_ge(s_wlo["o"], gr)
                        a = (2 * (t - 2) + bank - 1) * P
                        for hd in range(2):
                            o = tuple(x[:, hd, a:a + P] for x in oT[c])
                            w = tuple(x[:, hd * HID:(hd + 1) * HID] for x in ws["o"])
                            m = matmul3(pe, bj[bank][:, :], o, w, hd == 0, hd == 1)
                    else:
                        pe.sem_inc(s_jmm[bank], 1)
                        return
                    m.then_inc(s_jmm[bank], 1)

                def scores(s, c, t):
                    b, hd = t // 2, t % 2
                    need(pe, s_exp, s - 1)
                    q = [tuple(x[:, 2 * hd, b * S + i * P:b * S + (i + 1) * P] for x in qk[c]) for i in range(2)]
                    both = tuple(x[:, 2 * hd + 1, b * S:(b + 1) * S] for x in qk[c])
                    keys = qk_all[c][:, :, 2 * hd + 1, b * S:b * S + P]
                    apart = bs[t % 2][:, :].rearrange("p (a n) -> p a n", n=P)[:, 0:4:3, :]
                    pe.matmul(apart, q[0][0], keys, start=True, stop=False, skip_group_check=True)
                    pe.matmul(bs[t % 2][:, 0:P], q[0][1], keys[:, 0, :], start=False, stop=False,
                              skip_group_check=True)
                    matmul3(pe, bs[t % 2][:, P:3 * P], q[1], both, False, True).then_inc(s_smm, 1)

                def turn(s, t):
                    pe.wait_ge(s_norm, s + 1)
                    need(pe, s_tlo, s)
                    for i in range(3):
                        cols = slice(i * P, (i + 1) * P)
                        m = pe.transpose(bt[:, cols], pr[t % 2][:, cols], ident[:, :])
                    m.then_inc(s_tmm, 1)

                def values(s, c, t):
                    b, hd = t // 2, t % 2
                    pe.wait_ge(s_tlo, s + 1)
                    need(pe, s_olo, s - 1)
                    v0, v1 = (tuple(x[:, 2 * b + kt, hd * DV:(hd + 1) * DV] for x in v[c]) for kt in range(2))
                    matmul3(pe, bo[t % 2][:, 0:2 * P], v0, tuple(x[:, 0:2 * P] for x in pt), True, False)
                    last = pt_all[:, :, 2 * P:3 * P]
                    pe.matmul(bo[t % 2][:, P:3 * P].rearrange("p (a n) -> p a n", n=P), v1[0], last, start=False,
                              stop=False, skip_group_check=True)
                    pe.matmul(bo[t % 2][:, P:2 * P], v1[1], last[:, 0, :], start=False, stop=True,
                              skip_group_check=True).then_inc(s_pv, 1)

                def prologue(t):
                    for bank in range(3):
                        project(work(t, t), bank, t, 0, 0, t)
                    if t == 2:
                        for j in range(4, NT):
                            before.turn(pe, j, turned)
                    if t == 3:
                        pe.wait_ge(s_jlo[0], 2)
                        scores(0, 0, 0)

                def step(gr, c, t):
                    s = 8 * gr + 4 * c + t
                    r = s + 4
                    todo = work(r, t)
                    if isinstance(s, int) and s == 0:
                        pe.wait_ge(*before.split_until(NT - 1))
                    if has(s + 1, NSTEP):
                        if t == 3:
                            pe.wait_ge(s_jlo[0], r - 1)
                        if t == 0:
                            pe.wait_ge(s_jlo[0], r)
                        scores(s + 1, c if t < 3 else 1 - c, (t + 1) % 4)
                    if has(s, NSTEP):
                        turn(s, t)
                    unit = (gr, 1) if c == 0 else (gr + 1, 0)
                    for bank in range(3):
                        if todo.get(bank) == "o":
                            if t == 2 and bank == 1:
                                pe.wait_ge(s_olo, s - 2)
                        project(todo, bank, r, *unit, t)
                    if has(s, NSTEP):
                        if t == 0:
                            pe.wait_ge(s_jlo[1], r)
                            pe.wait_ge(s_jlo[2], r)
                        values(s, c, t)

                sweep(pe, prologue, step)


def ffn1_raw(k):
    return {"w": k.sb("wraw", [P, KC, W1F]), "bm": k.sb("braw", [P, HID]), "b": k.sb("bb", [P, HID]),
            "in": k.sem("in"), "hi": k.sem("whi"), "lo": k.sem("wlo")}


def ffn1_part(raw, c):
    half = KC * W1F + HID
    m = W1F if c < KC else HID
    w = raw["w"][:, c, :] if c < KC else raw["bm"][:, :]
    return w, *(raw["memory"][:, i * half + c * W1F:i * half + c * W1F + m] for i in range(2))


def ffn1_hi(act, raw, t):
    if t == 0:
        act.wait_ge(raw["in"], 48)
    for c in (t, KC) if t == KC - 1 else (t,):
        w, hi, _ = ffn1_part(raw, c)
        act.activation(hi, w, ACT.Identity).then_inc(raw["hi"], 1)


def ffn1_lo(pool, raw):
    for c in range(KC + 1):
        pool.wait_ge(raw["hi"], c + 1)
        w, hi, lo = ffn1_part(raw, c)
        pool.tensor_tensor(lo, w, f32(hi), ALU.subtract).then_inc(raw["lo"], 1)


def ffn1_first_loads(sp, io, raw):
    sp.dma_start(raw["w"][:, :, :], io["w_ffn1"].rearrange("(c p) n -> p c n", p=P)).then_inc(raw["in"], 16)
    sp.dma_start(raw["bm"][:, :], io["bm1"]).then_inc(raw["in"], 16)
    sp.dma_start(raw["b"][:, :], io["b1"][None, :].to_broadcast([P, HID])).then_inc(raw["in"], 16)


def ffn1(nc, k, io, g, raw, norm):
    res, ident, m = g["res"], g["ident"], g["m"]
    ws = [ffn1_part(raw, c)[1:] for c in range(KC)]
    bm = ffn1_part(raw, KC)[1:]
    st, mv, rs = k.sb("st2", [P, 6]), k.sb("mv2", [P, 2]), k.sb("rs2", [P, 1])
    x = [k.sb(f"x{i}", [P, HID]) for i in range(2)]
    xb = [k.sb(f"xb{i}", [P, HID]) for i in range(2)]
    xT = [(k.sb(f"xT{i}_hi", [P, HID], F32R), k.sb(f"xT{i}_lo", [P, HID], F32R)) for i in range(2)]
    qs = k.sb("qs", [P, E * DK])
    prod = k.sb("prod", [P, E * DK])
    sc, nm, nms, ex = k.sb("sc", [P, E]), k.sb("nm", [P, 1]), k.sb("nms", [P, 1]), k.sb("ex", [P, E])
    sm, ri = k.sb("sm", [P, 1]), k.sb("ri", [P, 1])
    gate = k.sb("gate", [P, E])
    wh = k.sb("wh", [P, E, R])
    whT = (k.sb("whT_hi", [P, P], F32R), k.sb("whT_lo", [P, P], F32R))
    y = k.sb("y", [P, HID])
    yo = [k.sb(f"yo{i}", [P, HID]) for i in range(2)]
    bx, bw = (k.ps(n) for n in ("bx", "bw"))
    bq, bk, br = ([k.ps(f"{n}{i}") for i in range(2)] for n in ("bq", "bk", "br"))
    s_x, s_xb, s_tx, s_xhi, s_xlo = (k.sem(n) for n in ("x", "xb", "tx", "xhi", "xlo"))
    s_bq, s_bk, s_r, s_q, s_gate, s_ex, s_wh, s_tw, s_whT, s_whl = (
        k.sem(n) for n in ("bq", "bk", "r", "q", "gate", "ex", "wh", "tw", "whT", "whl"))
    s_end, s_var, s_rs, s_yo = (k.sem(n) for n in ("end", "var", "rs", "yo"))
    s_out = [k.sem(f"out{i}") for i in range(2)]
    inv = float(DK) ** -0.5
    out = io["out"].rearrange("(t p) n -> t p n", p=P)
    NGATE, NEND = 6, 3

    def rounds(eng, round_):
        for t in (0, 1):
            round_(t, t, 0)
        with eng.Fori(1, NT // 2 - 1) as i:
            for u in range(2):
                round_(2 * i + u, u, i)
        for t in (NT - 2, NT - 1, NT):
            round_(t, t % 2, t // 2)

    with nc.Block() as block:
        @block.sync
        def _(sp):
            def store(t, u, i):
                if has(t, NT):
                    sp.wait_ge(s_yo, t + 1)
                    sp.dma_start(out[bass.ds(t, 1), :, :].rearrange("a p n -> (a p) n"), yo[u][:, :])\
                      .then_inc(s_out[u], 16)

            for free in s_out:
                sp.sem_inc(free, 16)
            rounds(sp, store)
            for stored in s_out:
                sp.wait_ge(stored, 16 * (NT // 2 + 1))

        @block.gpsimd
        def _(pool):
            def with_bias(t, u):
                pool.wait_ge(s_x, t + 1)
                need(pool, s_end, NEND * (t - 1))
                pool.tensor_tensor(xb[u][:, :], x[u][:, :], raw["b"][:, :], ALU.add).then_inc(s_xb, 1)

            def round_(t, u, i):
                if has(t + 1, NT):
                    with_bias(t + 1, 1 - u)
                if isinstance(t, int) and t == 1:
                    norm.power(pool, 1)
                if has(t - 1, NT):
                    pool.wait_ge(s_var, t)
                    pool.tensor_tensor(rs[:, :], mv[:, 1:2], m["mh"][:, 0:1], ALU.pow).then_inc(s_rs, 1)

            with_bias(0, 0)
            rounds(pool, round_)

        @block.scalar
        def _(act):
            act.preload_act_table(ACT.Exp)

            def xhi(t, u):
                act.wait_ge(s_tx, t + 1)
                act.activation(xT[u][0][:, :], bx[:, :], ACT.Identity).then_inc(s_xhi, 1)

            def round_(t, u, i):
                if has(t, NT):
                    act.wait_ge(s_bq, t + 1)
                    act.activation(qs[:, :], bq[u][:, 0:E * DK], ACT.Identity).then_inc(s_q, 1)
                if has(t - 1, NT):
                    act.wait_ge(s_tw, t)
                    need(act, s_r, t - 1)
                    act.activation(whT[0][:, :], bw[:, 0:P], ACT.Identity).then_inc(s_whT, 1)
                if has(t + 1, NT):
                    xhi(t + 1, 1 - u)
                if has(t, NT):
                    act.wait_ge(s_gate, NGATE * t + 4)
                    act.activation(ex[:, :], sc[:, :], ACT.Exp, bias=nms[:, :], scale=inv, accum_out=sm[:, :])\
                       .then_inc(s_ex, 1)

            xhi(0, 0)
            rounds(act, round_)

        @block.vector
        def _(dve):
            def begin(t, u):
                need(dve, s_tx, t - 1)
                need(dve, s_xb, t - 1)
                row = res[:, bass.ds(t, 1), :].rearrange("p a n -> p (a n)")
                mean = m["mv"][:, bass.ds(t, 1), 0]
                dve.tensor_scalar(x[u][:, :], row, mean, m["rs"][:, bass.ds(t, 1)], ALU.subtract, ALU.mult)\
                   .then_inc(s_x, 1)

            def xlo(t, u):
                dve.wait_ge(s_xhi, t + 1)
                dve.tensor_tensor(xT[u][1][:, :], bx[:, :], f32(xT[u][0][:, :]), ALU.subtract).then_inc(s_xlo, 1)

            def after(sem, value):
                dve.wait_ge(sem, value)
                plain(dve, g["tick"])

            def gates_and_end(t, u, before):
                a, b = NGATE * t, NEND * (t - 1)
                now, last = has(t, NT), has(t - 1, NT)
                v = 1 - u
                if now:
                    dve.wait_ge(s_q, t + 1)
                    dve.wait_ge(s_bk, t + 1)
                    dve.tensor_tensor(prod[:, :], bk[u][:, 0:E * DK], qs[:, :], ALU.mult).then_inc(s_gate, 1)
                if last:
                    dve.wait_ge(s_r, t)
                    dve.wait_ge(s_xb, t)
                    dve.tensor_tensor(y[:, :], br[v][:, :], xb[v][:, :], ALU.add).then_inc(s_end, 1)
                if now:
                    after(s_gate, a + 1)
                    dve.tensor_reduce(sc[:, :], prod[:, :].rearrange("p (e d) -> p e d", e=E), AX, ALU.add)\
                       .then_inc(s_gate, 1)
                if last:
                    after(s_end, b + 1)
                    dve.bn_stats(st[:, :], y[:, :]).then_inc(s_end, 1)
                if now:
                    after(s_gate, a + 2)
                    dve.tensor_reduce(nm[:, :], sc[:, :], AX, ALU.max, negate=True).then_inc(s_gate, 1)
                if last:
                    after(s_end, b + 2)
                    dve.bn_aggr(mv[:, :], st[:, :]).then_inc(s_end, 1)
                if now:
                    after(s_gate, a + 3)
                    dve.tensor_scalar(nms[:, :], nm[:, :], inv, None, ALU.mult).then_inc(s_gate, 1)
                if last:
                    after(s_end, b + 3)
                    dve.tensor_scalar(mv[:, 1:2], mv[:, 1:2], EPS, None, ALU.add).then_inc(s_var, 1)
                if has(t + 1, NT):
                    xlo(t + 1, 1 - u)
                if now:
                    dve.wait_ge(s_ex, t + 1)
                    plain(dve, g["tick"])
                    dve.reciprocal(ri[:, :], sm[:, :]).then_inc(s_gate, 1)
                    after(s_gate, a + 5)
                    dve.tensor_scalar(gate[:, :], ex[:, :], ri[:, 0:1], None, ALU.mult).then_inc(s_gate, 1)
                    after(s_gate, a + 6)
                    need(dve, s_tw, t)
                    for i, bank in enumerate((bq[u], bk[u])):
                        es = slice(i * E // 2, (i + 1) * E // 2)
                        h = bank[:, E * DK:W1H].rearrange("p (e r) -> p e r", e=E // 2)
                        dve.tensor_tensor(wh[:, es, :], h, gate[:, es][:, :, None].to_broadcast([P, E // 2, R]),
                                          ALU.mult).then_inc(s_wh, 1)
                if last:
                    dve.wait_ge(s_rs, t)
                    dve.wait_ge(s_out[v], 16 * before)
                    dve.tensor_scalar(yo[v][:, :], y[:, :], mv[:, 0:1], rs[:, 0:1], ALU.subtract, ALU.mult)\
                       .then_inc(s_yo, 1)

            def round_(t, u, i):
                if has(t + 1, NT):
                    begin(t + 1, 1 - u)
                if isinstance(t, int) and t < 2:
                    for j in (4 + 2 * t, 5 + 2 * t):
                        norm.stats(dve, j, (s_x, 1))
                    if t == 1:
                        norm.spread(dve, 1)
                if has(t - 1, NT):
                    dve.wait_ge(s_whT, t)
                    dve.tensor_tensor(whT[1][:, :], bw[:, 0:P], f32(whT[0][:, :]), ALU.subtract).then_inc(s_whl, 1)
                gates_and_end(t, u, i + u)

            dve.wait_ge(norm.s["rs"], norm.halves + 1)
            begin(0, 0)
            xlo(0, 0)
            rounds(dve, round_)

        @block.tensor
        def _(pe):
            def wide(bank, u, a, n, stop):
                for c in range(KC):
                    i = matmul3(pe, bank[:, 0:n], tuple(z[:, c * P:(c + 1) * P] for z in xT[u]),
                                tuple(z[:, a:a + n] for z in ws[c]), c == 0, stop and c == KC - 1)
                return i

            def turn(t, u):
                pe.wait_ge(s_x, t + 1)
                need(pe, s_xlo, t)
                for c in range(KC):
                    i = pe.transpose(bx[:, c * P:(c + 1) * P], x[u][:, c * P:(c + 1) * P], ident[:, :])
                i.then_inc(s_tx, 1)

            def round_(t, u, i):
                if has(t, NT):
                    pe.wait_ge(s_xlo, t + 1)
                    need(pe, s_wh, 2 * t - 2)
                    wide(bq[u], u, HID, W1H, True).then_inc(s_bq, 1)
                if has(t - 1, NT):
                    pe.wait_ge(s_wh, 2 * t)
                    need(pe, s_whl, t - 1)
                    pe.transpose(bw[:, 0:P], wh[:, :, :].rearrange("p e r -> p (e r)"), ident[:, :]).then_inc(s_tw, 1)
                if has(t, NT):
                    wide(bk[u], u, HID + W1H, W1H, True).then_inc(s_bk, 1)
                if has(t - 1, NT):
                    pe.wait_ge(s_whl, t)
                    matmul3(pe, br[1 - u][:, :], (whT[0][:, :], whT[1][:, :]), bm, False, True).then_inc(s_r, 1)
                if has(t + 1, NT):
                    turn(t + 1, 1 - u)
                if has(t, NT):
                    need(pe, s_end, NEND * (t - 2) + 1)
                    wide(br[u], u, 0, HID, False)

            turn(0, 0)
            rounds(pe, round_)


def _lay_out(i):
    c = np.ascontiguousarray
    f = np.float32
    a = {n: np.asarray(x) for n, x in i.items()}
    x = a["L0_attn_hidden_size"].reshape(T, HID)
    wqc, wkc = a["L0_attn_Wq_c"], a["L0_attn_Wkv_c"]
    bqc, bkc = a["L0_attn_bq_c"], a["L0_attn_bkv_c"]
    o = {"x": x, "xT": x.T}
    o["w_down0"] = np.concatenate([wqc.T, wqc[P:].T, wkc.T], 1)
    o["b_down0"] = np.stack([bqc[:P], np.concatenate([bqc[P:], bqc[P:]]), bkc], 1)
    wq = a["L0_attn_Wq_up"].reshape(NH, NOPE + ROPE, QL)
    bq = a["L0_attn_bq_up"].reshape(NH, NOPE + ROPE)
    wkv = a["L0_attn_Wkv_up"].reshape(NH, NOPE + VH, KVL)
    bkv = a["L0_attn_bkv_up"].reshape(NH, NOPE + VH)
    nope, rope = wq[:, :NOPE], wq[:, NOPE:].transpose(0, 2, 1)
    bias = np.zeros((NH, P, 2), f)
    bias[:, :, 0] = bq[:, :NOPE]
    bias[:, KVL:, 1] = bq[:, NOPE:]
    o["w_head0"] = np.concatenate([nope, nope[:, :, P:], wkv[:, :NOPE], rope[:, :P], np.concatenate(
        [rope[:, P:], rope[:, P:]], 1), bias], 2)
    wv = wkv[:, NOPE:].transpose(0, 2, 1)
    o["wv_head0"] = np.concatenate([wv, wv], 1)
    o["bv0"] = bkv[:, NOPE:].T
    o["wo0"] = a["L0_attn_Wo"].T
    o["bo0"] = a["L0_attn_bo"]

    gw, uw, dw = (a[f"L0_ffn_{n}_wq"] for n in ("gate", "up", "down"))
    blocks = np.zeros((NI, P, 3 * HID), gw.dtype)
    pad = np.zeros((NI * P, HID), gw.dtype)
    for j, w in enumerate((gw, uw)):
        pad[:INTER] = w
        blocks[:, :, j * HID:(j + 1) * HID] = pad.reshape(NI, P, KC, P).transpose(0, 3, 2, 1).reshape(NI, P, HID)
    pad[:INTER] = dw.T
    blocks[:, :, 2 * HID:] = pad.reshape(NI, P, HID)
    o["w_ffn0"] = blocks
    for n in ("gate", "up"):
        s = np.zeros(NI * P, f)
        s[:INTER] = a[f"L0_ffn_{n}_scale"]
        o[f"{n}_scale"] = s.reshape(NI, P).T
    o["down_scale"] = a["L0_ffn_down_scale"]

    wq1 = a["L1_attn_wq"].reshape(KC, P, NG, 2, DN + DR)[..., :DN]
    wkv1 = a["L1_attn_wkv"]
    wk1 = wkv1[:, :NH * DN].reshape(KC, P, NG, 2, DN)
    wv1 = wkv1[:, NH * DN:NH * (DN + DV)].reshape(KC, P, NG, 2 * DV)
    wo1 = a["L1_attn_wo"].reshape(NG, 2, P, HID)
    piece = lambda w: w.transpose(2, 1, 0, 3).reshape(NG, P, -1)
    o["w_attn1"] = np.concatenate([piece(wq1[:, :, :, 0]), piece(wk1[:, :, :, 0]), piece(wq1[:, :, :, 1]),
                                   piece(wk1[:, :, :, 1]), piece(wv1),
                                   wo1.transpose(0, 2, 1, 3).reshape(NG, P, -1)], 2)
    A = a["L1_ffn_A"].reshape(E * R, HID).T
    o["w_ffn1"] = np.concatenate([a["L1_ffn_W"].T, a["L1_ffn_Wq"].T, A[:, :E * R // 2], a["L1_ffn_Wk"].T,
                                  A[:, E * R // 2:]], 1)
    o["bm1"] = a["L1_ffn_Bm"].transpose(0, 2, 1).reshape(E * R, HID)
    o["b1"] = a["L1_ffn_b"]
    return {n: c(x) for n, x in o.items()}


def kernel(**inputs):
    import concourse.bacc as _bacc
    from concourse.bass_utils import run_bass_kernel_spmd as _run

    nc = _bacc.Bacc("TRN2", target_bir_lowering=False, num_devices=1)
    arrays = {f"in_{n}": x for n, x in _lay_out(inputs).items()}
    io = {n[3:]: nc.dram_tensor(n, x.shape, mybir.dt.from_np(x.dtype), kind="ExternalInput").ap()
          for n, x in arrays.items()}
    io["out"] = nc.dram_tensor("out", (T, HID), F32, kind="ExternalOutput").ap()
    build(nc, io)
    r = _run(nc, [arrays], core_ids=[0])
    return r.results[0]["out"].reshape(NB, S, HID)
```
